# Optimizing a Trainium2 kernel written in Bass

```python
import numpy as np
import jax
import jax.numpy as jnp

def _softmax(x, axis=-1):
    return jax.nn.softmax(x, axis=axis)

def _gelu(x):
    return jax.nn.gelu(x, approximate=True)

def _silu(x):
    return jax.nn.silu(x)

def _sigmoid(x):
    return jax.nn.sigmoid(x)

def _layernorm(x, axis=-1, eps=1e-05):
    m = jnp.mean(x, axis=axis, keepdims=True)
    v = jnp.var(x, axis=axis, keepdims=True)
    return (x - m) / jnp.sqrt(v + eps)

def _scatter_add(tgt, idx, src, axis=0):
    return tgt.at[idx].add(src)

def _segment_sum(src, seg, n):
    return jax.ops.segment_sum(src, seg, n)
kernel_name = 'mk_decoder_preln_d1_seqx_r2_042e71'

def setup_inputs(seed: int=0):
    np.random.seed(seed)
    _w = jnp.asarray

    def _rec_inputs():
        import jax
        import jax.numpy as jnp
        _rk = jax.random.key(seed)
        x = 7.22e-05 + 1 * jax.random.normal(jax.random.fold_in(_rk, 1), (2, 2048, 512), jnp.float32)
        _lenS = 2048 - jax.random.randint(jax.random.fold_in(_rk, 7), (2,), 0, max(1, 2048 // 4) + 1, jnp.int32)
        _lenS2 = 77 - jax.random.randint(jax.random.fold_in(_rk, 8), (2,), 0, max(1, 77 // 4) + 1, jnp.int32)
        _ctx_1024P = jax.random.normal(jax.random.fold_in(_rk, 11), (2, 16, 512), jnp.float32)
        _ctx_1024c = jax.random.dirichlet(jax.random.fold_in(_rk, 511), 0.3 * jnp.ones((16,), jnp.float32), (2, 77))
        _ctx_1024t = jnp.einsum('bsk,bkd->bsd', _ctx_1024c, _ctx_1024P)
        _ctx_1024t = _ctx_1024t * jax.lax.rsqrt(jnp.mean(jnp.square(_ctx_1024t)) + 1e-12) * 0.953939
        ctx_1024 = 4.13588e-05 + 0.999923 * (_ctx_1024t + 0.3 * jax.random.normal(jax.random.fold_in(_rk, 611), (2, 77, 512), jnp.float32))
        _validS = jnp.arange(2048)[None, :] < _lenS[:, None]
        _validS2 = jnp.arange(77)[None, :] < _lenS2[:, None]
        _causal = jnp.tril(jnp.ones((2048, 2048), dtype=bool))
        mask_BxS2_bk0 = jnp.logical_not(jnp.broadcast_to(_validS2[:, :], (2, 77)))
        return (x, ctx_1024, mask_BxS2_bk0)
    x, ctx_1024, mask_BxS2_bk0 = _rec_inputs()

    def _L0_attn_setup():
        import jax, jax.numpy as jnp
        import numpy as np
        EPS = 1e-06

        def _feature_map(x):
            return jax.nn.elu(x) + 1.0
        key = jax.random.key(seed)
        ks = jax.random.split(key, 4)
        B, L, C = (4, 4096, 512)
        s = 1.0 / np.sqrt(C)
        x = jax.random.normal(ks[0], (B, L, C), dtype=jnp.float32)
        Wq = jax.random.normal(ks[1], (C, C), dtype=jnp.float32) * s
        Wk = jax.random.normal(ks[2], (C, C), dtype=jnp.float32) * s
        Wv = jax.random.normal(ks[3], (C, C), dtype=jnp.float32) * s
        bq = jnp.zeros((C,), jnp.float32)
        bk = jnp.zeros((C,), jnp.float32)
        bv = jnp.zeros((C,), jnp.float32)
        return {'x': x, 'Wq': Wq, 'bq': bq, 'Wk': Wk, 'bk': bk, 'Wv': Wv, 'bv': bv}
    _L0_attn_all = _L0_attn_setup()
    _L0_attn_in = {k: v for k, v in _L0_attn_all.items() if k in ('Wq', 'bq', 'Wk', 'bk', 'Wv', 'bv')}
    del _L0_attn_all

    def _L0_xattn_setup():
        import math
        import jax, jax.numpy as jnp
        import numpy as np
        HIDDEN = 512
        NUM_HEADS = 16
        HEAD_DIM = HIDDEN // NUM_HEADS
        B, S = (4, 1024)

        def _layer_norm_scores(x, eps=1e-08):
            mean = jnp.mean(x, axis=-1, keepdims=True)
            sigma = jnp.std(x, axis=-1, keepdims=True, ddof=1)
            return (x - mean) / (sigma + eps)
        key = jax.random.key(seed)
        ks = jax.random.split(key, 10)
        sc_in = 1.0 / math.sqrt(HIDDEN)
        inp = {'query': jax.random.normal(ks[0], (B, S, HIDDEN), jnp.float32), 'key': jax.random.normal(ks[1], (B, S, HIDDEN), jnp.float32), 'value': jax.random.normal(ks[2], (B, S, HIDDEN), jnp.float32), 'mask': jax.random.randint(ks[3], (B, S), 0, 2).astype(bool), 'Wq': jax.random.normal(ks[4], (HIDDEN, HEAD_DIM), jnp.float32) * sc_in, 'bq': jnp.zeros((HEAD_DIM,), jnp.float32), 'Wk': jax.random.normal(ks[5], (HIDDEN, HEAD_DIM), jnp.float32) * sc_in, 'bk': jnp.zeros((HEAD_DIM,), jnp.float32), 'Wv': jax.random.normal(ks[6], (HIDDEN, HEAD_DIM), jnp.float32) * sc_in, 'bv': jnp.zeros((HEAD_DIM,), jnp.float32), 'Wout': jax.random.normal(ks[7], (HIDDEN, HIDDEN), jnp.float32) * sc_in, 'bout': jnp.zeros((HIDDEN,), jnp.float32), 'seq_mask': 0}
        return inp
    _L0_xattn_all = _L0_xattn_setup()
    _L0_xattn_in = {k: v for k, v in _L0_xattn_all.items() if k in ('Wq', 'bq', 'Wk', 'bk', 'Wv', 'bv', 'Wout', 'bout')}
    del _L0_xattn_all

    def _L0_ffn_setup():
        import jax, jax.numpy as jnp
        import numpy as np
        B, C, D = (2, 1024, 512)
        I = 1024
        E, K = (8, 2)
        CF = 1.25
        key = jax.random.key(seed)
        k1, k2, k3, k4 = jax.random.split(key, 4)
        scale = 0.02
        return {'hidden_states': jax.random.normal(k1, (B, C, D), jnp.float32), 'Wg': jax.random.normal(k2, (E, D), jnp.float32) * scale, 'W1': jax.random.normal(k3, (E, D, 2 * I), jnp.float32) * scale, 'W2': jax.random.normal(k4, (E, I, D), jnp.float32) * scale}
    _L0_ffn_all = _L0_ffn_setup()
    _L0_ffn_in = {k: v for k, v in _L0_ffn_all.items() if k in ('Wg', 'W1', 'W2')}
    del _L0_ffn_all
    return {'x': x, 'ctx_1024': ctx_1024, 'mask_BxS2_bk0': mask_BxS2_bk0, 'L0_attn_Wq': _L0_attn_in['Wq'], 'L0_attn_bq': _L0_attn_in['bq'], 'L0_attn_Wk': _L0_attn_in['Wk'], 'L0_attn_bk': _L0_attn_in['bk'], 'L0_attn_Wv': _L0_attn_in['Wv'], 'L0_attn_bv': _L0_attn_in['bv'], 'L0_xattn_Wq': _L0_xattn_in['Wq'], 'L0_xattn_bq': _L0_xattn_in['bq'], 'L0_xattn_Wk': _L0_xattn_in['Wk'], 'L0_xattn_bk': _L0_xattn_in['bk'], 'L0_xattn_Wv': _L0_xattn_in['Wv'], 'L0_xattn_bv': _L0_xattn_in['bv'], 'L0_xattn_Wout': _L0_xattn_in['Wout'], 'L0_xattn_bout': _L0_xattn_in['bout'], 'L0_ffn_Wg': _L0_ffn_in['Wg'], 'L0_ffn_W1': _L0_ffn_in['W1'], 'L0_ffn_W2': _L0_ffn_in['W2']}

def reference(x, ctx_1024, mask_BxS2_bk0, L0_attn_Wq, L0_attn_bq, L0_attn_Wk, L0_attn_bk, L0_attn_Wv, L0_attn_bv, L0_xattn_Wq, L0_xattn_bq, L0_xattn_Wk, L0_xattn_bk, L0_xattn_Wv, L0_xattn_bv, L0_xattn_Wout, L0_xattn_bout, L0_ffn_Wg, L0_ffn_W1, L0_ffn_W2):
    import jax
    import jax.numpy as jnp

    def _L0_attn_ref(x, Wq, bq, Wk, bk, Wv, bv):
        import jax, jax.numpy as jnp
        import numpy as np
        EPS = 1e-06

        def _feature_map(x):
            return jax.nn.elu(x) + 1.0
        B, L, C = x.shape
        H = 8
        D = C // H
        q = x @ Wq + bq
        k = x @ Wk + bk
        v = x @ Wv + bv
        q = q.reshape(B, L, H, D)
        k = k.reshape(B, L, H, D)
        v = v.reshape(B, L, H, D)
        Q = _feature_map(q)
        K = _feature_map(k)
        v_len = jnp.asarray(L, v.dtype)
        v_scaled = v / v_len
        KV = jnp.einsum('nshd,nshv->nhdv', K, v_scaled)
        Z = 1.0 / (jnp.einsum('nlhd,nhd->nlh', Q, K.sum(axis=1)) + EPS)
        out = jnp.einsum('nlhd,nhdv,nlh->nlhv', Q, KV, Z) * v_len
        return out.reshape(B, L, C)

    def _L0_xattn_ref(query, key, value, mask, Wq, bq, Wk, bk, Wv, bv, Wout, bout, seq_mask):
        import math
        import jax, jax.numpy as jnp
        import numpy as np
        HIDDEN = 512
        NUM_HEADS = 16
        HEAD_DIM = HIDDEN // NUM_HEADS
        B, S = (4, 1024)

        def _layer_norm_scores(x, eps=1e-08):
            mean = jnp.mean(x, axis=-1, keepdims=True)
            sigma = jnp.std(x, axis=-1, keepdims=True, ddof=1)
            return (x - mean) / (sigma + eps)
        q = query @ Wq + bq
        k = key @ Wk + bk
        v = value @ Wv + bv
        scores = jnp.einsum('bqd,bkd->bqk', q, k) / math.sqrt(HIDDEN)
        scores = _layer_norm_scores(scores)
        m = jnp.broadcast_to(mask[:, None, :], scores.shape)
        if seq_mask:
            tri = jnp.triu(jnp.ones(scores.shape[-2:], bool), k=1)
            m = m | tri[None]
        scores = scores + jnp.where(m, jnp.float32(-1e-32), jnp.float32(0.0))
        attn = jax.nn.softmax(scores, axis=-1)
        head = jnp.einsum('bqk,bkd->bqd', attn, v)
        attention = jnp.tile(head, (1, 1, NUM_HEADS))
        return attention @ Wout + bout

    def _L0_ffn_ref(hidden_states, Wg, W1, W2):
        import jax, jax.numpy as jnp
        import numpy as np
        B, C, D = (2, 1024, 512)
        I = 1024
        E, K = (8, 2)
        CF = 1.25
        Bx, Cx, d = hidden_states.shape
        N = Bx * Cx
        cap = int(N * K * CF / E)
        x = hidden_states.reshape(N, d)
        logits = x @ Wg.T
        top_v, top_i = jax.lax.top_k(logits, K)
        gates = jax.nn.softmax(top_v, axis=-1)
        flat_e = top_i.reshape(N * K)
        gates_f = gates.reshape(N * K)
        tok = jnp.repeat(jnp.arange(N), K)
        onehot = jax.nn.one_hot(flat_e, E, dtype=jnp.int32)
        pos = jnp.cumsum(onehot, axis=0) - 1
        pos_f = jnp.take_along_axis(pos, flat_e[:, None], axis=1)[:, 0]
        keep = pos_f < cap
        pos_safe = jnp.where(keep, pos_f, cap)
        exp_batches = jnp.zeros((E, cap, d), x.dtype).at[flat_e, pos_safe].set(x[tok], mode='drop')
        h = jnp.einsum('ecd,edf->ecf', exp_batches, W1)
        inp, gate = jnp.split(h, 2, axis=-1)
        h = jax.nn.gelu(inp, approximate=False) * gate
        exp_out = jnp.einsum('eci,eid->ecd', h, W2)
        gathered = exp_out[flat_e, jnp.minimum(pos_safe, cap - 1)]
        contrib = jnp.where(keep, gates_f, 0.0)[:, None] * gathered
        out = jax.ops.segment_sum(contrib, tok, num_segments=N)
        return out.reshape(Bx, Cx, d)
    x = x + _L0_attn_ref(_layernorm(x, axis=-1), L0_attn_Wq, L0_attn_bq, L0_attn_Wk, L0_attn_bk, L0_attn_Wv, L0_attn_bv)
    x = x + _L0_xattn_ref(_layernorm(x, axis=-1), ctx_1024, ctx_1024, mask_BxS2_bk0, L0_xattn_Wq, L0_xattn_bq, L0_xattn_Wk, L0_xattn_bk, L0_xattn_Wv, L0_xattn_bv, L0_xattn_Wout, L0_xattn_bout, 0)
    x = x + _L0_ffn_ref(_layernorm(x, axis=-1), L0_ffn_Wg, L0_ffn_W1, L0_ffn_W2)
    return x

_drawn_inputs = setup_inputs


def setup_inputs(seed=0):
    import zlib

    import numpy as np

    out = dict(_drawn_inputs(seed))
    spreads = {'L0_attn_bq': (0.0, 0.8),
     'L0_attn_bk': (0.0, 0.8),
     'L0_attn_bv': (0.0, 0.1),
     'L0_xattn_bq': (0.0, 0.336),
     'L0_xattn_bk': (0.0, 0.8),
     'L0_xattn_bv': (0.0, 0.1),
     'L0_xattn_bout': (0.0, 0.1)}
    factors = {'L0_attn_Wq': 8.0, 'L0_attn_Wk': 8.0, 'L0_attn_Wv': 2.812}
    for name, (base, spread) in spreads.items():
        noise = np.random.default_rng([zlib.crc32(name.encode()), seed]).standard_normal(out[name].shape)
        drawn = base * np.exp(spread * noise) if base else spread * noise
        out[name] = jnp.asarray(drawn.astype(out[name].dtype))
    for name, factor in factors.items():
        out[name] = (out[name] * factor).astype(out[name].dtype)
    return out
```

```python
from contextlib import ExitStack

import concourse.bass as bass
from concourse import mybir

F32 = mybir.dt.float32
F32R = mybir.dt.float32r
BF16 = mybir.dt.bfloat16
U32 = mybir.dt.uint32
I32 = mybir.dt.int32
U8 = mybir.dt.uint8
ALU = mybir.AluOpType
ACT = mybir.ActivationFunctionType
AX = mybir.AxisListType

P = 128
D = 512
KC = D // P
NB, S = 2, 2048
N = NB * S
GT = 512
NG = S // GT
TI = GT // P
H, HD = 8, 64
PAIRS = H // 2
HW = HD + 1
PW = 2 * HW
CK, XH = 77, 32
PADW = 96
EX, TOPK, INNER = 8, 2, 1024
CAP = int(N * TOPK * 1.25 / EX)
ET = CAP // P
FJ = INNER // P
W1P, W2P = FJ, FJ // 2
WP = W1P + W2P
STG = 4
CHUNKS = [4, 4, 2]
SLOTS = EX * CAP
PHANTOM = CAP
TRASH = SLOTS + PHANTOM
TABLE = TRASH + N * TOPK
LN_EPS, Z_EPS, SIG_EPS = 1e-5, 1e-6, 1e-8

DVE_B, POOL_B = 112, 24


def decoder(nc, x, wq, wk, wv, bq, bk, bv, ctxT, xwqT, xbq, xwk, xbk, xwv4, xbv4, wout, bout,
            mask, wg, w1, w2, out):
    x3d = nc.dram_tensor("x3_rows", (N + P, D), F32, kind="Internal").ap()
    table = nc.dram_tensor("slot_table", (TABLE, 2), U32, kind="Internal").ap()

    base = 16512
    front_at, ffn_at, keep_at = [0], [0], [0]

    def place(name, shape, dt, cursor):
        size = 2 if dt == BF16 else 1 if dt == U8 else 4
        for n in shape[1:]:
            size *= n
        t = nc.alloc_sbuf_tensor_at(name, list(shape), dt, offset=base + cursor[0])
        cursor[0] += (size + 31) // 32 * 32
        return t

    def keep(name, shape, dt=F32):
        return place(name, shape, dt, keep_at)

    ident = keep("ident", [P, P])
    tri = keep("tri", [P, P], BF16)
    onesb = keep("onesb", [P, P], BF16)
    ones = keep("ones", [P, P])
    ones_r = keep("ones_r", [1, P], F32R)
    bq_c = keep("bq_c", [P, KC])
    bk_row = keep("bk_row", [1, D])
    bk_hi = keep("bk_hi", [1, D], F32R)
    bk_lo = keep("bk_lo", [1, D], F32R)
    bv_row = keep("bv_row", [1, D])
    ksum_row = keep("ksum_row", [1, D])
    wqk = keep("wqk", [P, KC, NB * PADW])
    wgp = keep("wgp", [P, KC, PADW])
    sbias = keep("sbias", [P, NB, CK])
    maskf = keep("maskf", [P, NB, CK])
    kv = keep("kv", [P, PAIRS, PW])
    half_neg = keep("half_neg", [P, TI])
    half_pos = keep("half_pos", [P, TI])
    minus1 = keep("minus1", [P, TI])
    iota8 = keep("iota8", [P, EX])
    iota8i = keep("iota8i", [P, EX], I32)
    tok = keep("tok", [P, TI, TOPK])
    toki = keep("toki", [P, TI, TOPK], I32)
    trash = keep("trash", [P, TI, TOPK])
    trashi = keep("trashi", [P, TI, TOPK], I32)
    carry = keep("carry", [P, EX])
    st = keep("st", [P, TI, 6])
    mv = keep("mv", [P, TI, 2])
    rstd = keep("rstd", [P, TI])
    var_e = keep("var_e", [P, TI])
    st2 = keep("st2", [P, TI, 6])
    mv2 = keep("mv2", [P, TI, 2])
    sig = keep("sig", [P, TI, 4])
    den = keep("den", [P, 2, 2, 4])
    zz = keep("zz", [P, 2, 2, 4])
    smax = keep("smax", [P, TI])
    ssum = keep("ssum", [P, TI])
    sinv = keep("sinv", [P, TI])
    lg = keep("lg", [P, TI, EX])
    top = keep("top", [P, TI, EX])
    topi = keep("topi", [P, TI, EX], U32)
    gd = keep("gd", [P, TI])
    ge = keep("ge", [P, TI])
    gs = keep("gs", [P, TI])
    gate = keep("gate", [P, TI, TOPK])
    ef = keep("ef", [P, TI, TOPK])
    oh = keep("oh", [P, TI, TOPK, EX])
    hot = keep("hot", [P, TI, EX], BF16)
    pos = keep("pos", [P, TI, EX])
    ohp = keep("ohp", [P, TI, TOPK, EX])
    pe_ = keep("pe_", [P, TI, TOPK])
    kept = keep("kept", [P, TI, TOPK])
    slot = keep("slot", [P, TI, TOPK])
    dest = keep("dest", [P, TI * TOPK], U32)
    pack = keep("pack", [P, TI * TOPK, 2], U32)
    cnt = keep("cnt", [1, EX])
    more = keep("more", [1, 2, EX])
    need_t = keep("need_t", [1, EX])
    need_i = keep("need_i", [1, EX])
    zero8 = keep("zero8", [1, EX])
    metaf = keep("metaf", [1, 4, EX + 1])
    meta = keep("meta", [1, 4, EX + 1], U32)
    etab_next = keep("etab_next", [P, ET, 2], U32)
    etab = keep("etab", [P, ET, 2], U32)
    tabinit = keep("tabinit", [P, (EX + 1) * ET, 2], I32)
    front_at[0] = ffn_at[0] = keep_at[0]

    def fr(name, shape, dt=F32):
        return place(name, shape, dt, front_at)

    wq_hi, wq_lo, wk_hi, wk_lo = (fr(n, [P, KC, D], F32R) for n in ("wq_hi", "wq_lo", "wk_hi", "wk_lo"))
    x_in = fr("x_in", [P, TI, D])
    xn = fr("xn", [P, TI, D])
    gt_at = front_at[0]
    xT_hi = fr("xT_hi", [P, KC, GT], F32R)
    xT_lo = fr("xT_lo", [P, KC, GT], F32R)
    xn_hi = fr("xn_hi", [P, TI, D], F32R)
    xn_lo = fr("xn_lo", [P, TI, D], F32R)
    raw_at = front_at[0]
    qT = fr("qT", [P, KC, S])
    wv_sb = fr("wv_sb", [P, KC, D])
    k_at = front_at[0]
    k_hi = fr("k_hi", [P, TI, D], F32R)
    k_lo = fr("k_lo", [P, TI, D], F32R)
    k_sum = fr("k_sum", [P, D])
    fe = [fr(f"fe{i}", [P, D]) for i in range(2)]
    frl = [fr(f"frl{i}", [P, D]) for i in range(2)]
    kf = [fr(f"kf{i}", [P, D]) for i in range(2)]
    xr_at = front_at[0]
    xr = [fr(f"xr{i}", [P, TI, D]) for i in range(2)]
    xn2 = xn
    xn3 = fr("xn3", [P, TI, D])
    vp = fr("vp", [CK, NB * D])
    sc = fr("sc", [P, TI, CK])
    sT_at = front_at[0]
    sT = fr("sT", [CK, TI * P])
    assert base + front_at[0] <= nc.sbuf_usable_end, front_at

    def alias(name, shape, dt, at):
        return place(name, shape, dt, [at])

    gT = alias("gT", [P, KC, D], F32, gt_at)
    wq_raw = alias("wq_raw", [P, KC, D], F32, raw_at)
    wk_raw = alias("wk_raw", [P, KC, D], F32, raw_at + 8192)
    xT2 = alias("xT2", [P, KC, GT], F32, k_at)
    xT3 = alias("xT3", [P, KC, GT], F32, k_at + 8192)
    s_at = [xr_at]
    wout_sb = place("wout_sb", [P, KC, D], F32, s_at)
    ctx_sb = place("ctx_sb", [P, KC, NB * CK], F32, s_at)
    xwk_sb = place("xwk_sb", [P, KC, XH], F32, s_at)
    xwv_sb = place("xwv_sb", [P, KC, P], F32, s_at)
    s_at = [xr_at + 16384]
    xwqT_sb = place("xwqT_sb", [XH, D], F32, s_at)
    xbq_sb = place("xbq_sb", [XH, 1], F32, s_at)
    xbk_sb = place("xbk_sb", [XH, 1], F32, s_at)
    xbv_sb = place("xbv_sb", [P, 1], F32, s_at)
    bout_sb = place("bout_sb", [1, D], F32, s_at)
    mask_sb = place("mask_sb", [P, NB * CK], U8, s_at)
    wg_sb = place("wg_sb", [P, KC, EX], F32, s_at)
    kT = place("kT", [XH, NB * CK], F32, s_at)
    vT = place("vT", [P, NB * CK], F32, s_at)
    bq_b = place("bq_b", [XH, P], F32, s_at)
    zrow = alias("zrow", [P, D], F32, sT_at)

    def ff(name, shape, dt=F32):
        return place(name, shape, dt, ffn_at)

    w1_hi = ff("w1_hi", [P, FJ, KC, 2 * P], F32R)
    w1_lo = ff("w1_lo", [P, FJ, KC, 2 * P], F32R)
    stage = [ff(f"stage{i}", [P, 1024]) for i in range(STG)]
    w2_hi = ff("w2_hi", [P, FJ, D], F32R)
    w2_lo = ff("w2_lo", [P, FJ, D], F32R)
    hg_hi = ff("hg_hi", [P, FJ, GT], F32R)
    hg_lo = ff("hg_lo", [P, FJ, GT], F32R)
    xe_hi = ff("xe_hi", [P, KC, GT], F32R)
    xe_lo = ff("xe_lo", [P, KC, GT], F32R)
    xg = ff("xg", [P, TI, D])
    gl = [ff(f"gl{i}", [P, GT]) for i in range(2)]
    hp = [ff(f"hp{i}", [P, GT]) for i in range(2)]
    ost = [ff(f"ost{i}", [P, D]) for i in range(2)]
    assert base + ffn_at[0] <= nc.sbuf_usable_end, ffn_at

    with ExitStack() as ctx:
        pg = ctx.enter_context(nc.psum_tensor("pg", [P, 4, 512], F32))
        pt = [ctx.enter_context(nc.psum_tensor(f"pt{i}", [P, 512], F32)) for i in range(2)]
        pj = [ctx.enter_context(nc.psum_tensor(f"pj{i}", [P, 512], F32)) for i in range(2)]

        def sem(name):
            return ctx.enter_context(nc.semaphore(name))

        s_setup_in = sem("setup_loaded")
        s_const = sem("consts_ready")
        s_pself = sem("pool_setup_step")
        s_dself = sem("dve_setup_step")
        s_whi = sem("front_w_hi")
        s_wlo = sem("front_w_lo")
        s_xset = sem("xattn_psum_ready")
        s_xev = sem("xattn_copied")
        s_vpev = sem("vp_copied")
        s_init = sem("dram_initialised")
        s_xin = sem("x_in_loaded")
        s_stat = sem("stats_ready")
        s_rstd = sem("rstd_ready")
        s_xn = sem("xn_ready")
        s_xnhi = sem("xn_hi_ready")
        s_xnlo = sem("xn_lo_ready")
        s_t = sem("xT_psum_ready")
        s_thi = sem("xT_hi_ready")
        s_tlo = sem("xT_lo_ready")
        s_proj = sem("proj_psum_ready")
        s_feat = sem("exp_relu_ready")
        s_fm = sem("feature_map_ready")
        s_khi = sem("k_hi_ready")
        s_klo = sem("k_lo_ready")
        s_ks = sem("k_sum_added")
        s_g = sem("gT_psum_ready")
        s_gev = sem("gT_copied")
        s_krow = sem("ksum_row_psum_ready")
        s_krev = sem("ksum_row_copied")
        s_kv = sem("kv_psum_ready")
        s_kvev = sem("kv_copied")
        s_dve = sem("dve_step")
        s_pool = sem("pool_step")
        s_xr = sem("x_res_loaded")
        s_o = sem("attn_psum_ready")
        s_oev = sem("attn_scaled")
        s_xn2 = sem("xn2_ready")
        s_bt = sem("B_transposes_ready")
        s_btev = sem("B_transposes_copied")
        s_s = sem("scores_psum_ready")
        s_sev = sem("scores_copied")
        s_s2 = sem("score_stats_ready")
        s_sig = sem("sigma_ready")
        s_ex = sem("score_shifted")
        s_e = sem("score_exp_ready")
        s_x2p = sem("xattn_out_psum_ready")
        s_x2t = sem("x2_tile_ready")
        s_xn3 = sem("xn3_ready")
        s_lgp = sem("logits_psum_ready")
        s_lgev = sem("logits_copied")
        s_gd = sem("gate_diff_ready")
        s_ge = sem("gate_exp_ready")
        s_hot = sem("onehot_ready")
        s_pos = sem("positions_psum_ready")
        s_posev = sem("positions_copied")
        s_dest = sem("slots_ready")
        s_scat = sem("slots_written")
        s_st = sem("x2_x3_stored")
        s_meta = sem("meta_ready")

        s_wst = [sem(f"w_piece_loaded{i}") for i in range(STG)]
        s_w_hi = sem("w_hi_ready")
        s_w_lo = sem("w_lo_ready")
        s_etab = sem("expert_table_loaded")
        s_etc = sem("expert_table_copied")
        s_xg = sem("rows_gathered")
        s_xet = sem("xe_psum_ready")
        s_xehi = sem("xe_hi_ready")
        s_xelo = sem("xe_lo_ready")
        s_h = sem("h_psum_ready")
        s_gl = sem("gelu_ready")
        s_hp = sem("gelu_gate_ready")
        s_hghi = sem("hg_hi_ready")
        s_hglo = sem("hg_lo_ready")
        s_y = sem("expert_out_psum_ready")
        s_yev = sem("expert_out_scaled")
        s_add = sem("rows_added")

        x_g = x.rearrange("(b g i p) d -> b g p i d", b=NB, g=NG, i=TI, p=P)
        out_g = out[0:N, :].rearrange("(b g i p) d -> b g p i d", b=NB, g=NG, i=TI, p=P)
        x3_g = x3d[0:N, :].rearrange("(b g i p) d -> b g p i d", b=NB, g=NG, i=TI, p=P)
        table_t = table[0:TRASH, :].rearrange("(t p) w -> p t w", p=P)
        SETUP_LOADS = 17

        def batch_of(view, b):
            return view[bass.ds(b, 1)].rearrange("o g p i d -> (o g) p i d")

        block = ctx.enter_context(nc.Block())

        def wait(engine, semaphore, value):
            engine.wait_ge(semaphore, value)

        def wait_alone(engine, semaphore, value):
            engine.to_reg(value)
            engine.wait_ge(s_const, 2)
            engine.wait_ge(semaphore, value)

        @block.sync
        def _(sp):
            for dst, src in ((wk_raw[:], wk.rearrange("(k p) n -> p k n", p=P)),
                             (wq_raw[:], wq.rearrange("(k p) n -> p k n", p=P))):
                sp.dma_start(dst, src).then_inc(s_setup_in, 16)
            sp.dma_start(x_in[:], x_g[0, 0]).then_inc(s_xin, 16)
            for dst, src in ((wv_sb[:], wv.rearrange("(k p) n -> p k n", p=P)),
                             (bq_c[:], bq), (bk_row[:], bk), (bv_row[:], bv),
                             (ctx_sb[:], ctxT), (xwqT_sb[:], xwqT), (xbq_sb[:], xbq),
                             (xwk_sb[:], xwk), (xbk_sb[:], xbk), (xwv_sb[:], xwv4),
                             (xbv_sb[:], xbv4), (wout_sb[:], wout.rearrange("(k p) n -> p k n", p=P)),
                             (bout_sb[:], bout), (wg_sb[:], wg),
                             (mask_sb[:], mask.partition_broadcast(P))):
                sp.dma_start(dst, src).then_inc(s_setup_in, 16)
            sp.wait_ge(s_const, 1)
            sp.dma_start(table_t, tabinit[:].bitcast(U32)).then_inc(s_init, 16)
            sp.dma_start(x3d[N:N + P, :], zrow[:]).then_inc(s_init, 16)
            sp.dma_start(out[N:N + P, :], zrow[:]).then_inc(s_init, 16)
            sp.wait_ge(s_vpev, NB)
            sp.wait_ge(s_xev, 3)
            sp.wait_ge(s_init, 48)
            with sp.Fori(0, NB) as b:
                x_b = batch_of(x_g, b)
                out_b, x3_b = batch_of(out_g, b), batch_of(x3_g, b)
                for g in range(1, NG):
                    sp.wait_ge(s_xn, b * NG + g)
                    sp.dma_start(x_in[:], x_b[g]).then_inc(s_xin, 16)
                for g in range(2):
                    sp.dma_start(xr[g][:], x_b[g]).then_inc(s_xr, 16)
                    wait_alone(sp, s_xr, b * 16 * NG + 16 * (g + 1))
                wait_alone(sp, s_xn, b * NG + NG)
                with sp.If(b < NB - 1):
                    sp.dma_start(x_in[:], x_g[NB - 1, 0]).then_inc(s_xin, 16)
                for g in range(NG):
                    sp.wait_ge(s_x2t, (b * NG + g + 1) * TI)
                    sp.dma_start(out_b[g], xr[g % 2][:]).then_inc(s_st, 16)
                    sp.wait_ge(s_xn3, b * NG + g + 1)
                    sp.dma_start(x3_b[g], xn3[:]).then_inc(s_st, 16)
                    wait_alone(sp, s_st, b * 32 * NG + 32 * (g + 1))
                    if g + 2 < NG:
                        sp.dma_start(xr[g % 2][:], x_b[g + 2]).then_inc(s_xr, 16)

            def piece(e, s):
                if s < W1P:
                    return w1[e, s]
                return w2[e].rearrange("(q f p) n -> q p f n", q=W2P, p=P)[s - W1P]

            def dst(s):
                t = stage[s % STG]
                return t[:] if s < W1P else t[:].rearrange("p (f n) -> p f n", f=2)

            sp.wait_ge(s_kv, NB)
            for s in range(WP):
                if s == STG:
                    sp.wait_ge(s_meta, 1)
                    sp.dma_start(etab_next[:], table_t[:, 0:ET]).then_inc(s_etab, 16)
                if s >= STG:
                    sp.wait_ge(s_w_lo, s - STG + 1)
                sp.dma_start(dst(s), piece(0, s)).then_inc(s_wst[s % STG], 16)
            with sp.Fori(1, EX) as e:
                sp.wait_ge(s_etc, e)
                sp.dma_start(etab_next[:], table_t[:, bass.ds(e * ET, ET)]).then_inc(s_etab, 16)
                for s in range(WP):
                    sp.wait_ge(s_w_lo, e * WP + s - STG + 1)
                    if s < W1P:
                        src = w1[bass.ds(e, 1), s].rearrange("o p n -> (o p) n")
                    else:
                        src = w2[bass.ds(e, 1)].rearrange("o (q f p) n -> (o q) p f n",
                                                          q=W2P, p=P)[s - W1P]
                    sp.dma_start(dst(s), src).then_inc(s_wst[s % STG], 16)
            sp.wait_ge(s_etc, EX)
            sp.dma_start(etab_next[:], table_t[:, EX * ET:(EX + 1) * ET]).then_inc(s_etab, 16)
            tiles = sp.value_load(meta[0:1, 1, EX:EX + 1], min_val=0, max_val=EX * ET)
            wait_alone(sp, s_add, 16 * tiles)

        @block.gpsimd
        def _(pool):
            p = nc.gpsimd
            n = [0]

            def step(ins):
                n[0] += 1
                ins.then_inc(s_pself, 1)
                pool.wait_ge(s_pself, n[0])

            step(p.memset(tabinit[:], 0))
            step(p.iota(tabinit[:, :, 0], pattern=[[0, (EX + 1) * ET]], base=N, channel_multiplier=1))
            p.memset(zrow[:], 0.0).then_inc(s_const, 1)
            step(p.memset(ident[:], 0.0))
            step(p.affine_select(out=ident[:], in_=ident[:], compare_op=ALU.not_equal, fill=1.0, base=0,
                                 pattern=[[-1, P]], channel_multiplier=1))
            step(p.memset(onesb[:], 1.0))
            step(p.affine_select(out=tri[:], in_=onesb[:], compare_op=ALU.is_gt, fill=0.0, base=0,
                                 pattern=[[1, P]], channel_multiplier=-1))
            p.memset(ones[:], 1.0)
            p.memset(kv[:], 0.0)
            p.memset(wqk[:], 0.0)
            p.memset(wgp[:], 0.0)
            p.memset(half_neg[:], -0.5)
            p.memset(half_pos[:], 0.5)
            p.memset(minus1[:], -1.0)
            p.memset(carry[:], 0.0)
            p.memset(zero8[:], 0.0)
            p.memset(metaf[:], 0.0)
            p.iota(iota8i[:], pattern=[[1, EX]], base=0, channel_multiplier=0)
            p.iota(toki[:], pattern=[[P, TI], [0, TOPK]], base=0, channel_multiplier=1)
            p.iota(trashi[:], pattern=[[TOPK * P, TI], [P, TOPK]], base=TRASH,
                   channel_multiplier=1).then_inc(s_const, 1)
            pool.wait_ge(s_init, 48)

            with pool.Fori(0, NB) as b:
                n[0] = 0

                def link(ins):
                    n[0] += 1
                    ins.then_inc(s_pool, 1)
                    wait_alone(pool, s_pool, b * POOL_B + n[0])

                ns = [0]

                def rsqrt_var():
                    ns[0] += 1
                    wait_alone(pool, s_stat, b * 3 * NG + ns[0])
                    link(p.tensor_scalar(var_e[:], mv[:, :, 1], LN_EPS, None, ALU.add))
                    p.tensor_tensor(rstd[:], var_e[:], half_neg[:], ALU.pow).then_inc(s_rstd, 1)

                def k_sums(g):
                    for i in range(TI):
                        wait_alone(pool, s_fm, b * NG * 2 * TI + g * 2 * TI + i + 1)
                        if g == 0 and i == 0:
                            ins = p.tensor_copy(k_sum[:], kf[i % 2][:])
                        else:
                            wait_alone(pool, s_ks, b * NG * TI + g * TI + i)
                            ins = p.tensor_tensor(k_sum[:], k_sum[:], kf[i % 2][:], ALU.add)
                        ins.then_inc(s_ks, 1)

                def sigma(g):
                    wait_alone(pool, s_s2, b * NG + g + 1)
                    link(p.tensor_scalar(sig[:, :, 0], mv2[:, :, 1], CK / (CK - 1.0), None, ALU.mult))
                    link(p.tensor_tensor(sig[:, :, 1], sig[:, :, 0], half_pos[:], ALU.pow))
                    link(p.tensor_scalar(sig[:, :, 2], sig[:, :, 1], SIG_EPS, None, ALU.add))
                    p.tensor_tensor(sig[:, :, 3], sig[:, :, 2], minus1[:], ALU.pow).then_inc(s_sig, 1)

                def scatter(g):
                    wait_alone(pool, s_dest, b * NG + g + 1)
                    for c in range(TI * TOPK):
                        p.indirect_dma_start(
                            out=table, out_offset=bass.IndirectOffsetOnAxis(ap=dest[:, c:c + 1], axis=0),
                            in_=pack[:, c, :], in_offset=None).then_inc(s_scat, 16)

                rsqrt_var()
                for g in range(NG):
                    k_sums(g)
                    if g + 1 < NG:
                        rsqrt_var()
                for g in range(NG + 1):
                    if g < NG:
                        rsqrt_var()
                    if g >= 1:
                        rsqrt_var()
                    if g < NG:
                        sigma(g)
                    if g >= 1:
                        scatter(g - 1)
                assert n[0] == POOL_B, n[0]

            def gather(src_tab, t0, tiles):
                for i in range(tiles):
                    p.indirect_dma_start(
                        out=xg[:, i, :], out_offset=None, in_=x3d,
                        in_offset=bass.IndirectOffsetOnAxis(ap=src_tab[:, t0 + i, 0:1], axis=0)
                    ).then_inc(s_xg, 16)

            pool.wait_ge(s_meta, 1)
            pool.wait_ge(s_etab, 16)
            gather(etab_next, 0, CHUNKS[0])
            with pool.Fori(0, EX) as e:
                count = pool.value_load(meta[0:1, 0, bass.ds(e, 1)], min_val=0, max_val=CAP)
                tb = pool.value_load(meta[0:1, 1, bass.ds(e, 1)], min_val=0, max_val=EX * ET)
                wait_alone(pool, s_add, 16 * tb)
                wait_alone(pool, s_xg, 16 * tb + 16 * CHUNKS[0])
                p.tensor_copy(etab[:], etab_next[:]).then_inc(s_etc, 1)
                wait_alone(pool, s_etc, e + 1)

                def ahead(c, tiles, from_next):
                    wait_alone(pool, s_xet, tb + 4 * c + CHUNKS[c])
                    if from_next:
                        wait_alone(pool, s_etab, 16 * (e + 2))
                        gather(etab_next, 0, tiles)
                    else:
                        gather(etab, 4 * (c + 1), tiles)

                def add_rows(c):
                    for i in range(CHUNKS[c]):
                        t = 4 * c + i
                        wait_alone(pool, s_yev, tb + t + 1)
                        wait_alone(pool, s_add, 16 * (tb + t))
                        p.indirect_dma_start(
                            out=out, out_offset=bass.IndirectOffsetOnAxis(ap=etab[:, t, 0:1], axis=0),
                            in_=ost[i % 2][:], in_offset=None, compute_op=ALU.add).then_inc(s_add, 16)

                with pool.If(count > 4 * P):
                    ahead(0, CHUNKS[1], False)
                    add_rows(0)
                    with pool.If(count > 8 * P):
                        ahead(1, CHUNKS[2], False)
                        add_rows(1)
                        ahead(2, CHUNKS[0], True)
                        add_rows(2)
                    with pool.Else():
                        ahead(1, CHUNKS[0], True)
                        add_rows(1)
                with pool.Else():
                    ahead(0, CHUNKS[0], True)
                    add_rows(0)

        @block.scalar
        def _(act):
            a = nc.scalar
            act.wait_ge(s_setup_in, 16 * SETUP_LOADS)
            a.activation(wk_hi[:], wk_raw[:], ACT.Copy).then_inc(s_whi, 1)
            a.activation(wq_hi[:], wq_raw[:], ACT.Copy).then_inc(s_whi, 1)
            act.wait_ge(s_const, 2)
            a.activation(ones_r[:], ones[0:1, :], ACT.Copy)
            a.activation(bk_hi[:], bk_row[:], ACT.Copy).then_inc(s_whi, 1)
            for b in range(NB):
                act.wait_ge(s_xset, 3 + b)
                a.activation(vp[:, b * D:(b + 1) * D], pg[0:CK, b, :], ACT.Copy).then_inc(s_vpev, 1)

            with act.Fori(0, NB) as b:
                JG = 2 * TI

                def turned_hi(g):
                    for k in range(KC):
                        act.wait_ge(s_t, b * NG * KC + g * KC + k + 1)
                        a.activation(xT_hi[:, k, :], pt[k % 2][:], ACT.Copy).then_inc(s_thi, 1)

                def job(g, j):
                    n = b * NG * JG + g * JG + j
                    act.wait_ge(s_proj, n + 1)
                    if g or j >= 2:
                        act.wait_ge(s_fm, n - 1)
                    bias = 0.0 if j < TI else bq_c[:, j - TI:j - TI + 1]
                    a.activation(fe[j % 2][:], pj[j % 2][:], ACT.Exp, bias=bias)
                    a.activation(frl[j % 2][:], pj[j % 2][:], ACT.Relu, bias=bias).then_inc(s_feat, 1)

                def khi(g, i):
                    act.wait_ge(s_fm, b * NG * JG + g * JG + i + 1)
                    a.activation(k_hi[:, i, :], kf[i % 2][:], ACT.Copy).then_inc(s_khi, 1)

                for g in range(NG):
                    turned_hi(g)
                    act.wait_ge(s_xn, b * NG + g + 1)
                    if g:
                        act.wait_ge(s_g, b * NG + g)
                    a.activation(xn_hi[:], xn[:], ACT.Copy).then_inc(s_xnhi, 1)
                    for j in range(JG):
                        job(g, j)
                        if 1 <= j <= TI:
                            khi(g, j - 1)
                act.wait_ge(s_g, (b + 1) * NG)
                for c in range(2):
                    a.activation(gT[:, c, :], pg[:, c, :], ACT.Copy)
                act.wait_ge(s_krow, b + 1)
                a.activation(ksum_row[:], pj[0][0:1, :], ACT.Copy).then_inc(s_krev, 1)

                nt = [0]

                def turned(dst):
                    for k in range(KC):
                        nt[0] += 1
                        act.wait_ge(s_bt, b * (2 * KC + 1) * NG + nt[0])
                        a.activation(dst[:, k, :], pt[0][:], ACT.Copy).then_inc(s_btev, 1)

                for g in range(NG + 1):
                    if g < NG:
                        act.wait_ge(s_xn2, b * NG + g + 1)
                        turned(xT2)
                    if g >= 1:
                        turned(xT3)
                    if g < NG:
                        act.wait_ge(s_ex, b * NG + g + 1)
                        a.activation(sc[:], sc[:], ACT.Exp).then_inc(s_e, 1)
                    if g >= 1:
                        act.wait_ge(s_gd, b * NG + g)
                        a.activation(ge[:], gd[:], ACT.Exp).then_inc(s_ge, 1)
                    if g < NG:
                        nt[0] += 1
                        act.wait_ge(s_bt, b * (2 * KC + 1) * NG + nt[0])
                        a.activation(sT[:], pt[0][0:CK, :], ACT.Copy).then_inc(s_btev, 1)
                assert nt[0] == (2 * KC + 1) * NG

            act.wait_ge(s_meta, 1)

            def w_dst(s):
                return (w1_hi[:, s].rearrange("p k n -> p (k n)") if s < W1P else
                        w2_hi[:, 2 * (s - W1P):2 * (s - W1P) + 2].rearrange("p f n -> p (f n)"))

            def split(e, s, final):
                act.wait_ge(s_wst[s % STG], e * (16 * WP // STG) + 16 * (s // STG + 1))
                if final is not None and s < W1P:
                    act.wait_ge(s_h, final * FJ + s + 1)
                a.activation(w_dst(s), stage[s % STG][:], ACT.Copy).then_inc(s_w_hi, 1)

            def evac_x(first, tiles):
                for i in range(tiles):
                    act.wait_ge(s_xet, first + i + 1)
                    a.activation(xe_hi[:, :, i * P:(i + 1) * P],
                                 pt[i % 2][:].rearrange("p (k t) -> p k t", k=KC), ACT.Copy).then_inc(s_xehi, 1)

            evac_x(0, CHUNKS[0])
            for s in range(WP):
                split(0, s, None)
            with act.Fori(0, EX) as e:
                count = act.value_load(meta[0:1, 0, bass.ds(e, 1)], min_val=0, max_val=CAP)
                tb = act.value_load(meta[0:1, 1, bass.ds(e, 1)], min_val=0, max_val=EX * ET)
                ib = act.value_load(meta[0:1, 2, bass.ds(e, 1)], min_val=0, max_val=EX * 3)
                final = act.value_load(meta[0:1, 3, bass.ds(e + 1, 1)], min_val=0, max_val=EX * 3)
                ntb = act.value_load(meta[0:1, 1, bass.ds(e + 1, 1)], min_val=0, max_val=EX * ET)

                def jobs(c):
                    w = CHUNKS[c] * P
                    act.wait_ge(s_y, tb + 4 * c)
                    for j in range(FJ + 1):
                        if j < FJ:
                            act.wait_ge(s_h, (ib + c) * FJ + j + 1)
                            if j >= 2:
                                act.wait_ge(s_hp, (ib + c) * FJ + j - 1)
                            a.activation(gl[j % 2][:, 0:w], pg[:, j % 2, 0:w], ACT.Gelu).then_inc(s_gl, 1)
                        if j >= 1:
                            act.wait_ge(s_hp, (ib + c) * FJ + j)
                            a.activation(hg_hi[:, j - 1, 0:w], hp[(j - 1) % 2][:, 0:w],
                                         ACT.Copy).then_inc(s_hghi, 1)

                def outs(c, last):
                    per = W1P // CHUNKS[c]
                    for i in range(CHUNKS[c]):
                        t = 4 * c + i
                        if last:
                            with act.If(e < EX - 1):
                                for s in range(i * per, (i + 1) * per):
                                    split(e + 1, s, final)
                        act.wait_ge(s_y, tb + t + 1)
                        act.wait_ge(s_etc, e + 1)
                        if c or i >= 2:
                            act.wait_ge(s_add, 16 * (tb + t - 1))
                        a.activation(ost[i % 2][:], pj[i % 2][:], ACT.Copy,
                                     scale=etab[:, t, 1:2].bitcast(F32)).then_inc(s_yev, 1)

                jobs(0)
                with act.If(count > 4 * P):
                    evac_x(tb + 4, CHUNKS[1])
                    outs(0, False)
                    jobs(1)
                    with act.If(count > 8 * P):
                        evac_x(tb + 8, CHUNKS[2])
                        outs(1, False)
                        jobs(2)
                        evac_x(tb + 10, CHUNKS[0])
                        outs(2, True)
                    with act.Else():
                        evac_x(tb + 8, CHUNKS[0])
                        outs(1, True)
                with act.Else():
                    evac_x(tb + 4, CHUNKS[0])
                    outs(0, True)
                with act.If(e < EX - 1):
                    act.wait_ge(s_y, ntb)
                    for s in range(W1P, WP):
                        split(e + 1, s, final)

        @block.tensor
        def _(pe):
            def three(o, lh, ll, rh, rl, start, stop):
                nc.tensor.matmul(o, lh, rh, start=start, stop=False)
                nc.tensor.matmul(o, lh, rl, start=False, stop=False)
                return nc.tensor.matmul(o, ll, rh, start=False, stop=stop)

            mm = nc.tensor.matmul
            pe.wait_ge(s_setup_in, 16 * SETUP_LOADS)
            pe.wait_ge(s_const, 2)
            for k in range(KC):
                mm(pj[0][0:XH, 0:NB * CK], xwk_sb[:, k, :], ctx_sb[:, k, :], start=k == 0, stop=k == KC - 1)
            for k in range(KC):
                ins = mm(pj[1][:, 0:NB * CK], xwv_sb[:, k, :], ctx_sb[:, k, :], start=k == 0, stop=k == KC - 1)
            ins.then_inc(s_xset, 1)
            pe.wait_ge(s_xev, 1)
            for m in range(KC):
                mm(pt[m // 3][:, m % 3 * NB * CK:(m % 3 + 1) * NB * CK], xwqT_sb[:, m * P:(m + 1) * P], kT[:],
                   start=True, stop=True)
            mm(pt[1][:, NB * CK:2 * NB * CK], bq_b[:], kT[:], start=True, stop=True).then_inc(s_xset, 1)
            for b in range(NB):
                for r in range(KC):
                    mm(pg[0:CK, b, :], vT[:, b * CK:(b + 1) * CK], wout_sb[:, r, :], start=r == 0, stop=False)
                mm(pg[0:CK, b, :], ones[0:1, 0:CK], bout_sb[:], start=False, stop=True).then_inc(s_xset, 1)
            pe.wait_ge(s_xev, 3)
            pe.wait_ge(s_vpev, NB)
            pe.wait_ge(s_wlo, 3)
            pe.wait_ge(s_whi, 3)

            with pe.Fori(0, NB) as b:
                JG = 2 * TI

                def turn(g):
                    pe.wait_ge(s_xn, b * NG + g + 1)
                    for k in range(KC):
                        if g or k >= 2:
                            pe.wait_ge(s_tlo, b * NG * KC + g * KC + k - 1)
                        for i in range(TI):
                            ins = nc.tensor.transpose(pt[k % 2][:, i * P:(i + 1) * P],
                                                      xn[:, i, k * P:(k + 1) * P], ident[:])
                        ins.then_inc(s_t, 1)

                def project(g):
                    for j in range(JG):
                        n = b * NG * JG + g * JG + j
                        if j == 0:
                            pe.wait_ge(s_tlo, b * NG * KC + (g + 1) * KC)
                        if g or j >= 2:
                            pe.wait_ge(s_feat, n - 1)
                        o = pj[j % 2][:]
                        if j < TI:
                            tk = slice(j * P, (j + 1) * P)
                            mm(o, ones_r[:], bk_hi[:], start=True, stop=False)
                            mm(o, ones_r[:], bk_lo[:], start=False, stop=False)
                            for k in range(KC):
                                ins = three(o, xT_hi[:, k, tk], xT_lo[:, k, tk], wk_hi[:, k, :], wk_lo[:, k, :],
                                            False, k == KC - 1)
                        else:
                            m = slice((j - TI) * P, (j - TI + 1) * P)
                            for k in range(KC):
                                ins = three(o, wq_hi[:, k, m], wq_lo[:, k, m], xT_hi[:, k, :], xT_lo[:, k, :],
                                            k == 0, k == KC - 1)
                        ins.then_inc(s_proj, 1)

                def gram(g):
                    pe.wait_ge(s_xnlo, b * NG + g + 1)
                    for i in range(TI):
                        pe.wait_ge(s_klo, b * NG * TI + g * TI + i + 1)
                        for c in range(KC):
                            m = slice(c * P, (c + 1) * P)
                            ins = three(pg[:, c, :], xn_hi[:, i, m], xn_lo[:, i, m], k_hi[:, i, :], k_lo[:, i, :],
                                        g == 0 and i == 0, g == NG - 1 and i == TI - 1)
                    ins.then_inc(s_g, 1)

                turn(0)
                for g in range(NG):
                    project(g)
                    if g + 1 < NG:
                        turn(g + 1)
                    gram(g)

                pe.wait_ge(s_ks, (b + 1) * NG * TI)
                pe.wait_ge(s_feat, (b + 1) * NG * JG)
                mm(pj[0][0:1, :], ones[:, 0:1], k_sum[:], start=True, stop=True).then_inc(s_krow, 1)
                pe.wait_ge(s_krev, b + 1)
                for m in range(KC):
                    mm(pj[1][:, m:m + 1], ksum_row[0:1, m * P:(m + 1) * P], ones[0:1, 0:1], start=True, stop=True)
                pe.wait_ge(s_gev, b + 1)
                for m in range(KC):
                    cols = slice(m * P, (m + 1) * P)
                    for c in range(KC):
                        mm(pt[0][:, cols], gT[:, c, cols], wv_sb[:, c, cols], start=c == 0, stop=False)
                    ins = mm(pt[0][:, cols], ksum_row[0:1, cols], bv_row[0:1, cols], start=False, stop=True)
                ins.then_inc(s_kv, 1)

                def attend(g, tiles):
                    for i in tiles:
                        n = b * NG * TI + g * TI + i
                        if g or i >= 2:
                            pe.wait_ge(s_oev, n - 1)
                        for q in range(PAIRS):
                            ins = mm(pg[:, 2 * (i % 2) + q // 2, (q % 2) * PW:(q % 2 + 1) * PW],
                                     qT[:, q, g * GT + i * P:g * GT + (i + 1) * P], kv[:, q, :], start=True, stop=True)
                        ins.then_inc(s_o, 1)

                nt = [0]
                BT = (2 * KC + 1) * NG

                def bank_free():
                    if nt[0]:
                        pe.wait_ge(s_btev, b * BT + nt[0])
                    nt[0] += 1

                def turn_b(src):
                    for k in range(KC):
                        bank_free()
                        for i in range(TI):
                            ins = nc.tensor.transpose(pt[0][:, i * P:(i + 1) * P], src[:, i, k * P:(k + 1) * P],
                                                      ident[:])
                        ins.then_inc(s_bt, 1)

                def scores(g):
                    pe.wait_ge(s_xn2, b * NG + g + 1)
                    turn_b(xn2)
                    pe.wait_ge(s_btev, b * BT + nt[0])
                    for i in range(TI):
                        for k in range(KC):
                            ins = mm(pj[0][:, i * PADW:(i + 1) * PADW], xT2[:, k, i * P:(i + 1) * P],
                                     wqk[:, k, bass.ds(b * PADW, PADW)], start=k == 0, stop=k == KC - 1)
                    ins.then_inc(s_s, 1)

                def values(g):
                    pe.wait_ge(s_e, b * NG + g + 1)
                    bank_free()
                    for i in range(TI):
                        ins = nc.tensor.transpose(pt[0][0:CK, i * P:(i + 1) * P], sc[:, i, :], ident[:])
                    ins.then_inc(s_bt, 1)
                    pe.wait_ge(s_btev, b * BT + nt[0])
                    for i in range(TI):
                        if i >= 2:
                            pe.wait_ge(s_x2t, b * NG * TI + g * TI + i - 1)
                        bank = pj[1] if i % 2 == 0 else pt[1]
                        mm(bank[:], sT[:, i * P:(i + 1) * P], vp[:, bass.ds(b * D, D)],
                           start=True, stop=True).then_inc(s_x2p, 1)

                def logits(g):
                    pe.wait_ge(s_xn3, b * NG + g + 1)
                    turn_b(xn3)
                    pe.wait_ge(s_btev, b * BT + nt[0])
                    if g + 1 < NG:
                        pe.wait_ge(s_sev, b * NG + g + 2)
                    for i in range(TI):
                        for k in range(KC):
                            ins = mm(pj[0][:, i * PADW:(i + 1) * PADW], xT3[:, k, i * P:(i + 1) * P], wgp[:, k, :],
                                     start=k == 0, stop=k == KC - 1)
                    ins.then_inc(s_lgp, 1)

                def positions(g):
                    pe.wait_ge(s_hot, b * NG + g + 1)
                    bank = pj[0]
                    for i in range(TI):
                        for q in range(i + 1):
                            mm(bank[:, i * EX:(i + 1) * EX], (tri if q == i else onesb)[:], hot[:, q, :],
                               start=q == 0, stop=q == i)
                    for q in range(TI):
                        ins = mm(bank[:, TI * EX:(TI + 1) * EX], onesb[:], hot[:, q, :], start=q == 0, stop=q == TI - 1)
                    ins.then_inc(s_pos, 1)

                pe.wait_ge(s_kvev, b + 1)
                attend(0, range(TI))
                for g in range(NG + 1):
                    if g < NG:
                        scores(g)
                    if g >= 1:
                        logits(g - 1)
                    if g + 1 < NG:
                        attend(g + 1, range(2))
                    if g >= 1:
                        positions(g - 1)
                    if g + 1 < NG:
                        attend(g + 1, range(2, TI))
                    if g < NG:
                        values(g)
                    if g >= 1:
                        pe.wait_ge(s_posev, b * NG + g)

            pe.wait_ge(s_meta, 1)

            def turn_rows(first, tiles):
                pe.wait_ge(s_xg, 16 * (first + tiles))
                for i in range(tiles):
                    if i >= 2:
                        pe.wait_ge(s_xelo, first + i - 1)
                    for k in range(KC):
                        ins = nc.tensor.transpose(pt[i % 2][:, k * P:(k + 1) * P], xg[:, i, k * P:(k + 1) * P], ident[:])
                    ins.then_inc(s_xet, 1)

            turn_rows(0, CHUNKS[0])
            with pe.Fori(0, EX) as e:
                count = pe.value_load(meta[0:1, 0, bass.ds(e, 1)], min_val=0, max_val=CAP)
                tb = pe.value_load(meta[0:1, 1, bass.ds(e, 1)], min_val=0, max_val=EX * ET)
                ib = pe.value_load(meta[0:1, 2, bass.ds(e, 1)], min_val=0, max_val=EX * 3)

                def up(c):
                    w = CHUNKS[c] * P
                    pe.wait_ge(s_xelo, tb + 4 * c + CHUNKS[c])
                    for j in range(FJ):
                        if c == 0:
                            pe.wait_ge(s_w_lo, e * WP + j + 1)
                        if j >= 2:
                            pe.wait_ge(s_hp, (ib + c) * FJ + j - 1)
                        for half in range(2):
                            m = slice(half * P, (half + 1) * P)
                            for k in range(KC):
                                ins = three(pg[:, 2 * half + j % 2, 0:w], w1_hi[:, j, k, m], w1_lo[:, j, k, m],
                                            xe_hi[:, k, 0:w], xe_lo[:, k, 0:w], k == 0, k == KC - 1)
                        ins.then_inc(s_h, 1)

                def down(c):
                    if c == 0:
                        pe.wait_ge(s_w_lo, (e + 1) * WP)
                    for i in range(CHUNKS[c]):
                        m = slice(i * P, (i + 1) * P)
                        pe.wait_ge(s_yev, tb + 4 * c + max(i - 1, 0))
                        for j in range(FJ):
                            if i == 0:
                                pe.wait_ge(s_hglo, (ib + c) * FJ + j + 1)
                            ins = three(pj[i % 2][:], hg_hi[:, j, m], hg_lo[:, j, m], w2_hi[:, j, :], w2_lo[:, j, :],
                                        j == 0, j == FJ - 1)
                        ins.then_inc(s_y, 1)

                up(0)
                with pe.If(count > 4 * P):
                    turn_rows(tb + 4, CHUNKS[1])
                    down(0)
                    up(1)
                    with pe.If(count > 8 * P):
                        turn_rows(tb + 8, CHUNKS[2])
                        down(1)
                        up(2)
                        turn_rows(tb + 10, CHUNKS[0])
                        down(2)
                    with pe.Else():
                        turn_rows(tb + 8, CHUNKS[0])
                        down(1)
                with pe.Else():
                    turn_rows(tb + 4, CHUNKS[0])
                    down(0)

        @block.vector
        def _(dve):
            v = nc.vector
            n = [0]

            def step(ins):
                n[0] += 1
                ins.then_inc(s_dself, 1)
                dve.wait_ge(s_dself, n[0])

            def low(dst, src, hi):
                return v.tensor_tensor(dst, src, hi.bitcast(F32), ALU.subtract)

            dve.wait_ge(s_whi, 1)
            low(wk_lo[:], wk_raw[:], wk_hi[:]).then_inc(s_wlo, 1)
            dve.wait_ge(s_whi, 2)
            low(wq_lo[:], wq_raw[:], wq_hi[:]).then_inc(s_wlo, 1)
            dve.wait_ge(s_setup_in, 16 * SETUP_LOADS)
            v.tensor_copy(bq_b[:], xbq_sb[:].broadcast_to([XH, P]))
            dve.wait_ge(s_xset, 1)
            v.tensor_scalar(kT[:], pj[0][0:XH, 0:NB * CK], xbk_sb[:], float(D) ** -0.5, ALU.add, ALU.mult)
            v.tensor_scalar(vT[:], pj[1][:, 0:NB * CK], xbv_sb[:], None, ALU.add).then_inc(s_xev, 1)
            dve.wait_ge(s_whi, 3)
            low(bk_lo[:], bk_row[:], bk_hi[:]).then_inc(s_wlo, 1)
            dve.wait_ge(s_const, 2)
            dve.wait_ge(s_xset, 2)
            for m in range(KC):
                v.tensor_copy(wqk[:, m, :].rearrange("p (b c) -> p b c", b=NB)[:, :, 0:CK],
                              pt[m // 3][:, m % 3 * NB * CK:(m % 3 + 1) * NB * CK]
                              .rearrange("p (b c) -> p b c", b=NB))
            v.tensor_copy(sbias[:], pt[1][:, NB * CK:2 * NB * CK].rearrange("p (b c) -> p b c", b=NB)
                          ).then_inc(s_xev, 1)
            v.tensor_scalar(maskf[:].rearrange("p b c -> p (b c)"), mask_sb[:], -1e-32, None, ALU.mult)
            v.tensor_copy(iota8[:], iota8i[:])
            v.tensor_copy(tok[:], toki[:])
            v.tensor_copy(trash[:], trashi[:])
            v.tensor_copy(wgp[:, :, 0:EX], wg_sb[:]).then_inc(s_xev, 1)
            dve.wait_ge(s_xev, 3)

            with dve.Fori(0, NB) as b:
                n[0] = 0
                ns = [0]
                JG = 2 * TI

                def link(ins, alone=False):
                    n[0] += 1
                    ins.then_inc(s_dve, 1)
                    (wait_alone if alone else wait)(dve, s_dve, b * DVE_B + n[0])

                def aggregate():
                    for i in range(TI):
                        ins = v.bn_aggr(mv[:, i, :], st[:, i, :])
                    ins.then_inc(s_stat, 1)
                    ns[0] += 1

                def normalise(dst, src):
                    dve.wait_ge(s_rstd, b * 3 * NG + ns[0])
                    for i in range(TI):
                        ins = v.tensor_scalar(dst[:, i, :], src[:, i, :], mv[:, i, 0:1], rstd[:, i:i + 1],
                                              ALU.subtract, ALU.mult)
                    return ins

                def stats_in(g, tiles):
                    if tiles[0] == 0:
                        dve.wait_ge(s_xin, 16 * (b * NG + g + 1))
                    for i in tiles:
                        ins = v.bn_stats(st[:, i, :], x_in[:, i, :])
                    return ins

                def turned_lo(g):
                    for k in range(KC):
                        dve.wait_ge(s_thi, b * NG * KC + g * KC + k + 1)
                        low(xT_lo[:, k, :], pt[k % 2][:], xT_hi[:, k, :]).then_inc(s_tlo, 1)

                def job(g, j):
                    m = b * NG * JG + g * JG + j
                    dve.wait_ge(s_feat, m + 1)
                    if j < TI:
                        if g or j >= 2:
                            dve.wait_ge(s_ks, b * NG * TI + g * TI + j - 1)
                            dve.wait_ge(s_klo, b * NG * TI + g * TI + j - 1)
                        dst = kf[j % 2][:]
                    else:
                        dst = qT[:, j - TI, g * GT:(g + 1) * GT]
                    v.scalar_tensor_tensor(dst, fe[j % 2][:], 1.0, frl[j % 2][:], ALU.min, ALU.add
                                           ).then_inc(s_fm, 1)

                link(stats_in(0, range(TI)), True)
                aggregate()
                normalise(xn, x_in).then_inc(s_xn, 1)
                for g in range(NG):
                    turned_lo(g)
                    dve.wait_ge(s_xnhi, b * NG + g + 1)
                    low(xn_lo[:], xn[:], xn_hi[:]).then_inc(s_xnlo, 1)
                    for j in range(JG):
                        job(g, j)
                        if 1 <= j <= TI:
                            dve.wait_ge(s_khi, b * NG * TI + g * TI + j)
                            dve.wait_ge(s_fm, b * NG * JG + g * JG + j)
                            low(k_lo[:, j - 1, :], kf[(j - 1) % 2][:], k_hi[:, j - 1, :]).then_inc(s_klo, 1)
                        if g + 1 < NG:
                            if j == 0:
                                stats_in(g + 1, range(2))
                            if j == 1:
                                link(stats_in(g + 1, range(2, TI)))
                            if j == 2:
                                aggregate()
                            if j == 5:
                                normalise(xn, x_in).then_inc(s_xn, 1)

                dve.wait_ge(s_g, (b + 1) * NG)
                for c in range(2, KC):
                    ins = v.tensor_copy(gT[:, c, :], pg[:, c, :])
                ins.then_inc(s_gev, 1)
                dve.wait_ge(s_kv, b + 1)
                kvp = pt[0][:].rearrange("p (q c) -> p q c", q=PAIRS)
                v.tensor_copy(kv[0:HD, :, 0:HD], kvp[0:HD, :, 0:HD])
                v.tensor_copy(kv[HD:P, :, HW:HW + HD], kvp[HD:P, :, HD:P])
                v.tensor_copy(kv[0:HD, :, HD], pj[1][0:HD, 0:PAIRS])
                v.tensor_copy(kv[HD:P, :, HW + HD], pj[1][HD:P, 0:PAIRS]).then_inc(s_kvev, 1)

                def attention_out(g):
                    x1 = xr[g % 2]
                    dve.wait_ge(s_xr, 16 * (b * NG + g + 1))
                    for pair in range(TI // 2):
                        for q in range(2):
                            dve.wait_ge(s_o, b * NG * TI + g * TI + 2 * pair + q + 1)
                            ins = v.tensor_scalar(den[:, q], pg[:, 2 * q:2 * q + 2, HD:HD + 3 * HW + 1:HW],
                                                  Z_EPS, None, ALU.add)
                        link(ins)
                        for q in range(2):
                            ins = v.reciprocal(zz[:, q], den[:, q])
                        link(ins)
                        for q in range(2):
                            v.tensor_tensor(
                                fe[q][:].rearrange("p (a h c) -> p a h c", a=2, h=4),
                                pg[:, 2 * q:2 * q + 2, 0:4 * HW].rearrange("p a (h w) -> p a h w", w=HW)[:, :, :, 0:HD],
                                zz[:, q].unsqueeze(3).broadcast_to([P, 2, 4, HD]), ALU.mult).then_inc(s_oev, 1)
                        dve.wait_ge(s_oev, b * NG * TI + g * TI + 2 * pair + 2)
                        for q in range(2):
                            i = 2 * pair + q
                            ins = v.tensor_tensor(x1[:, i, :], x1[:, i, :], fe[q][:], ALU.add)
                        link(ins)
                        for q in range(2):
                            ins = v.bn_stats(st[:, 2 * pair + q, :], x1[:, 2 * pair + q, :])
                    link(ins, True)
                    aggregate()
                    normalise(xn2, x1).then_inc(s_xn2, 1)

                def softmax(g):
                    dve.wait_ge(s_s, b * NG + g + 1)
                    v.tensor_tensor(sc[:], pj[0][:, 0:TI * PADW].rearrange("p (i c) -> p i c", c=PADW)[:, :, 0:CK],
                                    sbias[:, bass.ds(b, 1), :].broadcast_to([P, TI, CK]), ALU.add).then_inc(s_sev, 1)
                    dve.wait_ge(s_sev, b * NG + g + 1)
                    for i in range(TI):
                        ins = v.bn_stats(st2[:, i, :], sc[:, i, :])
                    link(ins, True)
                    for i in range(TI):
                        ins = v.bn_aggr(mv2[:, i, :], st2[:, i, :])
                    ins.then_inc(s_s2, 1)
                    dve.wait_ge(s_sig, b * NG + g + 1)
                    for i in range(TI):
                        ins = v.tensor_scalar(sc[:, i, :], sc[:, i, :], mv2[:, i, 0:1], sig[:, i, 3:4],
                                              ALU.subtract, ALU.mult)
                    link(ins)
                    link(v.tensor_tensor(sc[:], sc[:], maskf[:, bass.ds(b, 1), :].broadcast_to([P, TI, CK]), ALU.add))
                    link(v.tensor_reduce(smax[:], sc[:], AX.X, ALU.max))
                    v.tensor_tensor(sc[:], sc[:], smax[:].unsqueeze(2).broadcast_to([P, TI, CK]),
                                    ALU.subtract).then_inc(s_ex, 1)

                def cross_out(g):
                    x2 = xr[g % 2]
                    dve.wait_ge(s_e, b * NG + g + 1)
                    link(v.tensor_reduce(ssum[:], sc[:], AX.X, ALU.add))
                    link(v.reciprocal(sinv[:], ssum[:]))
                    for i in range(TI + 1):
                        m = b * NG * TI + g * TI + i
                        if i < TI:
                            dve.wait_ge(s_x2p, m + 1)
                            bank = pj[1] if i % 2 == 0 else pt[1]
                            v.scalar_tensor_tensor(x2[:, i, :], bank[:], sinv[:, i:i + 1], x2[:, i, :],
                                                   ALU.mult, ALU.add).then_inc(s_x2t, 1)
                        if i >= 1:
                            dve.wait_ge(s_x2t, m)
                            ins = v.bn_stats(st[:, i - 1, :], x2[:, i - 1, :])
                    link(ins, True)
                    aggregate()
                    dve.wait_ge(s_st, 32 * (b * NG + g))
                    normalise(xn3, x2).then_inc(s_xn3, 1)

                def route(g):
                    dve.wait_ge(s_lgp, b * NG + g + 1)
                    v.tensor_copy(lg[:], pj[0][:, 0:TI * PADW].rearrange("p (i c) -> p i c", c=PADW)[:, :, 0:EX]
                                  ).then_inc(s_lgev, 1)
                    wait_alone(dve, s_lgev, b * NG + g + 1)
                    for i in range(TI):
                        ins = v.max(top[:, i, :], lg[:, i, :])
                    link(ins, True)
                    for i in range(TI):
                        ins = v.max_index(topi[:, i, :], top[:, i, :], lg[:, i, :])
                    v.tensor_tensor(gd[:], top[:, :, 1], top[:, :, 0], ALU.subtract).then_inc(s_gd, 1)
                    dve.wait_ge(s_gd, b * NG + g + 1)
                    link(v.tensor_copy(ef[:], topi[:, :, 0:TOPK]))
                    link(v.tensor_tensor(oh[:].rearrange("p i k e -> p (i k) e"),
                                         ef[:].rearrange("p i k -> p (i k)").unsqueeze(2).broadcast_to([P, TI * TOPK, EX]),
                                         iota8[:].unsqueeze(1).broadcast_to([P, TI * TOPK, EX]), ALU.is_equal))
                    v.tensor_tensor(hot[:], oh[:, :, 0, :], oh[:, :, 1, :], ALU.add).then_inc(s_hot, 1)
                    dve.wait_ge(s_ge, b * NG + g + 1)
                    link(v.tensor_scalar(gs[:], ge[:], 1.0, None, ALU.add))
                    link(v.reciprocal(gate[:, :, 0], gs[:]))
                    link(v.tensor_tensor(gate[:, :, 1], ge[:], gate[:, :, 0], ALU.mult))

                def place_tokens(g):
                    dve.wait_ge(s_pos, b * NG + g + 1)
                    link(v.tensor_tensor(pos[:], pj[0][:, 0:TI * EX].rearrange("p (i e) -> p i e", e=EX),
                                         carry[:].unsqueeze(1).broadcast_to([P, TI, EX]), ALU.add))
                    v.tensor_tensor(carry[:], pj[0][:, TI * EX:(TI + 1) * EX], carry[:], ALU.add).then_inc(s_posev, 1)
                    link(v.tensor_tensor(ohp[:], oh[:], pos[:].unsqueeze(2).broadcast_to([P, TI, TOPK, EX]), ALU.mult))
                    link(v.tensor_reduce(pe_[:], ohp[:], AX.X, ALU.add))
                    v.scalar_tensor_tensor(slot[:], ef[:], float(CAP), pe_[:], ALU.mult, ALU.add)
                    link(v.tensor_scalar(kept[:], pe_[:], float(CAP), None, ALU.is_lt))
                    link(v.tensor_tensor(slot[:], slot[:], trash[:], ALU.subtract))
                    link(v.tensor_tensor(slot[:], slot[:], kept[:], ALU.mult))
                    dve.wait_ge(s_scat, 16 * TI * TOPK * (b * NG + g))
                    v.tensor_tensor(dest[:], slot[:].rearrange("p i k -> p (i k)"),
                                    trash[:].rearrange("p i k -> p (i k)"), ALU.add)
                    v.tensor_copy(pack[:, :, 0], tok[:].rearrange("p i k -> p (i k)"))
                    v.tensor_copy(pack[:].bitcast(F32)[:, :, 1],
                                  gate[:].rearrange("p i k -> p (i k)")).then_inc(s_dest, 1)
                    dve.wait_ge(s_dest, b * NG + g + 1)
                    v.tensor_scalar(tok[:], tok[:], float(GT), None, ALU.add)
                    link(v.tensor_scalar(trash[:], trash[:], float(GT * TOPK), None, ALU.add))

                for g in range(NG + 1):
                    if g < NG:
                        attention_out(g)
                    if g >= 1:
                        cross_out(g - 1)
                    if g < NG:
                        softmax(g)
                    if g >= 1:
                        route(g - 1)
                        place_tokens(g - 1)
                assert n[0] == DVE_B, n[0]

            dve.wait_ge(s_scat, 16 * TI * TOPK * NB * NG)
            dve.wait_ge(s_st, 32 * NB * NG)
            n[0] = 0
            step(v.tensor_scalar(cnt[:], carry[0:1, :], float(CAP), None, ALU.min))
            v.tensor_copy(metaf[:, 0, 0:EX], cnt[:])
            v.tensor_scalar(more[:, 0, :], cnt[:], float(CHUNKS[0] * P), None, ALU.is_gt)
            step(v.tensor_scalar(more[:, 1, :], cnt[:], float((CHUNKS[0] + CHUNKS[1]) * P), None, ALU.is_gt))
            v.scalar_tensor_tensor(need_i[:], more[:, 0, :], 1.0, more[:, 1, :], ALU.add, ALU.add)
            step(v.tensor_scalar(need_t[:], more[:, 0, :], float(CHUNKS[1]), float(CHUNKS[0]), ALU.mult, ALU.add))
            step(v.scalar_tensor_tensor(need_t[:], more[:, 1, :], float(CHUNKS[2]), need_t[:], ALU.mult, ALU.add))
            v.tensor_tensor_scan(metaf[:, 1, 1:EX + 1], need_t[:], zero8[:], 0.0, ALU.add, ALU.add)
            step(v.tensor_tensor_scan(metaf[:, 2, 1:EX + 1], need_i[:], zero8[:], 0.0, ALU.add, ALU.add))
            step(v.tensor_scalar(metaf[:, 3, 1:EX + 1], metaf[:, 2, 1:EX + 1], 1.0, None, ALU.subtract))
            v.tensor_copy(meta[:], metaf[:]).then_inc(s_meta, 1)
            dve.wait_ge(s_meta, 1)

            def w_parts(s):
                if s < W1P:
                    return [t[:, s].rearrange("p k n -> p (k n)") for t in (w1_lo, w1_hi)]
                return [t[:, 2 * (s - W1P):2 * (s - W1P) + 2].rearrange("p f n -> p (f n)") for t in (w2_lo, w2_hi)]

            def split(e, s):
                dve.wait_ge(s_w_hi, e * WP + s + 1)
                lo, hi = w_parts(s)
                low(lo, stage[s % STG][:], hi).then_inc(s_w_lo, 1)

            def evac_x(first, tiles):
                for i in range(tiles):
                    dve.wait_ge(s_xehi, first + i + 1)
                    low(xe_lo[:, :, i * P:(i + 1) * P], pt[i % 2][:].rearrange("p (k t) -> p k t", k=KC),
                        xe_hi[:, :, i * P:(i + 1) * P]).then_inc(s_xelo, 1)

            evac_x(0, CHUNKS[0])
            for s in range(WP):
                split(0, s)
            with dve.Fori(0, EX) as e:
                count = dve.value_load(meta[0:1, 0, bass.ds(e, 1)], min_val=0, max_val=CAP)
                tb = dve.value_load(meta[0:1, 1, bass.ds(e, 1)], min_val=0, max_val=EX * ET)
                ib = dve.value_load(meta[0:1, 2, bass.ds(e, 1)], min_val=0, max_val=EX * 3)

                def jobs(c):
                    w = CHUNKS[c] * P
                    for j in range(FJ + 1):
                        if j < FJ:
                            dve.wait_ge(s_gl, (ib + c) * FJ + j + 1)
                            dve.wait_ge(s_hglo, (ib + c) * FJ + max(j - 1, 0))
                            v.tensor_tensor(hp[j % 2][:, 0:w], gl[j % 2][:, 0:w], pg[:, 2 + j % 2, 0:w],
                                            ALU.mult).then_inc(s_hp, 1)
                        if j >= 1:
                            dve.wait_ge(s_hghi, (ib + c) * FJ + j)
                            dve.wait_ge(s_hp, (ib + c) * FJ + j)
                            low(hg_lo[:, j - 1, 0:w], hp[(j - 1) % 2][:, 0:w],
                                hg_hi[:, j - 1, 0:w]).then_inc(s_hglo, 1)

                jobs(0)
                with dve.If(count > 4 * P):
                    evac_x(tb + 4, CHUNKS[1])
                    jobs(1)
                    with dve.If(count > 8 * P):
                        evac_x(tb + 8, CHUNKS[2])
                        jobs(2)
                        evac_x(tb + 10, CHUNKS[0])
                    with dve.Else():
                        evac_x(tb + 8, CHUNKS[0])
                with dve.Else():
                    evac_x(tb + 4, CHUNKS[0])
                with dve.If(e < EX - 1):
                    for s in range(WP):
                        split(e + 1, s)


def kernel(x, ctx_1024, mask_BxS2_bk0, L0_attn_Wq, L0_attn_bq, L0_attn_Wk, L0_attn_bk, L0_attn_Wv,
           L0_attn_bv, L0_xattn_Wq, L0_xattn_bq, L0_xattn_Wk, L0_xattn_bk, L0_xattn_Wv, L0_xattn_bv,
           L0_xattn_Wout, L0_xattn_bout, L0_ffn_Wg, L0_ffn_W1, L0_ffn_W2):
    import numpy as np
    import concourse.bacc as bacc
    from concourse.bass_utils import run_bass_kernel_spmd

    def a(t):
        return np.asarray(t)

    arrays = {
        "x": a(x).reshape(N, D),
        "wq": a(L0_attn_Wq), "wk": a(L0_attn_Wk), "wv": a(L0_attn_Wv),
        "bq": a(L0_attn_bq).reshape(KC, P).T, "bk": a(L0_attn_bk).reshape(1, D), "bv": a(L0_attn_bv).reshape(1, D),
        "ctxT": a(ctx_1024).reshape(NB * CK, KC, P).transpose(2, 1, 0),
        "xwqT": a(L0_xattn_Wq).T, "xbq": a(L0_xattn_bq).reshape(XH, 1),
        "xwk": a(L0_xattn_Wk).reshape(KC, P, XH).transpose(1, 0, 2), "xbk": a(L0_xattn_bk).reshape(XH, 1),
        "xwv4": np.tile(a(L0_xattn_Wv), (1, P // XH)).reshape(KC, P, P).transpose(1, 0, 2),
        "xbv4": np.tile(a(L0_xattn_bv), P // XH).reshape(P, 1),
        "wout": a(L0_xattn_Wout), "bout": a(L0_xattn_bout).reshape(1, D),
        "mask": a(mask_BxS2_bk0).reshape(NB * CK),
        "wg": a(L0_ffn_Wg).reshape(EX, KC, P).transpose(2, 1, 0),
        "w1": a(L0_ffn_W1).reshape(EX, KC, P, 2, FJ, P).transpose(0, 4, 2, 1, 3, 5).reshape(EX, FJ, P, 1024),
        "w2": a(L0_ffn_W2),
    }
    nc = bacc.Bacc("TRN2", target_bir_lowering=False, num_devices=1)
    args = {}
    for name, value in arrays.items():
        arrays[name] = value = np.ascontiguousarray(value)
        args[name] = nc.dram_tensor(name, value.shape, mybir.dt.from_np(value.dtype), kind="ExternalInput").ap()
    args["out"] = nc.dram_tensor("out_rows", (N + P, D), F32, kind="ExternalOutput").ap()
    decoder(nc, **args)
    r = run_bass_kernel_spmd(nc, [arrays], core_ids=[0])
    return r.results[0]["out_rows"][:N].reshape(NB, S, D)
```

```python
from contextlib import ExitStack

import concourse.bass as bass
from concourse import mybir

F32 = mybir.dt.float32
F32R = mybir.dt.float32r
BF16 = mybir.dt.bfloat16
U32 = mybir.dt.uint32
I32 = mybir.dt.int32
U8 = mybir.dt.uint8
ALU = mybir.AluOpType
ACT = mybir.ActivationFunctionType
AX = mybir.AxisListType

P = 128
D = 512
KC = D // P
NB, S = 2, 2048
N = NB * S
GT = 512
NG = S // GT
TI = GT // P
H, HD = 8, 64
PAIRS = H // 2
HW = HD + 1
PW = 2 * HW
CK, XH = 77, 32
PADW = 96
EX, TOPK, INNER = 8, 2, 1024
CAP = int(N * TOPK * 1.25 / EX)
ET = CAP // P
FJ = INNER // P
W1P, W2P = FJ, FJ // 2
WP = W1P + W2P
STG = 4
CHUNKS = [4, 4, 2]
POS = TI * PADW
SLOTS = EX * CAP
PHANTOM = CAP
TRASH = SLOTS + PHANTOM
TABLE = TRASH + N * TOPK
LN_EPS, Z_EPS, SIG_EPS = 1e-5, 1e-6, 1e-8

DVE_B, POOL_B = 112, 32


def decoder(nc, x, wq, wk, wv, bq, bk, bv, ctxT, xwqT, xbq, xwk, xbk, xwv4, xbv4, wout, bout,
            mask, wg, w1, w2, out):
    x3d = nc.dram_tensor("x3_rows", (N + P, D), F32, kind="Internal").ap()
    table = nc.dram_tensor("slot_table", (TABLE, 2), U32, kind="Internal").ap()

    base = 16512
    front_at, ffn_at, keep_at = [0], [0], [0]

    def place(name, shape, dt, cursor):
        size = 2 if dt == BF16 else 1 if dt == U8 else 4
        for n in shape[1:]:
            size *= n
        t = nc.alloc_sbuf_tensor_at(name, list(shape), dt, offset=base + cursor[0])
        cursor[0] += (size + 31) // 32 * 32
        return t

    def keep(name, shape, dt=F32):
        return place(name, shape, dt, keep_at)

    ident = keep("ident", [P, P])
    tri = keep("tri", [P, P], BF16)
    onesb = keep("onesb", [P, P], BF16)
    ones = keep("ones", [P, P])
    ones_r = keep("ones_r", [1, P], F32R)
    bq_c = keep("bq_c", [P, KC])
    bk_row = keep("bk_row", [1, D])
    bk_hi = keep("bk_hi", [1, D], F32R)
    bk_lo = keep("bk_lo", [1, D], F32R)
    bv_row = keep("bv_row", [1, D])
    ksum_row = keep("ksum_row", [1, D])
    wqk = keep("wqk", [P, KC, NB * PADW])
    wgp = keep("wgp", [P, KC, PADW])
    sbias = keep("sbias", [P, NB, CK])
    maskf = keep("maskf", [P, NB, CK])
    kv = keep("kv", [P, PAIRS, PW])
    half_neg = keep("half_neg", [P, TI])
    half_pos = keep("half_pos", [P, TI])
    minus1 = keep("minus1", [P, TI])
    iota8 = keep("iota8", [P, EX])
    iota8i = keep("iota8i", [P, EX], I32)
    tok = keep("tok", [P, TI, TOPK])
    toki = keep("toki", [P, TI, TOPK], I32)
    trash = keep("trash", [P, TI, TOPK])
    trashi = keep("trashi", [P, TI, TOPK], I32)
    carry = keep("carry", [P, EX])
    st, mv = ([keep(f"{n}{q}", [P, TI, w]) for q in range(2)] for n, w in (("st", 6), ("mv", 2)))
    var_e, rstd, neg_mean, shift = ([keep(f"{n}{q}", [P, TI]) for q in range(2)]
                                    for n in ("var_e", "rstd", "neg_mean", "shift"))
    st2 = keep("st2", [P, TI, 6])
    mv2 = keep("mv2", [P, TI, 2])
    sig = keep("sig", [P, TI, 4])
    den = keep("den", [P, 2, 2, 4])
    zz = keep("zz", [P, 2, 2, 4])
    smax = keep("smax", [P, TI])
    ssum = keep("ssum", [P, TI])
    sinv = keep("sinv", [P, TI])
    lg = keep("lg", [P, TI, EX])
    top = keep("top", [P, TI, EX])
    topi = keep("topi", [P, TI, EX], U32)
    gd = keep("gd", [P, TI])
    ge = keep("ge", [P, TI])
    gs = keep("gs", [P, TI])
    gate = keep("gate", [P, TI, TOPK])
    ef = keep("ef", [P, TI, TOPK])
    oh = keep("oh", [P, TI, TOPK, EX])
    hot = keep("hot", [P, TI, EX], BF16)
    pos = keep("pos", [P, TI, EX])
    ohp = keep("ohp", [P, TI, TOPK, EX])
    pe_ = keep("pe_", [P, TI, TOPK])
    kept = keep("kept", [P, TI, TOPK])
    slot = keep("slot", [P, TI, TOPK])
    dest = keep("dest", [P, TI * TOPK], U32)
    pack = keep("pack", [P, TI * TOPK, 2], U32)
    cnt = keep("cnt", [1, EX])
    more = keep("more", [1, 2, EX])
    need_t = keep("need_t", [1, EX])
    need_i = keep("need_i", [1, EX])
    zero8 = keep("zero8", [1, EX])
    metaf = keep("metaf", [1, 4, EX + 1])
    meta = keep("meta", [1, 4, EX + 1], U32)
    etab_next = keep("etab_next", [P, ET, 2], U32)
    etab = keep("etab", [P, ET, 2], U32)
    tabinit = keep("tabinit", [P, (EX + 1) * ET, 2], I32)
    front_at[0] = ffn_at[0] = keep_at[0]

    def fr(name, shape, dt=F32):
        return place(name, shape, dt, front_at)

    wq_hi, wq_lo, wk_hi, wk_lo = (fr(n, [P, KC, D], F32R) for n in ("wq_hi", "wq_lo", "wk_hi", "wk_lo"))
    x_in = fr("x_in", [P, TI, D])
    xn = fr("xn", [P, TI, D])
    gt_at = front_at[0]
    xT_hi = fr("xT_hi", [P, KC, GT], F32R)
    xT_lo = fr("xT_lo", [P, KC, GT], F32R)
    xn_hi = fr("xn_hi", [P, TI, D], F32R)
    xn_lo = fr("xn_lo", [P, TI, D], F32R)
    raw_at = front_at[0]
    qT = fr("qT", [P, KC, S])
    wv_sb = fr("wv_sb", [P, KC, D])
    k_at = front_at[0]
    k_hi = fr("k_hi", [P, TI, D], F32R)
    k_lo = fr("k_lo", [P, TI, D], F32R)
    k_sum = fr("k_sum", [P, D])
    fe = [fr(f"fe{i}", [P, D]) for i in range(2)]
    frl = [fr(f"frl{i}", [P, D]) for i in range(2)]
    kf = [fr(f"kf{i}", [P, D]) for i in range(2)]
    xr_at = front_at[0]
    xr = [fr(f"xr{i}", [P, TI, D]) for i in range(2)]
    xn2 = xn
    xn3 = fr("xn3", [P, TI, D])
    vp = fr("vp", [CK, NB * D])
    sc = fr("sc", [P, TI, CK])
    sT_at = front_at[0]
    sT = fr("sT", [CK, TI * P])
    assert base + front_at[0] <= nc.sbuf_usable_end, front_at

    def alias(name, shape, dt, at):
        return place(name, shape, dt, [at])

    gT = alias("gT", [P, KC, D], F32, gt_at)
    wq_raw = alias("wq_raw", [P, KC, D], F32, raw_at)
    wk_raw = alias("wk_raw", [P, KC, D], F32, raw_at + 8192)
    xT2 = alias("xT2", [P, KC, GT], F32, k_at)
    xT3 = alias("xT3", [P, KC, GT], F32, k_at + 8192)
    s_at = [xr_at]
    wout_sb = place("wout_sb", [P, KC, D], F32, s_at)
    ctx_sb = place("ctx_sb", [P, KC, NB * CK], F32, s_at)
    xwk_sb = place("xwk_sb", [P, KC, XH], F32, s_at)
    xwv_sb = place("xwv_sb", [P, KC, P], F32, s_at)
    s_at = [xr_at + 16384]
    xwqT_sb = place("xwqT_sb", [XH, D], F32, s_at)
    xbq_sb = place("xbq_sb", [XH, 1], F32, s_at)
    xbk_sb = place("xbk_sb", [XH, 1], F32, s_at)
    xbv_sb = place("xbv_sb", [P, 1], F32, s_at)
    bout_sb = place("bout_sb", [1, D], F32, s_at)
    mask_sb = place("mask_sb", [P, NB * CK], U8, s_at)
    wg_sb = place("wg_sb", [P, KC, EX], F32, s_at)
    kT = place("kT", [XH, NB * CK], F32, s_at)
    vT = place("vT", [P, NB * CK], F32, s_at)
    bq_b = place("bq_b", [XH, P], F32, s_at)
    zrow = alias("zrow", [P, D], F32, sT_at)

    def ff(name, shape, dt=F32):
        return place(name, shape, dt, ffn_at)

    w1_hi = ff("w1_hi", [P, FJ, KC, 2 * P], F32R)
    w1_lo = ff("w1_lo", [P, FJ, KC, 2 * P], F32R)
    stage = [ff(f"stage{i}", [P, 1024]) for i in range(STG)]
    w2_hi = ff("w2_hi", [P, FJ, D], F32R)
    w2_lo = ff("w2_lo", [P, FJ, D], F32R)
    hg_hi = ff("hg_hi", [P, FJ, GT], F32R)
    hg_lo = ff("hg_lo", [P, FJ, GT], F32R)
    xe_hi = ff("xe_hi", [P, KC, GT], F32R)
    xe_lo = ff("xe_lo", [P, KC, GT], F32R)
    xg = ff("xg", [P, TI, D])
    gl = [ff(f"gl{i}", [P, GT]) for i in range(2)]
    hp = [ff(f"hp{i}", [P, GT]) for i in range(2)]
    ost = [ff(f"ost{i}", [P, D]) for i in range(2)]
    assert base + ffn_at[0] <= nc.sbuf_usable_end, ffn_at

    with ExitStack() as ctx:
        pg = ctx.enter_context(nc.psum_tensor("pg", [P, 4, 512], F32))
        pt = [ctx.enter_context(nc.psum_tensor(f"pt{i}", [P, 512], F32)) for i in range(2)]
        pj = [ctx.enter_context(nc.psum_tensor(f"pj{i}", [P, 512], F32)) for i in range(2)]

        def sem(name):
            return ctx.enter_context(nc.semaphore(name))

        s_setup_in = sem("setup_loaded")
        s_const = sem("consts_ready")
        s_pself = sem("pool_setup_step")
        s_dself = sem("dve_setup_step")
        s_whi = sem("front_w_hi")
        s_wlo = sem("front_w_lo")
        s_xset = sem("xattn_psum_ready")
        s_xev = sem("xattn_copied")
        s_vpev = sem("vp_copied")
        s_init = sem("dram_initialised")
        s_xin = sem("x_in_loaded")
        s_stat = sem("stats_ready")
        s_stat2 = sem("second_stats_ready")
        s_rstd = sem("rstd_ready")
        s_rstd2 = sem("second_rstd_ready")
        s_xn = sem("xn_ready")
        s_xnhi = sem("xn_hi_ready")
        s_xnlo = sem("xn_lo_ready")
        s_t = sem("xT_psum_ready")
        s_thi = sem("xT_hi_ready")
        s_tlo = sem("xT_lo_ready")
        s_proj = sem("proj_psum_ready")
        s_feat = sem("exp_relu_ready")
        s_fm = sem("feature_map_ready")
        s_khi = sem("k_hi_ready")
        s_klo = sem("k_lo_ready")
        s_ks = sem("k_sum_added")
        s_g = sem("gT_psum_ready")
        s_gev = sem("gT_copied")
        s_krow = sem("ksum_row_psum_ready")
        s_krev = sem("ksum_row_copied")
        s_kv = sem("kv_psum_ready")
        s_kvev = sem("kv_copied")
        s_dve = sem("dve_step")
        s_pool = sem("pool_step")
        s_xr = sem("x_res_loaded")
        s_o = sem("attn_psum_ready")
        s_oev = sem("attn_scaled")
        s_xn2 = sem("xn2_ready")
        s_bt = sem("B_transposes_ready")
        s_btev = sem("B_transposes_copied")
        s_s = sem("scores_psum_ready")
        s_sev = sem("scores_copied")
        s_s2 = sem("score_stats_ready")
        s_sig = sem("sigma_ready")
        s_ex = sem("score_shifted")
        s_e = sem("score_exp_ready")
        s_x2p = sem("xattn_out_psum_ready")
        s_x2t = sem("x2_tile_ready")
        s_xn3 = sem("xn3_ready")
        s_lgp = sem("logits_psum_ready")
        s_lgev = sem("logits_copied")
        s_gd = sem("gate_diff_ready")
        s_ge = sem("gate_exp_ready")
        s_hot = sem("onehot_ready")
        s_pos = sem("positions_psum_ready")
        s_posev = sem("positions_copied")
        s_dest = sem("slots_ready")
        s_scat = sem("slots_written")
        s_st = sem("x2_x3_stored")
        s_meta = sem("meta_ready")

        s_wst = [sem(f"w_piece_loaded{i}") for i in range(STG)]
        s_w_hi = sem("w_hi_ready")
        s_w_lo = sem("w_lo_ready")
        s_etab = sem("expert_table_loaded")
        s_etc = sem("expert_table_copied")
        s_xg = sem("rows_gathered")
        s_xet = sem("xe_psum_ready")
        s_xehi = sem("xe_hi_ready")
        s_xelo = sem("xe_lo_ready")
        s_h = sem("h_psum_ready")
        s_gl = sem("gelu_ready")
        s_hp = sem("gelu_gate_ready")
        s_hghi = sem("hg_hi_ready")
        s_hglo = sem("hg_lo_ready")
        s_y = sem("expert_out_psum_ready")
        s_yev = sem("expert_out_scaled")
        s_add = sem("rows_added")

        x_g = x.rearrange("(b g i p) d -> b g p i d", b=NB, g=NG, i=TI, p=P)
        out_g = out[0:N, :].rearrange("(b g i p) d -> b g p i d", b=NB, g=NG, i=TI, p=P)
        x3_g = x3d[0:N, :].rearrange("(b g i p) d -> b g p i d", b=NB, g=NG, i=TI, p=P)
        table_t = table[0:TRASH, :].rearrange("(t p) w -> p t w", p=P)
        SETUP_LOADS = 17

        def batch_of(view, b):
            return view[bass.ds(b, 1)].rearrange("o g p i d -> (o g) p i d")

        block = ctx.enter_context(nc.Block())

        def wait(engine, semaphore, value):
            engine.wait_ge(semaphore, value)

        def wait_alone(engine, semaphore, value):
            engine.to_reg(value)
            engine.wait_ge(s_const, 2)
            engine.wait_ge(semaphore, value)

        @block.sync
        def _(sp):
            for dst, src in ((wk_raw[:], wk.rearrange("(k p) n -> p k n", p=P)),
                             (wq_raw[:], wq.rearrange("(k p) n -> p k n", p=P))):
                sp.dma_start(dst, src).then_inc(s_setup_in, 16)
            sp.dma_start(x_in[:], x_g[0, 0]).then_inc(s_xin, 16)
            for dst, src in ((wv_sb[:], wv.rearrange("(k p) n -> p k n", p=P)),
                             (bq_c[:], bq), (bk_row[:], bk), (bv_row[:], bv),
                             (ctx_sb[:], ctxT), (xwqT_sb[:], xwqT), (xbq_sb[:], xbq),
                             (xwk_sb[:], xwk), (xbk_sb[:], xbk), (xwv_sb[:], xwv4),
                             (xbv_sb[:], xbv4), (wout_sb[:], wout.rearrange("(k p) n -> p k n", p=P)),
                             (bout_sb[:], bout), (wg_sb[:], wg),
                             (mask_sb[:], mask.partition_broadcast(P))):
                sp.dma_start(dst, src).then_inc(s_setup_in, 16)
            sp.wait_ge(s_const, 1)
            sp.dma_start(table_t, tabinit[:].bitcast(U32)).then_inc(s_init, 16)
            sp.dma_start(x3d[N:N + P, :], zrow[:]).then_inc(s_init, 16)
            sp.dma_start(out[N:N + P, :], zrow[:]).then_inc(s_init, 16)
            sp.wait_ge(s_vpev, NB)
            sp.wait_ge(s_xev, 3)
            sp.wait_ge(s_init, 48)
            with sp.Fori(0, NB) as b:
                x_b = batch_of(x_g, b)
                out_b, x3_b = batch_of(out_g, b), batch_of(x3_g, b)
                for g in range(1, NG):
                    sp.wait_ge(s_xn, b * NG + g)
                    sp.dma_start(x_in[:], x_b[g]).then_inc(s_xin, 16)
                for g in range(2):
                    sp.dma_start(xr[g][:], x_b[g]).then_inc(s_xr, 16)
                    wait_alone(sp, s_xr, b * 16 * NG + 16 * (g + 1))
                wait_alone(sp, s_xn, b * NG + NG)
                with sp.If(b < NB - 1):
                    sp.dma_start(x_in[:], x_g[NB - 1, 0]).then_inc(s_xin, 16)
                for g in range(NG):
                    sp.wait_ge(s_x2t, (b * NG + g + 1) * TI)
                    sp.dma_start(out_b[g], xr[g % 2][:]).then_inc(s_st, 16)
                    sp.wait_ge(s_xn3, (b * NG + g + 1) * TI)
                    sp.dma_start(x3_b[g], xn3[:]).then_inc(s_st, 16)
                    wait_alone(sp, s_st, b * 32 * NG + 32 * (g + 1))
                    if g + 2 < NG:
                        sp.dma_start(xr[g % 2][:], x_b[g + 2]).then_inc(s_xr, 16)

            def piece(e, s):
                if s < W1P:
                    return w1[e, s]
                return w2[e].rearrange("(q f p) n -> q p f n", q=W2P, p=P)[s - W1P]

            def dst(s):
                t = stage[s % STG]
                return t[:] if s < W1P else t[:].rearrange("p (f n) -> p f n", f=2)

            sp.wait_ge(s_kv, NB)
            for s in range(WP):
                if s == STG:
                    sp.wait_ge(s_meta, 1)
                    sp.dma_start(etab_next[:], table_t[:, 0:ET]).then_inc(s_etab, 16)
                if s >= STG:
                    sp.wait_ge(s_w_lo, s - STG + 1)
                sp.dma_start(dst(s), piece(0, s)).then_inc(s_wst[s % STG], 16)
            with sp.Fori(1, EX) as e:
                sp.wait_ge(s_etc, e)
                sp.dma_start(etab_next[:], table_t[:, bass.ds(e * ET, ET)]).then_inc(s_etab, 16)
                for s in range(WP):
                    sp.wait_ge(s_w_lo, e * WP + s - STG + 1)
                    if s < W1P:
                        src = w1[bass.ds(e, 1), s].rearrange("o p n -> (o p) n")
                    else:
                        src = w2[bass.ds(e, 1)].rearrange("o (q f p) n -> (o q) p f n",
                                                          q=W2P, p=P)[s - W1P]
                    sp.dma_start(dst(s), src).then_inc(s_wst[s % STG], 16)
            sp.wait_ge(s_etc, EX)
            sp.dma_start(etab_next[:], table_t[:, EX * ET:(EX + 1) * ET]).then_inc(s_etab, 16)
            tiles = sp.value_load(meta[0:1, 1, EX:EX + 1], min_val=0, max_val=EX * ET)
            wait_alone(sp, s_add, 16 * tiles)

        @block.gpsimd
        def _(pool):
            p = nc.gpsimd
            n = [0]

            def step(ins):
                n[0] += 1
                ins.then_inc(s_pself, 1)
                pool.wait_ge(s_pself, n[0])

            step(p.memset(tabinit[:], 0))
            step(p.iota(tabinit[:, :, 0], pattern=[[0, (EX + 1) * ET]], base=N, channel_multiplier=1))
            p.memset(zrow[:], 0.0).then_inc(s_const, 1)
            step(p.memset(ident[:], 0.0))
            step(p.affine_select(out=ident[:], in_=ident[:], compare_op=ALU.not_equal, fill=1.0, base=0,
                                 pattern=[[-1, P]], channel_multiplier=1))
            step(p.memset(onesb[:], 1.0))
            step(p.affine_select(out=tri[:], in_=onesb[:], compare_op=ALU.is_gt, fill=0.0, base=0,
                                 pattern=[[1, P]], channel_multiplier=-1))
            p.memset(ones[:], 1.0)
            p.memset(kv[:], 0.0)
            p.memset(wqk[:], 0.0)
            p.memset(wgp[:], 0.0)
            p.memset(half_neg[:], -0.5)
            p.memset(half_pos[:], 0.5)
            p.memset(minus1[:], -1.0)
            p.memset(carry[:], 0.0)
            p.memset(zero8[:], 0.0)
            p.memset(metaf[:], 0.0)
            p.iota(iota8i[:], pattern=[[1, EX]], base=0, channel_multiplier=0)
            p.iota(toki[:], pattern=[[P, TI], [0, TOPK]], base=0, channel_multiplier=1)
            p.iota(trashi[:], pattern=[[TOPK * P, TI], [P, TOPK]], base=TRASH,
                   channel_multiplier=1).then_inc(s_const, 1)
            pool.wait_ge(s_init, 48)

            with pool.Fori(0, NB) as b:
                n[0] = 0

                def link(ins):
                    n[0] += 1
                    ins.then_inc(s_pool, 1)
                    wait_alone(pool, s_pool, b * POOL_B + n[0])

                ns = [0]

                def inverse_std(q):
                    link(p.tensor_scalar(var_e[q][:], mv[q][:, :, 1], LN_EPS, None, ALU.add))
                    return p.tensor_tensor(rstd[q][:], var_e[q][:], half_neg[:], ALU.pow)

                def shift_of(q):
                    return p.tensor_tensor(shift[q][:], neg_mean[q][:], rstd[q][:], ALU.mult)

                def rsqrt_var():
                    ns[0] += 1
                    wait_alone(pool, s_stat, b * 2 * NG + ns[0])
                    inverse_std(0).then_inc(s_rstd, 1)

                def norm2():
                    ns[0] += 1
                    wait_alone(pool, s_stat, b * 2 * NG + ns[0])
                    p.tensor_scalar(neg_mean[0][:], mv[0][:, :, 0], -1.0, None, ALU.mult)
                    link(inverse_std(0))
                    shift_of(0).then_inc(s_rstd, 1)

                def norm3(g):
                    wait_alone(pool, s_stat2, b * NG + g + 1)
                    wait_alone(pool, s_xn3, (b * NG + g) * TI)
                    p.tensor_scalar(neg_mean[1][:], mv[1][:, :, 0], -1.0, None, ALU.mult)
                    link(inverse_std(1))
                    shift_of(1).then_inc(s_rstd2, 1)

                def k_sums(g):
                    for i in range(TI):
                        wait_alone(pool, s_fm, b * NG * 2 * TI + g * 2 * TI + i + 1)
                        if g == 0 and i == 0:
                            ins = p.tensor_copy(k_sum[:], kf[i % 2][:])
                        else:
                            wait_alone(pool, s_ks, b * NG * TI + g * TI + i)
                            ins = p.tensor_tensor(k_sum[:], k_sum[:], kf[i % 2][:], ALU.add)
                        ins.then_inc(s_ks, 1)

                def sigma(g):
                    wait_alone(pool, s_s2, b * NG + g + 1)
                    link(p.tensor_scalar(sig[:, :, 0], mv2[:, :, 1], CK / (CK - 1.0), None, ALU.mult))
                    link(p.tensor_tensor(sig[:, :, 1], sig[:, :, 0], half_pos[:], ALU.pow))
                    link(p.tensor_scalar(sig[:, :, 2], sig[:, :, 1], SIG_EPS, None, ALU.add))
                    p.tensor_tensor(sig[:, :, 3], sig[:, :, 2], minus1[:], ALU.pow).then_inc(s_sig, 1)

                def scatter(g):
                    wait_alone(pool, s_dest, b * NG + g + 1)
                    for c in range(TI * TOPK):
                        p.indirect_dma_start(
                            out=table, out_offset=bass.IndirectOffsetOnAxis(ap=dest[:, c:c + 1], axis=0),
                            in_=pack[:, c, :], in_offset=None).then_inc(s_scat, 16)

                rsqrt_var()
                for g in range(NG):
                    k_sums(g)
                    if g + 1 < NG:
                        rsqrt_var()
                for g in range(NG + 2):
                    if g < NG:
                        norm2()
                    if 1 <= g <= NG:
                        norm3(g - 1)
                    if g < NG:
                        sigma(g)
                    if g >= 2:
                        scatter(g - 2)
                assert n[0] == POOL_B, n[0]

            def gather(src_tab, t0, tiles):
                for i in range(tiles):
                    p.indirect_dma_start(
                        out=xg[:, i, :], out_offset=None, in_=x3d,
                        in_offset=bass.IndirectOffsetOnAxis(ap=src_tab[:, t0 + i, 0:1], axis=0)
                    ).then_inc(s_xg, 16)

            pool.wait_ge(s_meta, 1)
            pool.wait_ge(s_etab, 16)
            gather(etab_next, 0, CHUNKS[0])
            with pool.Fori(0, EX) as e:
                count = pool.value_load(meta[0:1, 0, bass.ds(e, 1)], min_val=0, max_val=CAP)
                tb = pool.value_load(meta[0:1, 1, bass.ds(e, 1)], min_val=0, max_val=EX * ET)
                wait_alone(pool, s_add, 16 * tb)
                wait_alone(pool, s_xg, 16 * tb + 16 * CHUNKS[0])
                p.tensor_copy(etab[:], etab_next[:]).then_inc(s_etc, 1)
                wait_alone(pool, s_etc, e + 1)

                def ahead(c, tiles, from_next):
                    wait_alone(pool, s_xet, tb + 4 * c + CHUNKS[c])
                    if from_next:
                        wait_alone(pool, s_etab, 16 * (e + 2))
                        gather(etab_next, 0, tiles)
                    else:
                        gather(etab, 4 * (c + 1), tiles)

                def add_rows(c):
                    for i in range(CHUNKS[c]):
                        t = 4 * c + i
                        wait_alone(pool, s_yev, tb + t + 1)
                        wait_alone(pool, s_add, 16 * (tb + t))
                        p.indirect_dma_start(
                            out=out, out_offset=bass.IndirectOffsetOnAxis(ap=etab[:, t, 0:1], axis=0),
                            in_=ost[i % 2][:], in_offset=None, compute_op=ALU.add).then_inc(s_add, 16)

                with pool.If(count > 4 * P):
                    ahead(0, CHUNKS[1], False)
                    add_rows(0)
                    with pool.If(count > 8 * P):
                        ahead(1, CHUNKS[2], False)
                        add_rows(1)
                        ahead(2, CHUNKS[0], True)
                        add_rows(2)
                    with pool.Else():
                        ahead(1, CHUNKS[0], True)
                        add_rows(1)
                with pool.Else():
                    ahead(0, CHUNKS[0], True)
                    add_rows(0)

        @block.scalar
        def _(act):
            a = nc.scalar
            act.wait_ge(s_setup_in, 16 * SETUP_LOADS)
            a.activation(wk_hi[:], wk_raw[:], ACT.Copy).then_inc(s_whi, 1)
            a.activation(wq_hi[:], wq_raw[:], ACT.Copy).then_inc(s_whi, 1)
            act.wait_ge(s_const, 2)
            a.activation(ones_r[:], ones[0:1, :], ACT.Copy)
            a.activation(bk_hi[:], bk_row[:], ACT.Copy).then_inc(s_whi, 1)
            for b in range(NB):
                act.wait_ge(s_xset, 3 + b)
                a.activation(vp[:, b * D:(b + 1) * D], pg[0:CK, b, :], ACT.Copy).then_inc(s_vpev, 1)

            with act.Fori(0, NB) as b:
                JG = 2 * TI

                def turned_hi(g):
                    for k in range(KC):
                        act.wait_ge(s_t, b * NG * KC + g * KC + k + 1)
                        a.activation(xT_hi[:, k, :], pt[k % 2][:], ACT.Copy).then_inc(s_thi, 1)

                def job(g, j):
                    n = b * NG * JG + g * JG + j
                    act.wait_ge(s_proj, n + 1)
                    if g or j >= 2:
                        act.wait_ge(s_fm, n - 1)
                    bias = 0.0 if j < TI else bq_c[:, j - TI:j - TI + 1]
                    a.activation(fe[j % 2][:], pj[j % 2][:], ACT.Exp, bias=bias)
                    a.activation(frl[j % 2][:], pj[j % 2][:], ACT.Relu, bias=bias).then_inc(s_feat, 1)

                def khi(g, i):
                    act.wait_ge(s_fm, b * NG * JG + g * JG + i + 1)
                    a.activation(k_hi[:, i, :], kf[i % 2][:], ACT.Copy).then_inc(s_khi, 1)

                for g in range(NG):
                    turned_hi(g)
                    act.wait_ge(s_xn, b * NG + g + 1)
                    if g:
                        act.wait_ge(s_g, b * NG + g)
                    a.activation(xn_hi[:], xn[:], ACT.Copy).then_inc(s_xnhi, 1)
                    for j in range(JG):
                        job(g, j)
                        if 1 <= j <= TI:
                            khi(g, j - 1)
                act.wait_ge(s_g, (b + 1) * NG)
                for c in range(2):
                    a.activation(gT[:, c, :], pg[:, c, :], ACT.Copy)
                act.wait_ge(s_krow, b + 1)
                a.activation(ksum_row[:], pj[0][0:1, :], ACT.Copy).then_inc(s_krev, 1)

                nt = [0]
                BT = (2 * TI + 1) * NG

                def turned(dst):
                    bank = pt[nt[0] % 2]
                    nt[0] += 1
                    act.wait_ge(s_bt, b * BT + nt[0])
                    a.activation(dst, bank[0:dst.shape[0]].rearrange("p (k t) -> p k t", t=P) if len(dst.shape) == 3
                                 else bank[0:dst.shape[0], :], ACT.Copy).then_inc(s_btev, 1)

                def normalise(dst, src, q, done, dstT):
                    for i in range(TI + 1):
                        if i < TI:
                            a.activation(dst[:, i, :], src[:, i, :], ACT.Identity, bias=shift[q][:, i:i + 1],
                                         scale=rstd[q][:, i:i + 1]).then_inc(done, 1)
                        if i >= 1:
                            turned(dstT[:, :, (i - 1) * P:i * P])

                for g in range(NG + 2):
                    if g < NG:
                        act.wait_ge(s_rstd, b * 2 * NG + NG + g + 1)
                        normalise(xn2, xr[g % 2], 0, s_xn2, xT2)
                    if 1 <= g <= NG:
                        act.wait_ge(s_rstd2, b * NG + g)
                        act.wait_ge(s_st, 32 * (b * NG + g - 1))
                        normalise(xn3, xr[(g - 1) % 2], 1, s_xn3, xT3)
                    if g >= 2:
                        act.wait_ge(s_gd, b * NG + g - 1)
                        a.activation(ge[:], gd[:], ACT.Exp).then_inc(s_ge, 1)
                    if g < NG:
                        act.wait_ge(s_ex, b * NG + g + 1)
                        a.activation(sc[:], sc[:], ACT.Exp).then_inc(s_e, 1)
                        turned(sT[:])
                assert nt[0] == BT

            act.wait_ge(s_meta, 1)

            def w_dst(s):
                return (w1_hi[:, s].rearrange("p k n -> p (k n)") if s < W1P else
                        w2_hi[:, 2 * (s - W1P):2 * (s - W1P) + 2].rearrange("p f n -> p (f n)"))

            def split(e, s, final=None):
                act.wait_ge(s_wst[s % STG], e * (16 * WP // STG) + 16 * (s // STG + 1))
                if final is not None:
                    act.wait_ge(s_h, final * FJ + s + 1)
                a.activation(w_dst(s), stage[s % STG][:], ACT.Copy).then_inc(s_w_hi, 1)

            def evac_x(first, tiles):
                for i in tiles:
                    act.wait_ge(s_xet, first + i + 1)
                    a.activation(xe_hi[:, :, i * P:(i + 1) * P],
                                 pt[i % 2][:].rearrange("p (k t) -> p k t", k=KC), ACT.Copy).then_inc(s_xehi, 1)

            evac_x(0, range(CHUNKS[0]))
            for s in range(W1P):
                split(0, s)
            with act.Fori(0, EX) as e:
                count = act.value_load(meta[0:1, 0, bass.ds(e, 1)], min_val=0, max_val=CAP)
                tb = act.value_load(meta[0:1, 1, bass.ds(e, 1)], min_val=0, max_val=EX * ET)
                ib = act.value_load(meta[0:1, 2, bass.ds(e, 1)], min_val=0, max_val=EX * 3)

                def jobs(c):
                    w = CHUNKS[c] * P
                    act.wait_ge(s_y, tb + 4 * c)
                    for j in range(FJ + 1):
                        if j < FJ:
                            act.wait_ge(s_h, (ib + c) * FJ + j + 1)
                            if j >= 2:
                                act.wait_ge(s_hp, (ib + c) * FJ + j - 1)
                            a.activation(gl[j % 2][:, 0:w], pg[:, j % 2, 0:w], ACT.Gelu).then_inc(s_gl, 1)
                        if j >= 1:
                            act.wait_ge(s_hp, (ib + c) * FJ + j)
                            a.activation(hg_hi[:, j - 1, 0:w], hp[(j - 1) % 2][:, 0:w],
                                         ACT.Copy).then_inc(s_hghi, 1)
                        if c == 0 and 2 <= j < 2 + W2P:
                            split(e, W1P + j - 2)

                def outs(c, last, ahead):
                    per = W1P // CHUNKS[c]
                    following = tb + 4 * c + CHUNKS[c]
                    for i in range(CHUNKS[c]):
                        t = 4 * c + i
                        if i == 0:
                            evac_x(following, range(2))
                        if i == 1:
                            evac_x(following, range(2, ahead))
                        if last:
                            with act.If(e < EX - 1):
                                for s in range(i * per, (i + 1) * per):
                                    split(e + 1, s, ib + c)
                        act.wait_ge(s_y, tb + t + 1)
                        act.wait_ge(s_etc, e + 1)
                        if c or i >= 2:
                            act.wait_ge(s_add, 16 * (tb + t - 1))
                        a.activation(ost[i % 2][:], pj[i % 2][:], ACT.Copy,
                                     scale=etab[:, t, 1:2].bitcast(F32)).then_inc(s_yev, 1)

                jobs(0)
                with act.If(count > 4 * P):
                    outs(0, False, CHUNKS[1])
                    jobs(1)
                    with act.If(count > 8 * P):
                        outs(1, False, CHUNKS[2])
                        jobs(2)
                        outs(2, True, CHUNKS[0])
                    with act.Else():
                        outs(1, True, CHUNKS[0])
                with act.Else():
                    outs(0, True, CHUNKS[0])

        @block.tensor
        def _(pe):
            def three(o, lh, ll, rh, rl, start, stop):
                nc.tensor.matmul(o, lh, rh, start=start, stop=False)
                nc.tensor.matmul(o, lh, rl, start=False, stop=False)
                return nc.tensor.matmul(o, ll, rh, start=False, stop=stop)

            mm = nc.tensor.matmul
            pe.wait_ge(s_setup_in, 16 * SETUP_LOADS)
            pe.wait_ge(s_const, 2)
            for k in range(KC):
                mm(pj[0][0:XH, 0:NB * CK], xwk_sb[:, k, :], ctx_sb[:, k, :], start=k == 0, stop=k == KC - 1)
            for k in range(KC):
                ins = mm(pj[1][:, 0:NB * CK], xwv_sb[:, k, :], ctx_sb[:, k, :], start=k == 0, stop=k == KC - 1)
            ins.then_inc(s_xset, 1)
            pe.wait_ge(s_xev, 1)
            for m in range(KC):
                mm(pt[m // 3][:, m % 3 * NB * CK:(m % 3 + 1) * NB * CK], xwqT_sb[:, m * P:(m + 1) * P], kT[:],
                   start=True, stop=True)
            mm(pt[1][:, NB * CK:2 * NB * CK], bq_b[:], kT[:], start=True, stop=True).then_inc(s_xset, 1)
            for b in range(NB):
                for r in range(KC):
                    mm(pg[0:CK, b, :], vT[:, b * CK:(b + 1) * CK], wout_sb[:, r, :], start=r == 0, stop=False)
                mm(pg[0:CK, b, :], ones[0:1, 0:CK], bout_sb[:], start=False, stop=True).then_inc(s_xset, 1)
            pe.wait_ge(s_xev, 3)
            pe.wait_ge(s_vpev, NB)
            pe.wait_ge(s_wlo, 3)
            pe.wait_ge(s_whi, 3)

            with pe.Fori(0, NB) as b:
                JG = 2 * TI

                def turn(g):
                    pe.wait_ge(s_xn, b * NG + g + 1)
                    for k in range(KC):
                        if g or k >= 2:
                            pe.wait_ge(s_tlo, b * NG * KC + g * KC + k - 1)
                        for i in range(TI):
                            ins = nc.tensor.transpose(pt[k % 2][:, i * P:(i + 1) * P],
                                                      xn[:, i, k * P:(k + 1) * P], ident[:])
                        ins.then_inc(s_t, 1)

                def project(g):
                    for j in range(JG):
                        n = b * NG * JG + g * JG + j
                        if j == 0:
                            pe.wait_ge(s_tlo, b * NG * KC + (g + 1) * KC)
                        if g or j >= 2:
                            pe.wait_ge(s_feat, n - 1)
                        o = pj[j % 2][:]
                        if j < TI:
                            tk = slice(j * P, (j + 1) * P)
                            mm(o, ones_r[:], bk_hi[:], start=True, stop=False)
                            mm(o, ones_r[:], bk_lo[:], start=False, stop=False)
                            for k in range(KC):
                                ins = three(o, xT_hi[:, k, tk], xT_lo[:, k, tk], wk_hi[:, k, :], wk_lo[:, k, :],
                                            False, k == KC - 1)
                        else:
                            m = slice((j - TI) * P, (j - TI + 1) * P)
                            for k in range(KC):
                                ins = three(o, wq_hi[:, k, m], wq_lo[:, k, m], xT_hi[:, k, :], xT_lo[:, k, :],
                                            k == 0, k == KC - 1)
                        ins.then_inc(s_proj, 1)

                def gram(g):
                    pe.wait_ge(s_xnlo, b * NG + g + 1)
                    for i in range(TI):
                        pe.wait_ge(s_klo, b * NG * TI + g * TI + i + 1)
                        for c in range(KC):
                            m = slice(c * P, (c + 1) * P)
                            ins = three(pg[:, c, :], xn_hi[:, i, m], xn_lo[:, i, m], k_hi[:, i, :], k_lo[:, i, :],
                                        g == 0 and i == 0, g == NG - 1 and i == TI - 1)
                    ins.then_inc(s_g, 1)

                turn(0)
                for g in range(NG):
                    project(g)
                    if g + 1 < NG:
                        turn(g + 1)
                    gram(g)

                pe.wait_ge(s_ks, (b + 1) * NG * TI)
                pe.wait_ge(s_feat, (b + 1) * NG * JG)
                mm(pj[0][0:1, :], ones[:, 0:1], k_sum[:], start=True, stop=True).then_inc(s_krow, 1)
                pe.wait_ge(s_krev, b + 1)
                for m in range(KC):
                    mm(pj[1][:, m:m + 1], ksum_row[0:1, m * P:(m + 1) * P], ones[0:1, 0:1], start=True, stop=True)
                pe.wait_ge(s_gev, b + 1)
                for m in range(KC):
                    cols = slice(m * P, (m + 1) * P)
                    for c in range(KC):
                        mm(pt[0][:, cols], gT[:, c, cols], wv_sb[:, c, cols], start=c == 0, stop=False)
                    ins = mm(pt[0][:, cols], ksum_row[0:1, cols], bv_row[0:1, cols], start=False, stop=True)
                ins.then_inc(s_kv, 1)

                def attend(g, tiles):
                    if g >= 2 and tiles[0] == 0:
                        pe.wait_ge(s_x2t, (b * NG + g - 1) * TI)
                    for i in tiles:
                        n = b * NG * TI + g * TI + i
                        if g or i >= 2:
                            pe.wait_ge(s_oev, n - 1)
                        for q in range(PAIRS):
                            ins = mm(pg[:, 2 * (i % 2) + q // 2, (q % 2) * PW:(q % 2 + 1) * PW],
                                     qT[:, q, g * GT + i * P:g * GT + (i + 1) * P], kv[:, q, :], start=True, stop=True)
                        ins.then_inc(s_o, 1)

                nt = [0]
                BT = (2 * TI + 1) * NG

                def bank():
                    if nt[0] >= 2:
                        pe.wait_ge(s_btev, b * BT + nt[0] - 1)
                    nt[0] += 1
                    return pt[(nt[0] - 1) % 2]

                def turn_and_multiply(src, done, turned, g, out, w, ready):
                    for i in range(TI + 1):
                        if i < TI:
                            pe.wait_ge(done, (b * NG + g) * TI + i + 1)
                            to = bank()
                            for k in range(KC):
                                ins = nc.tensor.transpose(to[:, k * P:(k + 1) * P], src[:, i, k * P:(k + 1) * P],
                                                          ident[:])
                            ins.then_inc(s_bt, 1)
                        if i >= 1:
                            pe.wait_ge(s_btev, b * BT + nt[0] - (1 if i < TI else 0))
                            for k in range(KC):
                                ins = mm(out[:, (i - 1) * PADW:i * PADW], turned[:, k, (i - 1) * P:i * P], w(k),
                                         start=k == 0, stop=k == KC - 1)
                    ins.then_inc(ready, 1)

                def scores(g):
                    if g:
                        pe.wait_ge(s_sev, b * NG + g)
                    if g >= 3:
                        pe.wait_ge(s_posev, b * NG + g - 2)
                    turn_and_multiply(xn2, s_xn2, xT2, g, pj[0],
                                      lambda k: wqk[:, k, bass.ds(b * PADW, PADW)], s_s)

                def logits(g):
                    if g:
                        pe.wait_ge(s_lgev, b * NG + g)
                    turn_and_multiply(xn3, s_xn3, xT3, g, pj[1], lambda k: wgp[:, k, :], s_lgp)

                def turn_exp(g):
                    pe.wait_ge(s_e, b * NG + g + 1)
                    to = bank()
                    for i in range(TI):
                        ins = nc.tensor.transpose(to[0:CK, i * P:(i + 1) * P], sc[:, i, :], ident[:])
                    ins.then_inc(s_bt, 1)

                def values(g):
                    pe.wait_ge(s_btev, b * BT + nt[0])
                    pe.wait_ge(s_oev, (b * NG + min(g + 2, NG)) * TI)
                    for i in range(TI):
                        mm(pg[:, i, :], sT[:, i * P:(i + 1) * P], vp[:, bass.ds(b * D, D)],
                           start=True, stop=True).then_inc(s_x2p, 1)

                def positions(g):
                    pe.wait_ge(s_hot, b * NG + g + 1)
                    if g:
                        pe.wait_ge(s_posev, b * NG + g)
                    pe.wait_ge(s_sev, b * NG + min(g + 3, NG))
                    for i in range(TI):
                        for q in range(i + 1):
                            mm(pj[0][:, POS + i * EX:POS + (i + 1) * EX], (tri if q == i else onesb)[:], hot[:, q, :],
                               start=q == 0, stop=q == i)
                    for q in range(TI):
                        ins = mm(pj[0][:, POS + TI * EX:POS + (TI + 1) * EX], onesb[:], hot[:, q, :],
                                 start=q == 0, stop=q == TI - 1)
                    ins.then_inc(s_pos, 1)

                pe.wait_ge(s_kvev, b + 1)
                attend(0, range(TI))
                for g in range(NG + 2):
                    if 1 <= g <= NG:
                        values(g - 1)
                    if g < NG:
                        scores(g)
                    if 1 <= g <= NG:
                        logits(g - 1)
                    if g >= 2:
                        positions(g - 2)
                    if g + 1 < NG:
                        attend(g + 1, range(2))
                    if g < NG:
                        turn_exp(g)
                    if g + 1 < NG:
                        attend(g + 1, range(2, TI))
                assert nt[0] == BT

            pe.wait_ge(s_meta, 1)

            def turn_rows(first, tiles, total):
                pe.wait_ge(s_xg, 16 * (first + total))
                for i in tiles:
                    if i >= 2:
                        pe.wait_ge(s_xelo, first + i - 1)
                    for k in range(KC):
                        ins = nc.tensor.transpose(pt[i % 2][:, k * P:(k + 1) * P], xg[:, i, k * P:(k + 1) * P], ident[:])
                    ins.then_inc(s_xet, 1)

            turn_rows(0, range(CHUNKS[0]), CHUNKS[0])
            with pe.Fori(0, EX) as e:
                count = pe.value_load(meta[0:1, 0, bass.ds(e, 1)], min_val=0, max_val=CAP)
                tb = pe.value_load(meta[0:1, 1, bass.ds(e, 1)], min_val=0, max_val=EX * ET)
                ib = pe.value_load(meta[0:1, 2, bass.ds(e, 1)], min_val=0, max_val=EX * 3)

                def up(c, tiles):
                    w = tiles * P
                    pe.wait_ge(s_xelo, tb + 4 * c + CHUNKS[c])
                    for j in range(FJ):
                        if c == 0:
                            pe.wait_ge(s_w_lo, e * WP + j + 1)
                        if j >= 2:
                            pe.wait_ge(s_hp, (ib + c) * FJ + j - 1)
                        for half in range(2):
                            m = slice(half * P, (half + 1) * P)
                            for k in range(KC):
                                ins = three(pg[:, 2 * half + j % 2, 0:w], w1_hi[:, j, k, m], w1_lo[:, j, k, m],
                                            xe_hi[:, k, 0:w], xe_lo[:, k, 0:w], k == 0, k == KC - 1)
                        ins.then_inc(s_h, 1)

                def down(c, tiles, ahead):
                    following = tb + 4 * c + CHUNKS[c]
                    turn_rows(following, range(2), ahead)
                    if c == 0:
                        pe.wait_ge(s_w_lo, (e + 1) * WP)
                    for i in range(CHUNKS[c]):
                        m = slice(i * P, (i + 1) * P)
                        pe.wait_ge(s_yev, tb + 4 * c + max(i - 1, 0))
                        if i < tiles:
                            for j in range(FJ):
                                if i == 0:
                                    pe.wait_ge(s_hglo, (ib + c) * FJ + j + 1)
                                ins = three(pj[i % 2][:], hg_hi[:, j, m], hg_lo[:, j, m], w2_hi[:, j, :],
                                            w2_lo[:, j, :], j == 0, j == FJ - 1)
                        else:
                            ins = mm(pj[i % 2][:], w1_hi[:, 0, 0, 0:P], w2_hi[:, 0, :], start=True, stop=True)
                        ins.then_inc(s_y, 1)
                        if i == 0 and ahead > 2:
                            turn_rows(following, range(2, ahead), ahead)

                def chunk(c, tiles, ahead):
                    up(c, tiles)
                    down(c, tiles, ahead)

                def last_chunk(c):
                    with pe.If(count > (4 * c + 3) * P):
                        chunk(c, 4, CHUNKS[0])
                    with pe.Else():
                        with pe.If(count > (4 * c + 2) * P):
                            chunk(c, 3, CHUNKS[0])
                        with pe.Else():
                            chunk(c, 2, CHUNKS[0])

                with pe.If(count > 4 * P):
                    chunk(0, 4, CHUNKS[1])
                    with pe.If(count > 8 * P):
                        chunk(1, 4, CHUNKS[2])
                        chunk(2, 2, CHUNKS[0])
                    with pe.Else():
                        last_chunk(1)
                with pe.Else():
                    last_chunk(0)

        @block.vector
        def _(dve):
            v = nc.vector
            n = [0]

            def step(ins):
                n[0] += 1
                ins.then_inc(s_dself, 1)
                dve.wait_ge(s_dself, n[0])

            def low(dst, src, hi):
                return v.tensor_tensor(dst, src, hi.bitcast(F32), ALU.subtract)

            dve.wait_ge(s_whi, 1)
            low(wk_lo[:], wk_raw[:], wk_hi[:]).then_inc(s_wlo, 1)
            dve.wait_ge(s_whi, 2)
            low(wq_lo[:], wq_raw[:], wq_hi[:]).then_inc(s_wlo, 1)
            dve.wait_ge(s_setup_in, 16 * SETUP_LOADS)
            v.tensor_copy(bq_b[:], xbq_sb[:].broadcast_to([XH, P]))
            dve.wait_ge(s_xset, 1)
            v.tensor_scalar(kT[:], pj[0][0:XH, 0:NB * CK], xbk_sb[:], float(D) ** -0.5, ALU.add, ALU.mult)
            v.tensor_scalar(vT[:], pj[1][:, 0:NB * CK], xbv_sb[:], None, ALU.add).then_inc(s_xev, 1)
            dve.wait_ge(s_whi, 3)
            low(bk_lo[:], bk_row[:], bk_hi[:]).then_inc(s_wlo, 1)
            dve.wait_ge(s_const, 2)
            dve.wait_ge(s_xset, 2)
            for m in range(KC):
                v.tensor_copy(wqk[:, m, :].rearrange("p (b c) -> p b c", b=NB)[:, :, 0:CK],
                              pt[m // 3][:, m % 3 * NB * CK:(m % 3 + 1) * NB * CK]
                              .rearrange("p (b c) -> p b c", b=NB))
            v.tensor_copy(sbias[:], pt[1][:, NB * CK:2 * NB * CK].rearrange("p (b c) -> p b c", b=NB)
                          ).then_inc(s_xev, 1)
            v.tensor_scalar(maskf[:].rearrange("p b c -> p (b c)"), mask_sb[:], -1e-32, None, ALU.mult)
            v.tensor_copy(iota8[:], iota8i[:])
            v.tensor_copy(tok[:], toki[:])
            v.tensor_copy(trash[:], trashi[:])
            v.tensor_copy(wgp[:, :, 0:EX], wg_sb[:]).then_inc(s_xev, 1)
            dve.wait_ge(s_xev, 3)

            with dve.Fori(0, NB) as b:
                n[0] = 0
                ns = [0]
                JG = 2 * TI

                def link(ins, alone=False):
                    n[0] += 1
                    ins.then_inc(s_dve, 1)
                    (wait_alone if alone else wait)(dve, s_dve, b * DVE_B + n[0])

                def aggregate(q=0):
                    for i in range(TI):
                        ins = v.bn_aggr(mv[q][:, i, :], st[q][:, i, :])
                    ins.then_inc(s_stat2 if q else s_stat, 1)

                def normalise(g):
                    dve.wait_ge(s_rstd, b * 2 * NG + g + 1)
                    for i in range(TI):
                        ins = v.tensor_scalar(xn[:, i, :], x_in[:, i, :], mv[0][:, i, 0:1], rstd[0][:, i:i + 1],
                                              ALU.subtract, ALU.mult)
                    ins.then_inc(s_xn, 1)

                def stats_in(g, tiles):
                    if tiles[0] == 0:
                        dve.wait_ge(s_xin, 16 * (b * NG + g + 1))
                    for i in tiles:
                        ins = v.bn_stats(st[0][:, i, :], x_in[:, i, :])
                    return ins

                def turned_lo(g):
                    for k in range(KC):
                        dve.wait_ge(s_thi, b * NG * KC + g * KC + k + 1)
                        low(xT_lo[:, k, :], pt[k % 2][:], xT_hi[:, k, :]).then_inc(s_tlo, 1)

                def job(g, j):
                    m = b * NG * JG + g * JG + j
                    dve.wait_ge(s_feat, m + 1)
                    if j < TI:
                        if g or j >= 2:
                            dve.wait_ge(s_ks, b * NG * TI + g * TI + j - 1)
                            dve.wait_ge(s_klo, b * NG * TI + g * TI + j - 1)
                        dst = kf[j % 2][:]
                    else:
                        dst = qT[:, j - TI, g * GT:(g + 1) * GT]
                    v.scalar_tensor_tensor(dst, fe[j % 2][:], 1.0, frl[j % 2][:], ALU.min, ALU.add
                                           ).then_inc(s_fm, 1)

                link(stats_in(0, range(TI)), True)
                aggregate()
                normalise(0)
                for g in range(NG):
                    turned_lo(g)
                    dve.wait_ge(s_xnhi, b * NG + g + 1)
                    low(xn_lo[:], xn[:], xn_hi[:]).then_inc(s_xnlo, 1)
                    for j in range(JG):
                        job(g, j)
                        if 1 <= j <= TI:
                            dve.wait_ge(s_khi, b * NG * TI + g * TI + j)
                            dve.wait_ge(s_fm, b * NG * JG + g * JG + j)
                            low(k_lo[:, j - 1, :], kf[(j - 1) % 2][:], k_hi[:, j - 1, :]).then_inc(s_klo, 1)
                        if g + 1 < NG:
                            if j == 0:
                                stats_in(g + 1, range(2))
                            if j == 1:
                                link(stats_in(g + 1, range(2, TI)))
                            if j == 2:
                                aggregate()
                            if j == 5:
                                normalise(g + 1)

                dve.wait_ge(s_g, (b + 1) * NG)
                for c in range(2, KC):
                    ins = v.tensor_copy(gT[:, c, :], pg[:, c, :])
                ins.then_inc(s_gev, 1)
                dve.wait_ge(s_kv, b + 1)
                kvp = pt[0][:].rearrange("p (q c) -> p q c", q=PAIRS)
                v.tensor_copy(kv[0:HD, :, 0:HD], kvp[0:HD, :, 0:HD])
                v.tensor_copy(kv[HD:P, :, HW:HW + HD], kvp[HD:P, :, HD:P])
                v.tensor_copy(kv[0:HD, :, HD], pj[1][0:HD, 0:PAIRS])
                v.tensor_copy(kv[HD:P, :, HW + HD], pj[1][HD:P, 0:PAIRS]).then_inc(s_kvev, 1)

                def attention_out(g):
                    x1 = xr[g % 2]
                    dve.wait_ge(s_xr, 16 * (b * NG + g + 1))
                    for pair in range(TI // 2):
                        for q in range(2):
                            dve.wait_ge(s_o, b * NG * TI + g * TI + 2 * pair + q + 1)
                            ins = v.tensor_scalar(den[:, q], pg[:, 2 * q:2 * q + 2, HD:HD + 3 * HW + 1:HW],
                                                  Z_EPS, None, ALU.add)
                        link(ins)
                        for q in range(2):
                            ins = v.reciprocal(zz[:, q], den[:, q])
                        link(ins)
                        for q in range(2):
                            v.tensor_tensor(
                                fe[q][:].rearrange("p (a h c) -> p a h c", a=2, h=4),
                                pg[:, 2 * q:2 * q + 2, 0:4 * HW].rearrange("p a (h w) -> p a h w", w=HW)[:, :, :, 0:HD],
                                zz[:, q].unsqueeze(3).broadcast_to([P, 2, 4, HD]), ALU.mult).then_inc(s_oev, 1)
                        dve.wait_ge(s_oev, b * NG * TI + g * TI + 2 * pair + 2)
                        for q in range(2):
                            i = 2 * pair + q
                            ins = v.tensor_tensor(x1[:, i, :], x1[:, i, :], fe[q][:], ALU.add)
                        link(ins)
                        for q in range(2):
                            ins = v.bn_stats(st[0][:, 2 * pair + q, :], x1[:, 2 * pair + q, :])
                    link(ins, True)
                    aggregate()

                def score_stats(g):
                    dve.wait_ge(s_s, b * NG + g + 1)
                    v.tensor_tensor(sc[:], pj[0][:, 0:POS].rearrange("p (i c) -> p i c", c=PADW)[:, :, 0:CK],
                                    sbias[:, bass.ds(b, 1), :].broadcast_to([P, TI, CK]), ALU.add).then_inc(s_sev, 1)
                    dve.wait_ge(s_sev, b * NG + g + 1)
                    for i in range(TI):
                        ins = v.bn_stats(st2[:, i, :], sc[:, i, :])
                    link(ins, True)
                    for i in range(TI):
                        ins = v.bn_aggr(mv2[:, i, :], st2[:, i, :])
                    ins.then_inc(s_s2, 1)

                def softmax(g):
                    dve.wait_ge(s_sig, b * NG + g + 1)
                    for i in range(TI):
                        ins = v.tensor_scalar(sc[:, i, :], sc[:, i, :], mv2[:, i, 0:1], sig[:, i, 3:4],
                                              ALU.subtract, ALU.mult)
                    link(ins)
                    link(v.tensor_tensor(sc[:], sc[:], maskf[:, bass.ds(b, 1), :].broadcast_to([P, TI, CK]), ALU.add))
                    link(v.tensor_reduce(smax[:], sc[:], AX.X, ALU.max))
                    v.tensor_tensor(sc[:], sc[:], smax[:].unsqueeze(2).broadcast_to([P, TI, CK]),
                                    ALU.subtract).then_inc(s_ex, 1)

                def cross_out(g):
                    x2 = xr[g % 2]
                    for i in range(TI + 1):
                        m = b * NG * TI + g * TI + i
                        if i < TI:
                            dve.wait_ge(s_x2p, m + 1)
                            v.scalar_tensor_tensor(x2[:, i, :], pg[:, i, :], sinv[:, i:i + 1], x2[:, i, :],
                                                   ALU.mult, ALU.add).then_inc(s_x2t, 1)
                        if i >= 1:
                            dve.wait_ge(s_x2t, m)
                            ins = v.bn_stats(st[1][:, i - 1, :], x2[:, i - 1, :])
                    link(ins, True)
                    aggregate(1)

                def sums(g):
                    dve.wait_ge(s_e, b * NG + g + 1)
                    link(v.tensor_reduce(ssum[:], sc[:], AX.X, ALU.add))
                    link(v.reciprocal(sinv[:], ssum[:]))

                def route(g):
                    dve.wait_ge(s_lgp, b * NG + g + 1)
                    v.tensor_copy(lg[:], pj[1][:, 0:TI * PADW].rearrange("p (i c) -> p i c", c=PADW)[:, :, 0:EX]
                                  ).then_inc(s_lgev, 1)
                    wait_alone(dve, s_lgev, b * NG + g + 1)
                    for i in range(TI):
                        ins = v.max(top[:, i, :], lg[:, i, :])
                    link(ins, True)
                    for i in range(TI):
                        ins = v.max_index(topi[:, i, :], top[:, i, :], lg[:, i, :])
                    v.tensor_tensor(gd[:], top[:, :, 1], top[:, :, 0], ALU.subtract).then_inc(s_gd, 1)
                    dve.wait_ge(s_gd, b * NG + g + 1)
                    link(v.tensor_copy(ef[:], topi[:, :, 0:TOPK]))
                    link(v.tensor_tensor(oh[:].rearrange("p i k e -> p (i k) e"),
                                         ef[:].rearrange("p i k -> p (i k)").unsqueeze(2).broadcast_to([P, TI * TOPK, EX]),
                                         iota8[:].unsqueeze(1).broadcast_to([P, TI * TOPK, EX]), ALU.is_equal))
                    v.tensor_tensor(hot[:], oh[:, :, 0, :], oh[:, :, 1, :], ALU.add).then_inc(s_hot, 1)

                def gates(g):
                    dve.wait_ge(s_ge, b * NG + g + 1)
                    link(v.tensor_scalar(gs[:], ge[:], 1.0, None, ALU.add))
                    link(v.reciprocal(gate[:, :, 0], gs[:]))
                    link(v.tensor_tensor(gate[:, :, 1], ge[:], gate[:, :, 0], ALU.mult))

                def place_tokens(g):
                    dve.wait_ge(s_pos, b * NG + g + 1)
                    link(v.tensor_tensor(pos[:], pj[0][:, POS:POS + TI * EX].rearrange("p (i e) -> p i e", e=EX),
                                         carry[:].unsqueeze(1).broadcast_to([P, TI, EX]), ALU.add))
                    v.tensor_tensor(carry[:], pj[0][:, POS + TI * EX:POS + (TI + 1) * EX], carry[:], ALU.add).then_inc(s_posev, 1)
                    link(v.tensor_tensor(ohp[:], oh[:], pos[:].unsqueeze(2).broadcast_to([P, TI, TOPK, EX]), ALU.mult))
                    link(v.tensor_reduce(pe_[:], ohp[:], AX.X, ALU.add))
                    v.scalar_tensor_tensor(slot[:], ef[:], float(CAP), pe_[:], ALU.mult, ALU.add)
                    link(v.tensor_scalar(kept[:], pe_[:], float(CAP), None, ALU.is_lt))
                    link(v.tensor_tensor(slot[:], slot[:], trash[:], ALU.subtract))
                    link(v.tensor_tensor(slot[:], slot[:], kept[:], ALU.mult))
                    dve.wait_ge(s_scat, 16 * TI * TOPK * (b * NG + g))
                    v.tensor_tensor(dest[:], slot[:].rearrange("p i k -> p (i k)"),
                                    trash[:].rearrange("p i k -> p (i k)"), ALU.add)
                    v.tensor_copy(pack[:, :, 0], tok[:].rearrange("p i k -> p (i k)"))
                    v.tensor_copy(pack[:].bitcast(F32)[:, :, 1],
                                  gate[:].rearrange("p i k -> p (i k)")).then_inc(s_dest, 1)
                    dve.wait_ge(s_dest, b * NG + g + 1)
                    v.tensor_scalar(tok[:], tok[:], float(GT), None, ALU.add)
                    link(v.tensor_scalar(trash[:], trash[:], float(GT * TOPK), None, ALU.add))

                for g in range(NG + 2):
                    if g < NG:
                        attention_out(g)
                    if 1 <= g <= NG:
                        cross_out(g - 1)
                    if g >= 2:
                        route(g - 2)
                    if g < NG:
                        score_stats(g)
                    if g >= 2:
                        gates(g - 2)
                        place_tokens(g - 2)
                    if g < NG:
                        softmax(g)
                        sums(g)
                assert n[0] == DVE_B, n[0]

            dve.wait_ge(s_scat, 16 * TI * TOPK * NB * NG)
            dve.wait_ge(s_st, 32 * NB * NG)
            n[0] = 0
            step(v.tensor_scalar(cnt[:], carry[0:1, :], float(CAP), None, ALU.min))
            v.tensor_copy(metaf[:, 0, 0:EX], cnt[:])
            v.tensor_scalar(more[:, 0, :], cnt[:], float(CHUNKS[0] * P), None, ALU.is_gt)
            step(v.tensor_scalar(more[:, 1, :], cnt[:], float((CHUNKS[0] + CHUNKS[1]) * P), None, ALU.is_gt))
            v.scalar_tensor_tensor(need_i[:], more[:, 0, :], 1.0, more[:, 1, :], ALU.add, ALU.add)
            step(v.tensor_scalar(need_t[:], more[:, 0, :], float(CHUNKS[1]), float(CHUNKS[0]), ALU.mult, ALU.add))
            step(v.scalar_tensor_tensor(need_t[:], more[:, 1, :], float(CHUNKS[2]), need_t[:], ALU.mult, ALU.add))
            v.tensor_tensor_scan(metaf[:, 1, 1:EX + 1], need_t[:], zero8[:], 0.0, ALU.add, ALU.add)
            step(v.tensor_tensor_scan(metaf[:, 2, 1:EX + 1], need_i[:], zero8[:], 0.0, ALU.add, ALU.add))
            step(v.tensor_scalar(metaf[:, 3, 1:EX + 1], metaf[:, 2, 1:EX + 1], 1.0, None, ALU.subtract))
            v.tensor_copy(meta[:], metaf[:]).then_inc(s_meta, 1)
            dve.wait_ge(s_meta, 1)

            def w_parts(s):
                if s < W1P:
                    return [t[:, s].rearrange("p k n -> p (k n)") for t in (w1_lo, w1_hi)]
                return [t[:, 2 * (s - W1P):2 * (s - W1P) + 2].rearrange("p f n -> p (f n)") for t in (w2_lo, w2_hi)]

            def split(e, s):
                dve.wait_ge(s_w_hi, e * WP + s + 1)
                lo, hi = w_parts(s)
                low(lo, stage[s % STG][:], hi).then_inc(s_w_lo, 1)

            def evac_x(first, tiles):
                for i in range(tiles):
                    dve.wait_ge(s_xehi, first + i + 1)
                    low(xe_lo[:, :, i * P:(i + 1) * P], pt[i % 2][:].rearrange("p (k t) -> p k t", k=KC),
                        xe_hi[:, :, i * P:(i + 1) * P]).then_inc(s_xelo, 1)

            evac_x(0, CHUNKS[0])
            for s in range(W1P):
                split(0, s)
            with dve.Fori(0, EX) as e:
                count = dve.value_load(meta[0:1, 0, bass.ds(e, 1)], min_val=0, max_val=CAP)
                tb = dve.value_load(meta[0:1, 1, bass.ds(e, 1)], min_val=0, max_val=EX * ET)
                ib = dve.value_load(meta[0:1, 2, bass.ds(e, 1)], min_val=0, max_val=EX * 3)

                def jobs(c):
                    w = CHUNKS[c] * P
                    for j in range(FJ + 1):
                        if j < FJ:
                            dve.wait_ge(s_gl, (ib + c) * FJ + j + 1)
                            dve.wait_ge(s_hglo, (ib + c) * FJ + max(j - 1, 0))
                            v.tensor_tensor(hp[j % 2][:, 0:w], gl[j % 2][:, 0:w], pg[:, 2 + j % 2, 0:w],
                                            ALU.mult).then_inc(s_hp, 1)
                        if j >= 1:
                            dve.wait_ge(s_hghi, (ib + c) * FJ + j)
                            dve.wait_ge(s_hp, (ib + c) * FJ + j)
                            low(hg_lo[:, j - 1, 0:w], hp[(j - 1) % 2][:, 0:w],
                                hg_hi[:, j - 1, 0:w]).then_inc(s_hglo, 1)
                        if c == 0 and 2 <= j < 2 + W2P:
                            split(e, W1P + j - 2)

                jobs(0)
                with dve.If(count > 4 * P):
                    evac_x(tb + 4, CHUNKS[1])
                    jobs(1)
                    with dve.If(count > 8 * P):
                        evac_x(tb + 8, CHUNKS[2])
                        jobs(2)
                        evac_x(tb + 10, CHUNKS[0])
                    with dve.Else():
                        evac_x(tb + 8, CHUNKS[0])
                with dve.Else():
                    evac_x(tb + 4, CHUNKS[0])
                with dve.If(e < EX - 1):
                    for s in range(W1P):
                        split(e + 1, s)


def kernel(x, ctx_1024, mask_BxS2_bk0, L0_attn_Wq, L0_attn_bq, L0_attn_Wk, L0_attn_bk, L0_attn_Wv,
           L0_attn_bv, L0_xattn_Wq, L0_xattn_bq, L0_xattn_Wk, L0_xattn_bk, L0_xattn_Wv, L0_xattn_bv,
           L0_xattn_Wout, L0_xattn_bout, L0_ffn_Wg, L0_ffn_W1, L0_ffn_W2):
    import numpy as np
    import concourse.bacc as bacc
    from concourse.bass_utils import run_bass_kernel_spmd

    def a(t):
        return np.asarray(t)

    arrays = {
        "x": a(x).reshape(N, D),
        "wq": a(L0_attn_Wq), "wk": a(L0_attn_Wk), "wv": a(L0_attn_Wv),
        "bq": a(L0_attn_bq).reshape(KC, P).T, "bk": a(L0_attn_bk).reshape(1, D), "bv": a(L0_attn_bv).reshape(1, D),
        "ctxT": a(ctx_1024).reshape(NB * CK, KC, P).transpose(2, 1, 0),
        "xwqT": a(L0_xattn_Wq).T, "xbq": a(L0_xattn_bq).reshape(XH, 1),
        "xwk": a(L0_xattn_Wk).reshape(KC, P, XH).transpose(1, 0, 2), "xbk": a(L0_xattn_bk).reshape(XH, 1),
        "xwv4": np.tile(a(L0_xattn_Wv), (1, P // XH)).reshape(KC, P, P).transpose(1, 0, 2),
        "xbv4": np.tile(a(L0_xattn_bv), P // XH).reshape(P, 1),
        "wout": a(L0_xattn_Wout), "bout": a(L0_xattn_bout).reshape(1, D),
        "mask": a(mask_BxS2_bk0).reshape(NB * CK),
        "wg": a(L0_ffn_Wg).reshape(EX, KC, P).transpose(2, 1, 0),
        "w1": a(L0_ffn_W1).reshape(EX, KC, P, 2, FJ, P).transpose(0, 4, 2, 1, 3, 5).reshape(EX, FJ, P, 1024),
        "w2": a(L0_ffn_W2),
    }
    nc = bacc.Bacc("TRN2", target_bir_lowering=False, num_devices=1)
    args = {}
    for name, value in arrays.items():
        arrays[name] = value = np.ascontiguousarray(value)
        args[name] = nc.dram_tensor(name, value.shape, mybir.dt.from_np(value.dtype), kind="ExternalInput").ap()
    args["out"] = nc.dram_tensor("out_rows", (N + P, D), F32, kind="ExternalOutput").ap()
    decoder(nc, **args)
    r = run_bass_kernel_spmd(nc, [arrays], core_ids=[0])
    return r.results[0]["out_rows"][:N].reshape(NB, S, D)
```

```python
from contextlib import ExitStack

import concourse.bass as bass
from concourse import mybir

F32 = mybir.dt.float32
F32R = mybir.dt.float32r
BF16 = mybir.dt.bfloat16
U32 = mybir.dt.uint32
I32 = mybir.dt.int32
U8 = mybir.dt.uint8
ALU = mybir.AluOpType
ACT = mybir.ActivationFunctionType
AX = mybir.AxisListType

P = 128
D = 512
KC = D // P
NB, S = 2, 2048
N = NB * S
GT = 512
NG = S // GT
TI = GT // P
H, HD = 8, 64
PAIRS = H // 2
HW = HD + 1
PW = 2 * HW
CK, XH = 77, 32
BR = 33
PADW = 96
EX, TOPK, INNER = 8, 2, 1024
CAP = int(N * TOPK * 1.25 / EX)
ET = CAP // P
FJ = INNER // P
W1P, W2P = FJ, FJ // 2
WP = W1P + W2P
STG = 4
CHUNKS = [4, 4, 2]
QA = NG - 2
JOBS = [2 * TI if g < QA else TI for g in range(NG)]
FIRST = [sum(JOBS[:g]) for g in range(NG)]
JA, JT = sum(JOBS), NG * 2 * TI
JB = JT - JA
POS = TI * PADW
SLOTS = EX * CAP
PHANTOM = CAP
TRASH = SLOTS + PHANTOM
TABLE = TRASH + N * TOPK
LN_EPS, Z_EPS, SIG_EPS = 1e-5, 1e-6, 1e-8

DVE_B, POOL_B = 123, 19


def decoder(nc, x, wq, wk, wv, bq, bk, bv, ctxT, xwqT, xbq, xwk, xbk, xwv4, xbv4, wout, bout,
            mask, wg, w1, w2, out):
    x3d = nc.dram_tensor("x3_rows", (N + P, D), F32, kind="Internal").ap()
    table = nc.dram_tensor("slot_table", (TABLE, 2), U32, kind="Internal").ap()

    base = 16512
    front_at, ffn_at, keep_at = [0], [0], [0]

    def place(name, shape, dt, cursor):
        size = 2 if dt == BF16 else 1 if dt == U8 else 4
        for n in shape[1:]:
            size *= n
        t = nc.alloc_sbuf_tensor_at(name, list(shape), dt, offset=base + cursor[0])
        cursor[0] += (size + 31) // 32 * 32
        return t

    def keep(name, shape, dt=F32):
        return place(name, shape, dt, keep_at)

    ident = keep("ident", [P, P])
    tri = keep("tri", [P, P], BF16)
    onesb = keep("onesb", [P, P], BF16)
    ones = keep("ones", [P, P])
    ones_r = keep("ones_r", [BR, P], F32R)
    bq_c = keep("bq_c", [P, KC])
    bq_neg = keep("bq_neg", [P, KC])
    bk_rows = keep("bk_rows", [BR, D])
    bk_parts = keep("bk_parts", [BR, D], F32R)
    bv_row = keep("bv_row", [1, D])
    ksum_row = keep("ksum_row", [1, D])
    wqk = keep("wqk", [P, KC, NB * PADW])
    wgp = keep("wgp", [P, KC, PADW])
    sbias = keep("sbias", [P, NB, CK])
    maskf = keep("maskf", [P, NB, CK])
    kv = keep("kv", [P, PAIRS, PW])
    half_neg = keep("half_neg", [P, TI])
    half_pos = keep("half_pos", [P, TI])
    iota8 = keep("iota8", [P, EX])
    iota8i = keep("iota8i", [P, EX], I32)
    tok = keep("tok", [P, TI, TOPK])
    toki = keep("toki", [P, TI, TOPK], I32)
    trash = keep("trash", [P, TI, TOPK])
    trashi = keep("trashi", [P, TI, TOPK], I32)
    carry = keep("carry", [P, EX])
    st, mv = ([keep(f"{n}{q}", [P, TI, w]) for q in range(2)] for n, w in (("st", 6), ("mv", 2)))
    var_e, rstd, neg_mean, shift = ([keep(f"{n}{q}", [P, TI]) for q in range(2)]
                                    for n in ("var_e", "rstd", "neg_mean", "shift"))
    st2 = keep("st2", [P, TI, 6])
    mv2 = keep("mv2", [P, TI, 2])
    sig = keep("sig", [P, TI, 4])
    den = keep("den", [P, 2, 2, 4])
    zz = keep("zz", [P, 2, 2, 4])
    smax = keep("smax", [P, TI])
    ssum = keep("ssum", [P, TI])
    sinv = keep("sinv", [P, TI])
    lg = keep("lg", [P, TI, EX])
    top = keep("top", [P, TI, EX])
    topi = keep("topi", [P, TI, EX], U32)
    gd = keep("gd", [P, TI])
    ge = keep("ge", [P, TI])
    gs = keep("gs", [P, TI])
    gate = keep("gate", [P, TI, TOPK])
    ef = keep("ef", [P, TI, TOPK])
    oh = keep("oh", [P, TI, TOPK, EX])
    hot = keep("hot", [P, TI, EX], BF16)
    pos = keep("pos", [P, TI, EX])
    ohp = keep("ohp", [P, TI, TOPK, EX])
    pe_ = keep("pe_", [P, TI, TOPK])
    kept = keep("kept", [P, TI, TOPK])
    slot = keep("slot", [P, TI, TOPK])
    dest = keep("dest", [P, TI * TOPK], U32)
    pack = keep("pack", [P, TI * TOPK, 2], U32)
    cnt = keep("cnt", [1, EX])
    more = keep("more", [1, 2, EX])
    need_t = keep("need_t", [1, EX])
    need_i = keep("need_i", [1, EX])
    zero8 = keep("zero8", [1, EX])
    metaf = keep("metaf", [1, 4, EX + 1])
    meta = keep("meta", [1, 4, EX + 1], U32)
    etab_next = keep("etab_next", [P, ET, 2], U32)
    etab = keep("etab", [P, ET, 2], U32)
    tabinit = keep("tabinit", [P, (EX + 1) * ET, 2], I32)
    front_at[0] = ffn_at[0] = keep_at[0]

    def fr(name, shape, dt=F32):
        return place(name, shape, dt, front_at)

    wq_hi, wq_lo, wk_hi, wk_lo = (fr(n, [P, KC, D], F32R) for n in ("wq_hi", "wq_lo", "wk_hi", "wk_lo"))
    x_in = fr("x_in", [P, TI, D])
    xn = fr("xn", [P, TI, D])
    xT_hi = fr("xT_hi", [P, KC, GT], F32R)
    xT_lo = fr("xT_lo", [P, KC, GT], F32R)
    xn_hi_at = front_at[0]
    xn_hi = fr("xn_hi", [P, TI, D], F32R)
    xn_lo = fr("xn_lo", [P, TI, D], F32R)
    raw_at = front_at[0]
    qT = [fr(f"qT{g}", [P, KC, GT]) for g in range(QA)]
    xTq_at = front_at[0]
    xTq_hi = fr("xTq_hi", [P, KC, GT], F32R)
    xTq_lo = fr("xTq_lo", [P, KC, GT], F32R)
    wv_sb = fr("wv_sb", [P, KC, D])
    k_at = front_at[0]
    k_hi = fr("k_hi", [P, TI, D], F32R)
    k_lo = fr("k_lo", [P, TI, D], F32R)
    k_sum = fr("k_sum", [P, D])
    fe = [fr(f"fe{i}", [P, D]) for i in range(2)]
    frl = [fr(f"frl{i}", [P, D]) for i in range(2)]
    kf = [fr(f"kf{i}", [P, D]) for i in range(2)]
    xr_at = front_at[0]
    xr = [fr(f"xr{i}", [P, TI, D]) for i in range(2)]
    xn2 = xn
    xn3 = fr("xn3", [P, TI, D])
    vp = fr("vp", [CK, NB * D])
    sc = fr("sc", [P, TI, CK])
    sT_at = front_at[0]
    sT = fr("sT", [CK, TI * P])
    assert base + front_at[0] <= nc.sbuf_usable_end, front_at

    def alias(name, shape, dt, at):
        return place(name, shape, dt, [at])

    xr.append(alias("xr2", [P, TI, D], F32, xn_hi_at))
    gT = alias("gT", [P, KC, D], F32, xn_hi_at)
    qT.append(alias("qT2", [P, KC, GT], F32, xn_hi_at + 8192))
    qT.append(alias("qT3", [P, KC, GT], F32, xTq_at))
    xT = [(xTq_hi, xTq_lo) if g == QA else (xT_hi, xT_lo) for g in range(NG)]
    wq_raw = alias("wq_raw", [P, KC, D], F32, raw_at)
    wk_raw = alias("wk_raw", [P, KC, D], F32, raw_at + 8192)
    xT2 = alias("xT2", [P, KC, GT], F32, k_at)
    xT3 = alias("xT3", [P, KC, GT], F32, k_at + 8192)
    s_at = [xr_at]
    wout_sb = place("wout_sb", [P, KC, D], F32, s_at)
    ctx_sb = place("ctx_sb", [P, KC, NB * CK], F32, s_at)
    xwk_sb = place("xwk_sb", [P, KC, XH], F32, s_at)
    xwv_sb = place("xwv_sb", [P, KC, P], F32, s_at)
    s_at = [xr_at + 16384]
    xwqT_sb = place("xwqT_sb", [XH, D], F32, s_at)
    xbq_sb = place("xbq_sb", [XH, 1], F32, s_at)
    xbk_sb = place("xbk_sb", [XH, 1], F32, s_at)
    xbv_sb = place("xbv_sb", [P, 1], F32, s_at)
    bout_sb = place("bout_sb", [1, D], F32, s_at)
    mask_sb = place("mask_sb", [P, NB * CK], U8, s_at)
    wg_sb = place("wg_sb", [P, KC, EX], F32, s_at)
    kT = place("kT", [XH, NB * CK], F32, s_at)
    vT = place("vT", [P, NB * CK], F32, s_at)
    bq_b = place("bq_b", [XH, P], F32, s_at)
    zrow = alias("zrow", [P, D], F32, sT_at)

    def ff(name, shape, dt=F32):
        return place(name, shape, dt, ffn_at)

    w1_hi = ff("w1_hi", [P, FJ, KC, 2 * P], F32R)
    w1_lo = ff("w1_lo", [P, FJ, KC, 2 * P], F32R)
    stage = [ff(f"stage{i}", [P, 1024]) for i in range(STG)]
    w2_hi = ff("w2_hi", [P, FJ, D], F32R)
    w2_lo = ff("w2_lo", [P, FJ, D], F32R)
    hg_hi = ff("hg_hi", [P, FJ, GT], F32R)
    hg_lo = ff("hg_lo", [P, FJ, GT], F32R)
    xe_hi = ff("xe_hi", [P, KC, GT], F32R)
    xe_lo = ff("xe_lo", [P, KC, GT], F32R)
    xg = ff("xg", [P, TI, D])
    gl = [ff(f"gl{i}", [P, GT]) for i in range(2)]
    hp = [ff(f"hp{i}", [P, GT]) for i in range(2)]
    ost = [ff(f"ost{i}", [P, D]) for i in range(2)]
    assert base + ffn_at[0] <= nc.sbuf_usable_end, ffn_at

    with ExitStack() as ctx:
        pg = ctx.enter_context(nc.psum_tensor("pg", [P, 4, 512], F32))
        pt = [ctx.enter_context(nc.psum_tensor(f"pt{i}", [P, 512], F32)) for i in range(2)]
        pj = [ctx.enter_context(nc.psum_tensor(f"pj{i}", [P, 512], F32)) for i in range(2)]

        def sem(name):
            return ctx.enter_context(nc.semaphore(name))

        s_xattn_in = sem("xattn_weights_loaded")
        s_wout_in = sem("wout_mask_wg_loaded")
        s_wk_in = sem("wk_loaded")
        s_wq_in = sem("wq_wv_loaded")
        s_const = sem("consts_ready")
        s_pself = sem("pool_setup_step")
        s_dself = sem("dve_setup_step")
        s_bk = sem("bk_rows_cleared")
        s_whi = sem("front_w_hi")
        s_wlo = sem("front_w_lo")
        s_xset = sem("xattn_psum_ready")
        s_xev = sem("xattn_copied")
        s_vpev = sem("vp_copied")
        s_init = sem("dram_initialised")
        s_xin = sem("x_in_loaded")
        s_stat = sem("stats_ready")
        s_first = sem("first_stats_step")
        s_pfirst = sem("first_rstd_step")
        s_stat2 = sem("second_stats_ready")
        s_rstd = sem("rstd_ready")
        s_rstd2 = sem("second_rstd_ready")
        s_xn = sem("xn_ready")
        s_xnhi = sem("xn_hi_ready")
        s_xnlo = sem("xn_lo_ready")
        s_t = sem("xT_psum_ready")
        s_thi = sem("xT_hi_ready")
        s_tlo = sem("xT_lo_ready")
        s_proj = sem("proj_psum_ready")
        s_feat = sem("exp_relu_ready")
        s_fm = sem("feature_map_ready")
        s_relu = sem("late_q_relu_of_negative")
        s_fmq = sem("late_q_ready")
        s_khi = sem("k_hi_ready")
        s_klo = sem("k_lo_ready")
        s_ks = sem("k_sum_added")
        s_g = sem("gT_psum_ready")
        s_gev = sem("gT_copied")
        s_krow = sem("ksum_row_psum_ready")
        s_krev = sem("ksum_row_copied")
        s_kv = sem("kv_psum_ready")
        s_kvev = sem("kv_copied")
        s_dve = sem("dve_step")
        s_pool = sem("pool_step")
        s_xr = sem("x_res_loaded")
        s_o = sem("attn_psum_ready")
        s_oev = sem("attn_scaled")
        s_xn2 = sem("xn2_ready")
        s_bt = sem("B_transposes_ready")
        s_btev = sem("B_transposes_copied")
        s_s = sem("scores_psum_ready")
        s_sev = sem("scores_copied")
        s_s2 = sem("score_stats_ready")
        s_sig = sem("sigma_ready")
        s_ex = sem("score_shifted")
        s_e = sem("score_exp_ready")
        s_x2p = sem("xattn_out_psum_ready")
        s_x2t = sem("x2_tile_ready")
        s_xn3 = sem("xn3_ready")
        s_lgp = sem("logits_psum_ready")
        s_lgev = sem("logits_copied")
        s_gd = sem("gate_diff_ready")
        s_ge = sem("gate_exp_ready")
        s_hot = sem("onehot_ready")
        s_pos = sem("positions_psum_ready")
        s_posev = sem("positions_copied")
        s_dest = sem("slots_ready")
        s_scat = sem("slots_written")
        s_st = sem("x2_x3_stored")
        s_meta = sem("meta_ready")

        s_wst = [sem(f"w_piece_loaded{i}") for i in range(STG)]
        s_w_hi = sem("w_hi_ready")
        s_w_lo = sem("w_lo_ready")
        s_etab = sem("expert_table_loaded")
        s_etc = sem("expert_table_copied")
        s_xg = sem("rows_gathered")
        s_xet = sem("xe_psum_ready")
        s_xehi = sem("xe_hi_ready")
        s_xelo = sem("xe_lo_ready")
        s_h = sem("h_psum_ready")
        s_gl = sem("gelu_ready")
        s_hp = sem("gelu_gate_ready")
        s_hghi = sem("hg_hi_ready")
        s_hglo = sem("hg_lo_ready")
        s_y = sem("expert_out_psum_ready")
        s_yev = sem("expert_out_scaled")
        s_add = sem("rows_added")

        x_g = x.rearrange("(b g i p) d -> b g p i d", b=NB, g=NG, i=TI, p=P)
        out_g = out[0:N, :].rearrange("(b g i p) d -> b g p i d", b=NB, g=NG, i=TI, p=P)
        x3_g = x3d[0:N, :].rearrange("(b g i p) d -> b g p i d", b=NB, g=NG, i=TI, p=P)
        table_t = table[0:TRASH, :].rearrange("(t p) w -> p t w", p=P)
        XATTN_LOADS, WOUT_LOADS, WK_LOADS, WQ_LOADS = 7, 4, 3, 4

        def batch_of(view, b):
            return view[bass.ds(b, 1)].rearrange("o g p i d -> (o g) p i d")

        block = ctx.enter_context(nc.Block())

        def wait(engine, semaphore, value):
            engine.wait_ge(semaphore, value)

        def wait_alone(engine, semaphore, value):
            if not isinstance(value, int):
                engine.to_reg(value)
            engine.wait_ge(s_const, 2)
            engine.wait_ge(semaphore, value)

        @block.sync
        def _(sp):
            xattn = ((ctx_sb[:], ctxT), (xwk_sb[:], xwk), (xwv_sb[:], xwv4), (xbk_sb[:], xbk),
                     (xbv_sb[:], xbv4), (xwqT_sb[:], xwqT), (xbq_sb[:], xbq))
            for dst, src in xattn:
                sp.dma_start(dst, src).then_inc(s_xattn_in, 16)
            sp.dma_start(x_in[:], x_g[0, 0]).then_inc(s_xin, 16)
            for dst, src in ((wout_sb[:], wout.rearrange("(k p) n -> p k n", p=P)), (bout_sb[:], bout),
                             (wg_sb[:], wg), (mask_sb[:], mask.partition_broadcast(P))):
                sp.dma_start(dst, src).then_inc(s_wout_in, 16)
            for dst, src in ((wk_raw[:], wk.rearrange("(k p) n -> p k n", p=P)),
                             (bk_rows[0:1, :], bk), (bk_rows[BR - 1:BR, :], bk)):
                sp.dma_start(dst, src).then_inc(s_wk_in, 16)
            for dst, src in ((wq_raw[:], wq.rearrange("(k p) n -> p k n", p=P)), (bq_c[:], bq),
                             (wv_sb[:], wv.rearrange("(k p) n -> p k n", p=P)), (bv_row[:], bv)):
                sp.dma_start(dst, src).then_inc(s_wq_in, 16)
            sp.wait_ge(s_const, 1)
            sp.dma_start(table_t, tabinit[:].bitcast(U32)).then_inc(s_init, 16)
            sp.wait_ge(s_vpev, NB)
            sp.wait_ge(s_xev, 3)
            sp.wait_ge(s_init, 16)
            with sp.Fori(0, NB) as b:
                x_b = batch_of(x_g, b)
                out_b, x3_b = batch_of(out_g, b), batch_of(x3_g, b)
                for g in range(1, NG):
                    sp.wait_ge(s_xn, b * NG + g)
                    sp.dma_start(x_in[:], x_b[g]).then_inc(s_xin, 16)
                for g in range(2):
                    sp.dma_start(xr[g][:], x_b[g]).then_inc(s_xr, 16)
                    wait_alone(sp, s_xr, b * 16 * NG + 16 * (g + 1))
                wait_alone(sp, s_xn, b * NG + NG)
                with sp.If(b < NB - 1):
                    sp.dma_start(x_in[:], x_g[NB - 1, 0]).then_inc(s_xin, 16)
                sp.wait_ge(s_kv, b + 1)
                sp.dma_start(xr[2][:], x_b[2]).then_inc(s_xr, 16)
                wait_alone(sp, s_xr, b * 16 * NG + 48)
                for g in range(NG):
                    sp.wait_ge(s_x2t, (b * NG + g + 1) * TI)
                    sp.dma_start(out_b[g], xr[g % 3][:]).then_inc(s_st, 16)
                    sp.wait_ge(s_xn3, (b * NG + g + 1) * TI)
                    sp.dma_start(x3_b[g], xn3[:]).then_inc(s_st, 16)
                    wait_alone(sp, s_st, b * 32 * NG + 32 * (g + 1))
                    if g + 3 < NG:
                        sp.dma_start(xr[g % 3][:], x_b[g + 3]).then_inc(s_xr, 16)

            def piece(e, s):
                if s < W1P:
                    return w1[e, s]
                return w2[e].rearrange("(q f p) n -> q p f n", q=W2P, p=P)[s - W1P]

            def dst(s):
                t = stage[s % STG]
                return t[:] if s < W1P else t[:].rearrange("p (f n) -> p f n", f=2)

            sp.wait_ge(s_kv, NB)
            for s in range(WP):
                if s == W1P:
                    sp.wait_ge(s_scat, 16 + 16 * TI * TOPK * NB * NG)
                    sp.dma_start(etab_next[:], table_t[:, 0:ET]).then_inc(s_etab, 16)
                if s >= STG:
                    sp.wait_ge(s_w_lo, s - STG + 1)
                sp.dma_start(dst(s), piece(0, s)).then_inc(s_wst[s % STG], 16)
            with sp.Fori(1, EX) as e:
                sp.wait_ge(s_etc, e)
                sp.dma_start(etab_next[:], table_t[:, bass.ds(e * ET, ET)]).then_inc(s_etab, 16)
                for s in range(WP):
                    sp.wait_ge(s_w_lo, e * WP + s - STG + 1)
                    if s < W1P:
                        src = w1[bass.ds(e, 1), s].rearrange("o p n -> (o p) n")
                    else:
                        src = w2[bass.ds(e, 1)].rearrange("o (q f p) n -> (o q) p f n",
                                                          q=W2P, p=P)[s - W1P]
                    sp.dma_start(dst(s), src).then_inc(s_wst[s % STG], 16)
            sp.wait_ge(s_etc, EX)
            sp.dma_start(etab_next[:], table_t[:, EX * ET:(EX + 1) * ET]).then_inc(s_etab, 16)
            tiles = sp.value_load(meta[0:1, 1, EX:EX + 1], min_val=0, max_val=EX * ET)
            wait_alone(sp, s_add, 16 + 16 * tiles)

        @block.gpsimd
        def _(pool):
            p = nc.gpsimd
            n = [0]

            def step(ins):
                n[0] += 1
                ins.then_inc(s_pself, 1)
                pool.wait_ge(s_pself, n[0])

            step(p.memset(tabinit[:], 0))
            step(p.iota(tabinit[:, :, 0], pattern=[[0, (EX + 1) * ET]], base=N, channel_multiplier=1))
            p.memset(zrow[:], 0.0).then_inc(s_const, 1)
            step(p.memset(ident[:], 0.0))
            step(p.affine_select(out=ident[:], in_=ident[:], compare_op=ALU.not_equal, fill=1.0, base=0,
                                 pattern=[[-1, P]], channel_multiplier=1))
            step(p.memset(onesb[:], 1.0))
            step(p.affine_select(out=tri[:], in_=onesb[:], compare_op=ALU.is_gt, fill=0.0, base=0,
                                 pattern=[[1, P]], channel_multiplier=-1))
            p.memset(ones[:], 1.0)
            p.memset(kv[:], 0.0)
            p.memset(wqk[:], 0.0)
            p.memset(wgp[:], 0.0)
            p.memset(half_neg[:], -0.5)
            p.memset(half_pos[:], 0.5)
            p.memset(carry[:], 0.0)
            p.memset(zero8[:], 0.0)
            p.memset(metaf[:], 0.0)
            p.iota(iota8i[:], pattern=[[1, EX]], base=0, channel_multiplier=0)
            p.iota(toki[:], pattern=[[P, TI], [0, TOPK]], base=0, channel_multiplier=1)
            p.iota(trashi[:], pattern=[[TOPK * P, TI], [P, TOPK]], base=TRASH,
                   channel_multiplier=1).then_inc(s_const, 1)
            pool.wait_ge(s_const, 1)
            p.dma_start(x3d[N:N + P, :], zrow[:]).then_inc(s_scat, 16)
            p.dma_start(out[N:N + P, :], zrow[:]).then_inc(s_add, 16)
            def first_rstd(b):
                wait_alone(pool, s_stat, b * 2 * NG + 1)
                p.tensor_scalar(var_e[0][:], mv[0][:, :, 1], LN_EPS, None, ALU.add).then_inc(s_pfirst, 1)
                wait_alone(pool, s_pfirst, b + 1)
                p.tensor_tensor(rstd[0][:], var_e[0][:], half_neg[:], ALU.pow).then_inc(s_rstd, 1)

            first_rstd(0)
            pool.wait_ge(s_init, 16)
            pool.wait_ge(s_scat, 16)
            pool.wait_ge(s_add, 16)
            with pool.Fori(0, NB) as b:
                n[0] = 0

                def link(ins):
                    n[0] += 1
                    ins.then_inc(s_pool, 1)
                    wait_alone(pool, s_pool, b * POOL_B + n[0])

                ns = [0]

                def inverse_std(q):
                    link(p.tensor_scalar(var_e[q][:], mv[q][:, :, 1], LN_EPS, None, ALU.add))
                    return p.tensor_tensor(rstd[q][:], var_e[q][:], half_neg[:], ALU.pow)

                def shift_of(q):
                    return p.tensor_tensor(shift[q][:], neg_mean[q][:], rstd[q][:], ALU.mult)

                def rsqrt_var():
                    ns[0] += 1
                    wait_alone(pool, s_stat, b * 2 * NG + ns[0])
                    inverse_std(0).then_inc(s_rstd, 1)

                def norm2():
                    ns[0] += 1
                    wait_alone(pool, s_stat, b * 2 * NG + ns[0])
                    p.tensor_scalar(neg_mean[0][:], mv[0][:, :, 0], -1.0, None, ALU.mult)
                    link(inverse_std(0))
                    shift_of(0).then_inc(s_rstd, 1)

                def norm3(g):
                    wait_alone(pool, s_stat2, b * NG + g + 1)
                    if g:
                        wait_alone(pool, s_xn3, (b * NG + g) * TI)
                    p.tensor_scalar(neg_mean[1][:], mv[1][:, :, 0], -1.0, None, ALU.mult)
                    link(inverse_std(1))
                    shift_of(1).then_inc(s_rstd2, 1)

                def k_sums(g, tiles):
                    for i in tiles:
                        wait_alone(pool, s_fm, b * JA + FIRST[g] + i + 1)
                        if g == 0 and i == 0:
                            ins = p.tensor_copy(k_sum[:], kf[i % 2][:])
                        else:
                            wait_alone(pool, s_ks, b * NG * TI + g * TI + i)
                            ins = p.tensor_tensor(k_sum[:], k_sum[:], kf[i % 2][:], ALU.add)
                        ins.then_inc(s_ks, 1)

                def late_q(jobs):
                    for s in jobs:
                        wait_alone(pool, s_feat, b * JT + JA + s + 1)
                        p.tensor_tensor(qT[QA + s // KC][:, s % KC, :], fe[s % 2][:], frl[s % 2][:],
                                        ALU.add).then_inc(s_fmq, 1)

                def sigma(g):
                    wait_alone(pool, s_s2, b * NG + g + 1)
                    p.tensor_tensor(sig[:, :, 1], sig[:, :, 0], half_pos[:], ALU.pow).then_inc(s_sig, 1)

                def scatter(g):
                    wait_alone(pool, s_dest, b * NG + g + 1)
                    for c in range(TI * TOPK):
                        p.indirect_dma_start(
                            out=table, out_offset=bass.IndirectOffsetOnAxis(ap=dest[:, c:c + 1], axis=0),
                            in_=pack[:, c, :], in_offset=None).then_inc(s_scat, 16)

                ns[0] = 1
                for g in range(NG):
                    k_sums(g, range(2))
                    if g + 1 < NG:
                        rsqrt_var()
                    k_sums(g, range(2, TI))
                late_q(range(2))
                for g in range(NG + 2):
                    if g < NG:
                        norm2()
                    if g == 0:
                        late_q(range(2, 3))
                    if g == NG:
                        scatter(g - 2)
                    if 1 <= g <= NG:
                        norm3(g - 1)
                    if g < NG:
                        sigma(g)
                    if g == 0:
                        late_q(range(3, JB))
                    if g == NG:
                        with pool.If(b < NB - 1):
                            first_rstd(b + 1)
                    if g >= 2 and g != NG:
                        scatter(g - 2)
                assert n[0] == POOL_B, n[0]

            def gather(src_tab, t0, tiles):
                for i in range(tiles):
                    p.indirect_dma_start(
                        out=xg[:, i, :], out_offset=None, in_=x3d,
                        in_offset=bass.IndirectOffsetOnAxis(ap=src_tab[:, t0 + i, 0:1], axis=0)
                    ).then_inc(s_xg, 16)

            pool.wait_ge(s_meta, 1)
            pool.wait_ge(s_etab, 16)
            gather(etab_next, 0, CHUNKS[0])
            with pool.Fori(0, EX) as e:
                count = pool.value_load(meta[0:1, 0, bass.ds(e, 1)], min_val=0, max_val=CAP)
                tb = pool.value_load(meta[0:1, 1, bass.ds(e, 1)], min_val=0, max_val=EX * ET)
                wait_alone(pool, s_add, 16 + 16 * tb)
                wait_alone(pool, s_xg, 16 * tb + 16 * CHUNKS[0])
                p.tensor_copy(etab[:], etab_next[:]).then_inc(s_etc, 1)
                wait_alone(pool, s_etc, e + 1)

                def ahead(c, tiles, from_next):
                    wait_alone(pool, s_xet, tb + 4 * c + CHUNKS[c])
                    if from_next:
                        wait_alone(pool, s_etab, 16 * (e + 2))
                        gather(etab_next, 0, tiles)
                    else:
                        gather(etab, 4 * (c + 1), tiles)

                def add_rows(c):
                    for i in range(CHUNKS[c]):
                        t = 4 * c + i
                        wait_alone(pool, s_yev, tb + t + 2)
                        wait_alone(pool, s_add, 16 + 16 * (tb + t))
                        p.indirect_dma_start(
                            out=out, out_offset=bass.IndirectOffsetOnAxis(ap=etab[:, t, 0:1], axis=0),
                            in_=ost[i % 2][:], in_offset=None, compute_op=ALU.add).then_inc(s_add, 16)

                with pool.If(count > 4 * P):
                    ahead(0, CHUNKS[1], False)
                    add_rows(0)
                    with pool.If(count > 8 * P):
                        ahead(1, CHUNKS[2], False)
                        add_rows(1)
                        ahead(2, CHUNKS[0], True)
                        add_rows(2)
                    with pool.Else():
                        ahead(1, CHUNKS[0], True)
                        add_rows(1)
                with pool.Else():
                    ahead(0, CHUNKS[0], True)
                    add_rows(0)

        @block.scalar
        def _(act):
            a = nc.scalar
            act.wait_ge(s_const, 2)
            a.activation(ones_r[:], ones[0:BR, :], ACT.Copy).then_inc(s_yev, 1)
            a.activation(bk_parts[:], zrow[0:BR, :], ACT.Copy).then_inc(s_bk, 1)
            act.wait_ge(s_wk_in, 16 * WK_LOADS)
            a.activation(wk_hi[:], wk_raw[:], ACT.Copy).then_inc(s_whi, 1)
            act.wait_ge(s_bk, 1)
            a.activation(bk_parts[0:1, :], bk_rows[0:1, :], ACT.Copy)
            a.activation(bk_parts[BR - 1:BR, :], bk_rows[BR - 1:BR, :], ACT.Copy).then_inc(s_whi, 1)
            act.wait_ge(s_wq_in, 16 * WQ_LOADS)
            a.activation(wq_hi[:], wq_raw[:], ACT.Copy).then_inc(s_whi, 1)
            for b in range(NB):
                act.wait_ge(s_xset, 3 + b)
                a.activation(vp[:, b * D:(b + 1) * D], pg[0:CK, b, :], ACT.Copy).then_inc(s_vpev, 1)

            with act.Fori(0, NB) as b:
                def turned_hi(g):
                    for k in range(KC):
                        act.wait_ge(s_t, b * NG * KC + g * KC + k + 1)
                        a.activation(xT[g][0][:, k, :], pt[k % 2][:], ACT.Copy).then_inc(s_thi, 1)

                def exp_relu(i, bias):
                    a.activation(fe[i][:], pj[i][:], ACT.Exp, bias=bias)
                    a.activation(frl[i][:], pj[i][:], ACT.Relu, bias=bias).then_inc(s_feat, 1)

                def job(g, j):
                    act.wait_ge(s_proj, b * JT + FIRST[g] + j + 1)
                    if g or j >= 2:
                        act.wait_ge(s_fm, b * JA + FIRST[g] + j - 1)
                    exp_relu(j % 2, 0.0 if j < TI else bq_c[:, j - TI:j - TI + 1])

                def late_q(jobs):
                    for s in jobs:
                        act.wait_ge(s_proj, b * JT + JA + s + 1)
                        if s >= 2:
                            act.wait_ge(s_fmq, b * JB + s - 1)
                        i, c = s % 2, slice(s % KC, s % KC + 1)
                        a.activation(fe[i][:], pj[i][:], ACT.Relu, bias=bq_neg[:, c], scale=-1.0
                                     ).then_inc(s_relu, 1)
                        a.activation(frl[i][:], pj[i][:], ACT.Relu, bias=bq_c[:, c])
                        act.wait_ge(s_relu, b * JB + s + 1)
                        a.activation(fe[i][:], fe[i][:], ACT.Exp, scale=-1.0).then_inc(s_feat, 1)

                def khi(g, i):
                    act.wait_ge(s_fm, b * JA + FIRST[g] + i + 1)
                    a.activation(k_hi[:, i, :], kf[i % 2][:], ACT.Copy).then_inc(s_khi, 1)

                for g in range(NG):
                    turned_hi(g)
                    act.wait_ge(s_xn, b * NG + g + 1)
                    if g:
                        act.wait_ge(s_g, b * NG + g)
                    a.activation(xn_hi[:], xn[:], ACT.Copy).then_inc(s_xnhi, 1)
                    for j in range(max(JOBS[g], TI + 1)):
                        if j < JOBS[g]:
                            job(g, j)
                        if 1 <= j <= TI:
                            khi(g, j - 1)
                act.wait_ge(s_g, (b + 1) * NG)
                for c in range(2):
                    a.activation(gT[:, c, :], pg[:, c, :], ACT.Copy)
                act.wait_ge(s_krow, b + 1)
                a.activation(ksum_row[:], pj[0][0:1, :], ACT.Copy).then_inc(s_krev, 1)

                nt = [0]
                BT = (2 * TI + 1) * NG

                def turned(dst):
                    bank = pt[nt[0] % 2]
                    nt[0] += 1
                    act.wait_ge(s_bt, b * BT + nt[0])
                    a.activation(dst, bank[0:dst.shape[0]].rearrange("p (k t) -> p k t", t=P) if len(dst.shape) == 3
                                 else bank[0:dst.shape[0], :], ACT.Copy).then_inc(s_btev, 1)

                def normalise(dst, src, q, done, dstT):
                    for i in range(TI + 1):
                        if i < TI:
                            a.activation(dst[:, i, :], src[:, i, :], ACT.Identity, bias=shift[q][:, i:i + 1],
                                         scale=rstd[q][:, i:i + 1]).then_inc(done, 1)
                        if i >= 1:
                            turned(dstT[:, :, (i - 1) * P:i * P])

                for g in range(NG + 2):
                    if g == 0:
                        act.wait_ge(s_fm, (b + 1) * JA)
                        late_q(range(3))
                    if g < NG:
                        act.wait_ge(s_rstd, b * 2 * NG + NG + g + 1)
                        normalise(xn2, xr[g % 3], 0, s_xn2, xT2)
                    if g >= 2:
                        act.wait_ge(s_gd, b * NG + g - 1)
                        a.activation(ge[:], gd[:], ACT.Exp).then_inc(s_ge, 1)
                    if 1 <= g <= NG:
                        act.wait_ge(s_rstd2, b * NG + g)
                        if g >= 2:
                            act.wait_ge(s_st, 32 * (b * NG + g - 1))
                        normalise(xn3, xr[(g - 1) % 3], 1, s_xn3, xT3)
                    if g == 0:
                        late_q(range(3, JB - 2))
                    if g < NG:
                        act.wait_ge(s_ex, b * NG + g + 1)
                        a.activation(sc[:], sc[:], ACT.Exp).then_inc(s_e, 1)
                        turned(sT[:])
                    if g == 0:
                        late_q(range(JB - 2, JB))
                assert nt[0] == BT

            def w_dst(s):
                return (w1_hi[:, s].rearrange("p k n -> p (k n)") if s < W1P else
                        w2_hi[:, 2 * (s - W1P):2 * (s - W1P) + 2].rearrange("p f n -> p (f n)"))

            def split(e, s, final=None):
                act.wait_ge(s_wst[s % STG], e * (16 * WP // STG) + 16 * (s // STG + 1))
                if final is not None:
                    act.wait_ge(s_h, final * FJ + s + 1)
                a.activation(w_dst(s), stage[s % STG][:], ACT.Copy).then_inc(s_w_hi, 1)

            def evac_x(first, tiles):
                for i in tiles:
                    act.wait_ge(s_xet, first + i + 1)
                    a.activation(xe_hi[:, :, i * P:(i + 1) * P],
                                 pt[i % 2][:].rearrange("p (k t) -> p k t", k=KC), ACT.Copy).then_inc(s_xehi, 1)

            for s in range(W1P):
                split(0, s)
            evac_x(0, range(CHUNKS[0]))
            act.wait_ge(s_meta, 1)
            with act.Fori(0, EX) as e:
                count = act.value_load(meta[0:1, 0, bass.ds(e, 1)], min_val=0, max_val=CAP)
                tb = act.value_load(meta[0:1, 1, bass.ds(e, 1)], min_val=0, max_val=EX * ET)
                ib = act.value_load(meta[0:1, 2, bass.ds(e, 1)], min_val=0, max_val=EX * 3)

                def jobs(c):
                    w = CHUNKS[c] * P
                    act.wait_ge(s_y, tb + 4 * c + 1)
                    for j in range(FJ + 1):
                        if j < FJ:
                            act.wait_ge(s_h, (ib + c) * FJ + j + 1)
                            if j >= 2:
                                act.wait_ge(s_hp, (ib + c) * FJ + j - 1)
                            a.activation(gl[j % 2][:, 0:w], pg[:, j % 2, 0:w], ACT.Gelu).then_inc(s_gl, 1)
                        if j >= 1:
                            act.wait_ge(s_hp, (ib + c) * FJ + j)
                            a.activation(hg_hi[:, j - 1, 0:w], hp[(j - 1) % 2][:, 0:w],
                                         ACT.Copy).then_inc(s_hghi, 1)
                        if c == 0 and 2 <= j < 2 + W2P:
                            split(e, W1P + j - 2)

                def outs(c, last, ahead):
                    per = W1P // CHUNKS[c]
                    following = tb + 4 * c + CHUNKS[c]
                    for i in range(CHUNKS[c]):
                        t = 4 * c + i
                        if i == 0:
                            evac_x(following, range(2))
                        if i == 1:
                            evac_x(following, range(2, ahead))
                        if last:
                            with act.If(e < EX - 1):
                                for s in range(i * per, (i + 1) * per):
                                    split(e + 1, s, ib + c)
                        act.wait_ge(s_y, tb + t + 2)
                        act.wait_ge(s_etc, e + 1)
                        if c or i >= 2:
                            act.wait_ge(s_add, 16 * (tb + t))
                        a.activation(ost[i % 2][:], pj[i % 2][:], ACT.Copy,
                                     scale=etab[:, t, 1:2].bitcast(F32)).then_inc(s_yev, 1)

                jobs(0)
                with act.If(count > 4 * P):
                    outs(0, False, CHUNKS[1])
                    jobs(1)
                    with act.If(count > 8 * P):
                        outs(1, False, CHUNKS[2])
                        jobs(2)
                        outs(2, True, CHUNKS[0])
                    with act.Else():
                        outs(1, True, CHUNKS[0])
                with act.Else():
                    outs(0, True, CHUNKS[0])

        @block.tensor
        def _(pe):
            def three(o, lh, ll, rh, rl, start, stop):
                nc.tensor.matmul(o, lh, rh, start=start, stop=False)
                nc.tensor.matmul(o, lh, rl, start=False, stop=False)
                return nc.tensor.matmul(o, ll, rh, start=False, stop=stop)

            mm = nc.tensor.matmul
            pe.wait_ge(s_xattn_in, 16 * XATTN_LOADS)
            pe.wait_ge(s_const, 2)
            for k in range(KC):
                ins = mm(pj[0][0:XH, 0:NB * CK], xwk_sb[:, k, :], ctx_sb[:, k, :], start=k == 0, stop=k == KC - 1)
            ins.then_inc(s_y, 1)
            for k in range(KC):
                ins = mm(pj[1][:, 0:NB * CK], xwv_sb[:, k, :], ctx_sb[:, k, :], start=k == 0, stop=k == KC - 1)
            ins.then_inc(s_xset, 1)
            pe.wait_ge(s_xev, 1)
            for m in range(KC):
                mm(pt[m // 3][:, m % 3 * NB * CK:(m % 3 + 1) * NB * CK], xwqT_sb[:, m * P:(m + 1) * P], kT[:],
                   start=True, stop=True)
            mm(pt[1][:, NB * CK:2 * NB * CK], bq_b[:], kT[:], start=True, stop=True).then_inc(s_xset, 1)
            pe.wait_ge(s_wout_in, 16 * WOUT_LOADS)
            for b in range(NB):
                for r in range(KC):
                    mm(pg[0:CK, b, :], vT[:, b * CK:(b + 1) * CK], wout_sb[:, r, :], start=r == 0, stop=False)
                mm(pg[0:CK, b, :], ones[0:1, 0:CK], bout_sb[:], start=False, stop=True).then_inc(s_xset, 1)
            pe.wait_ge(s_xev, 3)
            pe.wait_ge(s_vpev, NB)
            pe.wait_ge(s_wlo, 3)
            pe.wait_ge(s_whi, 3)

            with pe.Fori(0, NB) as b:
                def turn(g, chunks):
                    pe.wait_ge(s_xn, b * NG + g + 1)
                    for k in chunks:
                        if g or k >= 2:
                            pe.wait_ge(s_tlo, b * NG * KC + g * KC + k - 1)
                        for i in range(TI):
                            ins = nc.tensor.transpose(pt[k % 2][:, i * P:(i + 1) * P],
                                                      xn[:, i, k * P:(k + 1) * P], ident[:])
                        ins.then_inc(s_t, 1)

                def q_job(o, m, x_hi, x_lo):
                    for k in range(KC):
                        ins = three(o, wq_hi[:, k, m], wq_lo[:, k, m], x_hi[:, k, :], x_lo[:, k, :],
                                    k == 0, k == KC - 1)
                    ins.then_inc(s_proj, 1)

                def project(g):
                    x_hi, x_lo = xT[g]
                    for j in range(JOBS[g]):
                        if j == 0:
                            pe.wait_ge(s_tlo, b * NG * KC + (g + 1) * KC)
                        if g or j >= 2:
                            pe.wait_ge(s_feat, b * JT + FIRST[g] + j - 1)
                        o = pj[j % 2][:]
                        if j < TI:
                            tk = slice(j * P, (j + 1) * P)
                            mm(o, ones_r[:], bk_parts[:], start=True, stop=False)
                            for k in range(KC):
                                ins = three(o, x_hi[:, k, tk], x_lo[:, k, tk], wk_hi[:, k, :], wk_lo[:, k, :],
                                            False, k == KC - 1)
                            ins.then_inc(s_proj, 1)
                        else:
                            q_job(o, slice((j - TI) * P, (j - TI + 1) * P), x_hi, x_lo)

                def late_q(jobs):
                    for s in jobs:
                        if s >= 2:
                            pe.wait_ge(s_feat, b * JT + JA + s - 1)
                        q_job(pj[s % 2][:], slice(s % KC * P, (s % KC + 1) * P), *xT[QA + s // KC])

                def gram(g, tiles):
                    pe.wait_ge(s_xnlo, b * NG + g + 1)
                    for i in tiles:
                        pe.wait_ge(s_klo, b * NG * TI + g * TI + i + 1)
                        for c in range(KC):
                            m = slice(c * P, (c + 1) * P)
                            ins = three(pg[:, c, :], xn_hi[:, i, m], xn_lo[:, i, m], k_hi[:, i, :], k_lo[:, i, :],
                                        g == 0 and i == 0, g == NG - 1 and i == TI - 1)
                    return ins

                turn(0, range(KC))
                for g in range(NG):
                    project(g)
                    gram(g, range(1))
                    if g + 1 < NG:
                        turn(g + 1, range(2))
                    gram(g, range(1, 2))
                    if g + 1 < NG:
                        turn(g + 1, range(2, KC))
                    gram(g, range(2, TI)).then_inc(s_g, 1)

                pe.wait_ge(s_ks, (b + 1) * NG * TI)
                pe.wait_ge(s_feat, b * JT + JA)
                mm(pj[0][0:1, :], ones[:, 0:1], k_sum[:], start=True, stop=True).then_inc(s_krow, 1)
                pe.wait_ge(s_krev, b + 1)
                for m in range(KC):
                    mm(pj[1][:, m:m + 1], ksum_row[0:1, m * P:(m + 1) * P], ones[0:1, 0:1], start=True, stop=True)
                pe.wait_ge(s_gev, b + 1)
                for m in range(KC):
                    cols = slice(m * P, (m + 1) * P)
                    for c in range(KC):
                        mm(pt[0][:, cols], gT[:, c, cols], wv_sb[:, c, cols], start=c == 0, stop=False)
                    ins = mm(pt[0][:, cols], ksum_row[0:1, cols], bv_row[0:1, cols], start=False, stop=True)
                ins.then_inc(s_kv, 1)

                def attend(g, tiles):
                    if g >= QA:
                        pe.wait_ge(s_fmq, b * JB + (g - QA + 1) * KC)
                    if g >= 2 and tiles[0] == 0:
                        pe.wait_ge(s_x2t, (b * NG + g - 1) * TI)
                    for i in tiles:
                        n = b * NG * TI + g * TI + i
                        if g or i >= 2:
                            pe.wait_ge(s_oev, n - 1)
                        for q in range(PAIRS):
                            ins = mm(pg[:, 2 * (i % 2) + q // 2, (q % 2) * PW:(q % 2 + 1) * PW],
                                     qT[g][:, q, i * P:(i + 1) * P], kv[:, q, :], start=True, stop=True)
                        ins.then_inc(s_o, 1)

                nt = [0]
                BT = (2 * TI + 1) * NG

                def bank():
                    if nt[0] >= 2:
                        pe.wait_ge(s_btev, b * BT + nt[0] - 1)
                    nt[0] += 1
                    return pt[(nt[0] - 1) % 2]

                def turn_and_multiply(src, done, turned, g, out, w, ready):
                    for i in range(TI + 1):
                        if i < TI:
                            pe.wait_ge(done, (b * NG + g) * TI + i + 1)
                            to = bank()
                            for k in range(KC):
                                ins = nc.tensor.transpose(to[:, k * P:(k + 1) * P], src[:, i, k * P:(k + 1) * P],
                                                          ident[:])
                            ins.then_inc(s_bt, 1)
                        if i >= 1:
                            pe.wait_ge(s_btev, b * BT + nt[0] - (1 if i < TI else 0))
                            for k in range(KC):
                                ins = mm(out[:, (i - 1) * PADW:i * PADW], turned[:, k, (i - 1) * P:i * P], w(k),
                                         start=k == 0, stop=k == KC - 1)
                    ins.then_inc(ready, 1)

                def scores(g):
                    if g < 2:
                        pe.wait_ge(s_feat, b * JT + (JT if g else JA + 3))
                    if g:
                        pe.wait_ge(s_sev, b * NG + g)
                    if g >= 3:
                        pe.wait_ge(s_posev, b * NG + g - 2)
                    turn_and_multiply(xn2, s_xn2, xT2, g, pj[0],
                                      lambda k: wqk[:, k, bass.ds(b * PADW, PADW)], s_s)

                def logits(g):
                    if g:
                        pe.wait_ge(s_lgev, b * NG + g)
                    turn_and_multiply(xn3, s_xn3, xT3, g, pj[1], lambda k: wgp[:, k, :], s_lgp)

                def turn_exp(g):
                    pe.wait_ge(s_e, b * NG + g + 1)
                    to = bank()
                    for i in range(TI):
                        ins = nc.tensor.transpose(to[0:CK, i * P:(i + 1) * P], sc[:, i, :], ident[:])
                    ins.then_inc(s_bt, 1)

                def values(g):
                    pe.wait_ge(s_btev, b * BT + nt[0])
                    pe.wait_ge(s_oev, (b * NG + min(g + 2, NG)) * TI)
                    for i in range(TI):
                        mm(pg[:, i, :], sT[:, i * P:(i + 1) * P], vp[:, bass.ds(b * D, D)],
                           start=True, stop=True).then_inc(s_x2p, 1)

                def positions(g):
                    pe.wait_ge(s_hot, b * NG + g + 1)
                    if g:
                        pe.wait_ge(s_posev, b * NG + g)
                    pe.wait_ge(s_sev, b * NG + min(g + 3, NG))
                    for i in range(TI):
                        for q in range(i + 1):
                            mm(pj[0][:, POS + i * EX:POS + (i + 1) * EX], (tri if q == i else onesb)[:], hot[:, q, :],
                               start=q == 0, stop=q == i)
                    for q in range(TI):
                        ins = mm(pj[0][:, POS + TI * EX:POS + (TI + 1) * EX], onesb[:], hot[:, q, :],
                                 start=q == 0, stop=q == TI - 1)
                    ins.then_inc(s_pos, 1)

                pe.wait_ge(s_kvev, b + 1)
                attend(0, range(2))
                late_q(range(1))
                attend(0, range(2, TI))
                late_q(range(1, 3))
                for g in range(NG + 2):
                    if g == NG:
                        positions(g - 2)
                    if 1 <= g <= NG:
                        values(g - 1)
                    if g < NG:
                        scores(g)
                    if g >= 2 and g != NG:
                        positions(g - 2)
                    if 1 <= g <= NG:
                        logits(g - 1)
                    if g + 1 < NG:
                        attend(g + 1, range(2))
                    if g == 0:
                        pe.wait_ge(s_sev, b * NG + 1)
                        late_q(range(3, JB - 2))
                    if g < NG:
                        turn_exp(g)
                    if g == 0:
                        late_q(range(JB - 2, JB - 1))
                    if g + 1 < NG:
                        attend(g + 1, range(2, TI))
                    if g == 0:
                        late_q(range(JB - 1, JB))
                assert nt[0] == BT

            pe.wait_ge(s_meta, 1)

            def turn_rows(first, tiles, total):
                pe.wait_ge(s_xg, 16 * (first + total))
                for i in tiles:
                    if i >= 2:
                        pe.wait_ge(s_xelo, first + i - 1)
                    for k in range(KC):
                        ins = nc.tensor.transpose(pt[i % 2][:, k * P:(k + 1) * P], xg[:, i, k * P:(k + 1) * P], ident[:])
                    ins.then_inc(s_xet, 1)

            turn_rows(0, range(CHUNKS[0]), CHUNKS[0])
            with pe.Fori(0, EX) as e:
                count = pe.value_load(meta[0:1, 0, bass.ds(e, 1)], min_val=0, max_val=CAP)
                tb = pe.value_load(meta[0:1, 1, bass.ds(e, 1)], min_val=0, max_val=EX * ET)
                ib = pe.value_load(meta[0:1, 2, bass.ds(e, 1)], min_val=0, max_val=EX * 3)

                def up(c, tiles):
                    w = tiles * P
                    pe.wait_ge(s_xelo, tb + 4 * c + CHUNKS[c])
                    for j in range(FJ):
                        if c == 0:
                            pe.wait_ge(s_w_lo, e * WP + j + 1)
                        if j >= 2:
                            pe.wait_ge(s_hp, (ib + c) * FJ + j - 1)
                        for half in range(2):
                            m = slice(half * P, (half + 1) * P)
                            for k in range(KC):
                                ins = three(pg[:, 2 * half + j % 2, 0:w], w1_hi[:, j, k, m], w1_lo[:, j, k, m],
                                            xe_hi[:, k, 0:w], xe_lo[:, k, 0:w], k == 0, k == KC - 1)
                        ins.then_inc(s_h, 1)

                def down(c, tiles, ahead):
                    following = tb + 4 * c + CHUNKS[c]
                    turn_rows(following, range(2), ahead)
                    if c == 0:
                        pe.wait_ge(s_w_lo, (e + 1) * WP)
                    for i in range(CHUNKS[c]):
                        m = slice(i * P, (i + 1) * P)
                        pe.wait_ge(s_yev, tb + 4 * c + max(i, 1))
                        if i < tiles:
                            for j in range(FJ):
                                if i == 0:
                                    pe.wait_ge(s_hglo, (ib + c) * FJ + j + 2)
                                ins = three(pj[i % 2][:], hg_hi[:, j, m], hg_lo[:, j, m], w2_hi[:, j, :],
                                            w2_lo[:, j, :], j == 0, j == FJ - 1)
                        else:
                            ins = mm(pj[i % 2][:], w1_hi[:, 0, 0, 0:P], w2_hi[:, 0, :], start=True, stop=True)
                        ins.then_inc(s_y, 1)
                        if i == 0 and ahead > 2:
                            turn_rows(following, range(2, ahead), ahead)

                def chunk(c, tiles, ahead):
                    up(c, tiles)
                    down(c, tiles, ahead)

                def last_chunk(c):
                    with pe.If(count > (4 * c + 3) * P):
                        chunk(c, 4, CHUNKS[0])
                    with pe.Else():
                        with pe.If(count > (4 * c + 2) * P):
                            chunk(c, 3, CHUNKS[0])
                        with pe.Else():
                            chunk(c, 2, CHUNKS[0])

                with pe.If(count > 4 * P):
                    chunk(0, 4, CHUNKS[1])
                    with pe.If(count > 8 * P):
                        chunk(1, 4, CHUNKS[2])
                        chunk(2, 2, CHUNKS[0])
                    with pe.Else():
                        last_chunk(1)
                with pe.Else():
                    last_chunk(0)

        @block.vector
        def _(dve):
            v = nc.vector
            n = [0]

            def step(ins):
                n[0] += 1
                ins.then_inc(s_dself, 1)
                dve.wait_ge(s_dself, n[0])

            def low(dst, src, hi):
                return v.tensor_tensor(dst, src, hi.bitcast(F32), ALU.subtract)

            def first_stats(b):
                dve.wait_ge(s_xin, 16 * (b * NG + 1))
                for i in range(TI):
                    ins = v.bn_stats(st[0][:, i, :], x_in[:, i, :])
                ins.then_inc(s_first, 1)
                wait_alone(dve, s_first, b + 1)
                for i in range(TI):
                    ins = v.bn_aggr(mv[0][:, i, :], st[0][:, i, :])
                ins.then_inc(s_stat, 1)

            def normalise(b, g):
                dve.wait_ge(s_rstd, b * 2 * NG + g + 1)
                for i in range(TI):
                    ins = v.tensor_scalar(xn[:, i, :], x_in[:, i, :], mv[0][:, i, 0:1], rstd[0][:, i:i + 1],
                                          ALU.subtract, ALU.mult)
                ins.then_inc(s_xn, 1)

            dve.wait_ge(s_xattn_in, 16 * XATTN_LOADS)
            v.tensor_copy(bq_b[:], xbq_sb[:].broadcast_to([XH, P]))
            dve.wait_ge(s_xset, 1)
            v.tensor_scalar(kT[:], pj[0][0:XH, 0:NB * CK], xbk_sb[:], float(D) ** -0.5, ALU.add, ALU.mult)
            v.tensor_scalar(vT[:], pj[1][:, 0:NB * CK], xbv_sb[:], None, ALU.add).then_inc(s_xev, 1)
            first_stats(0)
            dve.wait_ge(s_const, 2)
            dve.wait_ge(s_xset, 2)
            for m in range(KC):
                v.tensor_copy(wqk[:, m, :].rearrange("p (b c) -> p b c", b=NB)[:, :, 0:CK],
                              pt[m // 3][:, m % 3 * NB * CK:(m % 3 + 1) * NB * CK]
                              .rearrange("p (b c) -> p b c", b=NB))
            v.tensor_copy(sbias[:], pt[1][:, NB * CK:2 * NB * CK].rearrange("p (b c) -> p b c", b=NB)
                          ).then_inc(s_xev, 1)
            normalise(0, 0)
            dve.wait_ge(s_wout_in, 16 * WOUT_LOADS)
            v.tensor_scalar(maskf[:].rearrange("p b c -> p (b c)"), mask_sb[:], -1e-32, None, ALU.mult)
            v.tensor_copy(iota8[:], iota8i[:]).then_inc(s_hglo, 1)
            v.tensor_copy(tok[:], toki[:])
            v.tensor_copy(trash[:], trashi[:])
            v.tensor_copy(wgp[:, :, 0:EX], wg_sb[:]).then_inc(s_xev, 1)
            dve.wait_ge(s_whi, 1)
            low(wk_lo[:], wk_raw[:], wk_hi[:]).then_inc(s_wlo, 1)
            dve.wait_ge(s_whi, 2)
            low(bk_parts[BR - 1:BR, :], bk_rows[BR - 1:BR, :], bk_parts[BR - 1:BR, :]).then_inc(s_wlo, 1)
            dve.wait_ge(s_wq_in, 16 * WQ_LOADS)
            v.tensor_scalar(bq_neg[:], bq_c[:], -1.0, None, ALU.mult)
            dve.wait_ge(s_whi, 3)
            low(wq_lo[:], wq_raw[:], wq_hi[:]).then_inc(s_wlo, 1)
            dve.wait_ge(s_xev, 3)

            with dve.Fori(0, NB) as b:
                n[0] = 0
                ns = [0]
                def link(ins, alone=False):
                    n[0] += 1
                    ins.then_inc(s_dve, 1)
                    (wait_alone if alone else wait)(dve, s_dve, b * DVE_B + n[0])

                def aggregate(q=0):
                    for i in range(TI):
                        ins = v.bn_aggr(mv[q][:, i, :], st[q][:, i, :])
                    ins.then_inc(s_stat2 if q else s_stat, 1)

                def stats_in(g, tiles):
                    if tiles[0] == 0:
                        dve.wait_ge(s_xin, 16 * (b * NG + g + 1))
                    for i in tiles:
                        ins = v.bn_stats(st[0][:, i, :], x_in[:, i, :])
                    return ins

                def turned_lo(g):
                    for k in range(KC):
                        dve.wait_ge(s_thi, b * NG * KC + g * KC + k + 1)
                        low(xT[g][1][:, k, :], pt[k % 2][:], xT[g][0][:, k, :]).then_inc(s_tlo, 1)

                def job(g, j):
                    dve.wait_ge(s_feat, b * JT + FIRST[g] + j + 1)
                    if j < TI:
                        if g or j >= 2:
                            dve.wait_ge(s_ks, b * NG * TI + g * TI + j - 1)
                            dve.wait_ge(s_klo, b * NG * TI + g * TI + j - 1)
                        dst = kf[j % 2][:]
                    else:
                        dst = qT[g][:, j - TI, :]
                    v.scalar_tensor_tensor(dst, fe[j % 2][:], 1.0, frl[j % 2][:], ALU.min, ALU.add
                                           ).then_inc(s_fm, 1)

                for g in range(NG):
                    turned_lo(g)
                    dve.wait_ge(s_xnhi, b * NG + g + 1)
                    low(xn_lo[:], xn[:], xn_hi[:]).then_inc(s_xnlo, 1)
                    for j in range(max(JOBS[g], TI + 1)):
                        if j < JOBS[g]:
                            job(g, j)
                        if 1 <= j <= TI:
                            dve.wait_ge(s_khi, b * NG * TI + g * TI + j)
                            dve.wait_ge(s_fm, b * JA + FIRST[g] + j)
                            low(k_lo[:, j - 1, :], kf[(j - 1) % 2][:], k_hi[:, j - 1, :]).then_inc(s_klo, 1)
                        if g + 1 < NG:
                            if j == 0:
                                stats_in(g + 1, range(2))
                            if j == 1:
                                link(stats_in(g + 1, range(2, TI)), True)
                                aggregate()
                            if j == 3:
                                normalise(b, g + 1)

                dve.wait_ge(s_g, (b + 1) * NG)
                for c in range(2, KC):
                    ins = v.tensor_copy(gT[:, c, :], pg[:, c, :])
                ins.then_inc(s_gev, 1)
                dve.wait_ge(s_kv, b + 1)
                kvp = pt[0][:].rearrange("p (q c) -> p q c", q=PAIRS)
                v.tensor_copy(kv[0:HD, :, 0:HD], kvp[0:HD, :, 0:HD])
                v.tensor_copy(kv[HD:P, :, HW:HW + HD], kvp[HD:P, :, HD:P])
                v.tensor_copy(kv[0:HD, :, HD], pj[1][0:HD, 0:PAIRS])
                v.tensor_copy(kv[HD:P, :, HW + HD], pj[1][HD:P, 0:PAIRS]).then_inc(s_kvev, 1)

                def attention_out(g):
                    x1 = xr[g % 3]
                    dve.wait_ge(s_xr, 16 * (b * NG + g + 1))
                    for pair in range(TI // 2):
                        for q in range(2):
                            dve.wait_ge(s_o, b * NG * TI + g * TI + 2 * pair + q + 1)
                            ins = v.tensor_scalar(den[:, q], pg[:, 2 * q:2 * q + 2, HD:HD + 3 * HW + 1:HW],
                                                  Z_EPS, None, ALU.add)
                        link(ins)
                        for q in range(2):
                            ins = v.reciprocal(zz[:, q], den[:, q])
                        link(ins)
                        for q in range(2):
                            v.tensor_tensor(
                                kf[q][:].rearrange("p (a h c) -> p a h c", a=2, h=4),
                                pg[:, 2 * q:2 * q + 2, 0:4 * HW].rearrange("p a (h w) -> p a h w", w=HW)[:, :, :, 0:HD],
                                zz[:, q].unsqueeze(3).broadcast_to([P, 2, 4, HD]), ALU.mult).then_inc(s_oev, 1)
                        dve.wait_ge(s_oev, b * NG * TI + g * TI + 2 * pair + 2)
                        for q in range(2):
                            i = 2 * pair + q
                            ins = v.tensor_tensor(x1[:, i, :], x1[:, i, :], kf[q][:], ALU.add)
                        link(ins)
                        for q in range(2):
                            ins = v.bn_stats(st[0][:, 2 * pair + q, :], x1[:, 2 * pair + q, :])
                    link(ins, True)
                    aggregate()

                def score_stats(g):
                    dve.wait_ge(s_s, b * NG + g + 1)
                    v.tensor_tensor(sc[:], pj[0][:, 0:POS].rearrange("p (i c) -> p i c", c=PADW)[:, :, 0:CK],
                                    sbias[:, bass.ds(b, 1), :].broadcast_to([P, TI, CK]), ALU.add).then_inc(s_sev, 1)
                    dve.wait_ge(s_sev, b * NG + g + 1)
                    for i in range(TI):
                        ins = v.bn_stats(st2[:, i, :], sc[:, i, :])
                    link(ins, True)
                    for i in range(TI):
                        ins = v.bn_aggr(mv2[:, i, :], st2[:, i, :])
                    link(ins)
                    v.tensor_scalar(sig[:, :, 0], mv2[:, :, 1], CK / (CK - 1.0), None, ALU.mult).then_inc(s_s2, 1)

                def softmax(g):
                    dve.wait_ge(s_sig, b * NG + g + 1)
                    link(v.tensor_scalar(sig[:, :, 2], sig[:, :, 1], SIG_EPS, None, ALU.add))
                    link(v.reciprocal(sig[:, :, 3], sig[:, :, 2]))
                    for i in range(TI):
                        ins = v.tensor_scalar(sc[:, i, :], sc[:, i, :], mv2[:, i, 0:1], sig[:, i, 3:4],
                                              ALU.subtract, ALU.mult)
                    link(ins)
                    link(v.tensor_tensor(sc[:], sc[:], maskf[:, bass.ds(b, 1), :].broadcast_to([P, TI, CK]), ALU.add))
                    link(v.tensor_reduce(smax[:], sc[:], AX.X, ALU.max))
                    v.tensor_tensor(sc[:], sc[:], smax[:].unsqueeze(2).broadcast_to([P, TI, CK]),
                                    ALU.subtract).then_inc(s_ex, 1)

                def cross_out(g):
                    x2 = xr[g % 3]
                    for i in range(TI + 1):
                        m = b * NG * TI + g * TI + i
                        if i < TI:
                            dve.wait_ge(s_x2p, m + 1)
                            v.scalar_tensor_tensor(x2[:, i, :], pg[:, i, :], sinv[:, i:i + 1], x2[:, i, :],
                                                   ALU.mult, ALU.add).then_inc(s_x2t, 1)
                        if i >= 1:
                            dve.wait_ge(s_x2t, m)
                            ins = v.bn_stats(st[1][:, i - 1, :], x2[:, i - 1, :])
                    link(ins, True)
                    aggregate(1)

                def sums(g):
                    dve.wait_ge(s_e, b * NG + g + 1)
                    link(v.tensor_reduce(ssum[:], sc[:], AX.X, ALU.add))
                    link(v.reciprocal(sinv[:], ssum[:]))

                def route(g):
                    dve.wait_ge(s_lgp, b * NG + g + 1)
                    v.tensor_copy(lg[:], pj[1][:, 0:TI * PADW].rearrange("p (i c) -> p i c", c=PADW)[:, :, 0:EX]
                                  ).then_inc(s_lgev, 1)
                    wait_alone(dve, s_lgev, b * NG + g + 1)
                    for i in range(TI):
                        ins = v.max(top[:, i, :], lg[:, i, :])
                    link(ins, True)
                    for i in range(TI):
                        ins = v.max_index(topi[:, i, :], top[:, i, :], lg[:, i, :])
                    v.tensor_tensor(gd[:], top[:, :, 1], top[:, :, 0], ALU.subtract).then_inc(s_gd, 1)
                    dve.wait_ge(s_gd, b * NG + g + 1)
                    link(v.tensor_copy(ef[:], topi[:, :, 0:TOPK]))
                    link(v.tensor_tensor(oh[:].rearrange("p i k e -> p (i k) e"),
                                         ef[:].rearrange("p i k -> p (i k)").unsqueeze(2).broadcast_to([P, TI * TOPK, EX]),
                                         iota8[:].unsqueeze(1).broadcast_to([P, TI * TOPK, EX]), ALU.is_equal))
                    v.tensor_tensor(hot[:], oh[:, :, 0, :], oh[:, :, 1, :], ALU.add).then_inc(s_hot, 1)

                def gates(g):
                    dve.wait_ge(s_ge, b * NG + g + 1)
                    link(v.tensor_scalar(gs[:], ge[:], 1.0, None, ALU.add))
                    link(v.reciprocal(gate[:, :, 0], gs[:]))
                    link(v.tensor_tensor(gate[:, :, 1], ge[:], gate[:, :, 0], ALU.mult))

                def place_tokens(g):
                    dve.wait_ge(s_pos, b * NG + g + 1)
                    link(v.tensor_tensor(pos[:], pj[0][:, POS:POS + TI * EX].rearrange("p (i e) -> p i e", e=EX),
                                         carry[:].unsqueeze(1).broadcast_to([P, TI, EX]), ALU.add))
                    v.tensor_tensor(carry[:], pj[0][:, POS + TI * EX:POS + (TI + 1) * EX], carry[:], ALU.add).then_inc(s_posev, 1)
                    link(v.tensor_tensor(ohp[:], oh[:], pos[:].unsqueeze(2).broadcast_to([P, TI, TOPK, EX]), ALU.mult))
                    link(v.tensor_reduce(pe_[:], ohp[:], AX.X, ALU.add))
                    v.scalar_tensor_tensor(slot[:], ef[:], float(CAP), pe_[:], ALU.mult, ALU.add)
                    link(v.tensor_scalar(kept[:], pe_[:], float(CAP), None, ALU.is_lt))
                    link(v.tensor_tensor(slot[:], slot[:], trash[:], ALU.subtract))
                    link(v.tensor_tensor(slot[:], slot[:], kept[:], ALU.mult))
                    dve.wait_ge(s_scat, 16 + 16 * TI * TOPK * (b * NG + g))
                    v.tensor_tensor(dest[:], slot[:].rearrange("p i k -> p (i k)"),
                                    trash[:].rearrange("p i k -> p (i k)"), ALU.add)
                    v.tensor_copy(pack[:, :, 0], tok[:].rearrange("p i k -> p (i k)"))
                    v.tensor_copy(pack[:].bitcast(F32)[:, :, 1],
                                  gate[:].rearrange("p i k -> p (i k)")).then_inc(s_dest, 1)
                    dve.wait_ge(s_dest, b * NG + g + 1)
                    v.tensor_scalar(tok[:], tok[:], float(GT), None, ALU.add)
                    link(v.tensor_scalar(trash[:], trash[:], float(GT * TOPK), None, ALU.add))

                for g in range(NG + 2):
                    if g < NG:
                        attention_out(g)
                    if g == NG:
                        route(g - 2)
                        gates(g - 2)
                        place_tokens(g - 2)
                    if 1 <= g <= NG:
                        cross_out(g - 1)
                    if g >= 2 and g != NG:
                        route(g - 2)
                    if g < NG:
                        score_stats(g)
                    if g >= 2 and g != NG:
                        gates(g - 2)
                        place_tokens(g - 2)
                    if g == NG:
                        with dve.If(b < NB - 1):
                            first_stats(b + 1)
                            normalise(b + 1, 0)
                    if g < NG:
                        softmax(g)
                        sums(g)
                assert n[0] == DVE_B, n[0]

            n[0] = 0
            step(v.tensor_scalar(cnt[:], carry[0:1, :], float(CAP), None, ALU.min))
            v.tensor_copy(metaf[:, 0, 0:EX], cnt[:])
            v.tensor_scalar(more[:, 0, :], cnt[:], float(CHUNKS[0] * P), None, ALU.is_gt)
            step(v.tensor_scalar(more[:, 1, :], cnt[:], float((CHUNKS[0] + CHUNKS[1]) * P), None, ALU.is_gt))
            v.scalar_tensor_tensor(need_i[:], more[:, 0, :], 1.0, more[:, 1, :], ALU.add, ALU.add)
            step(v.tensor_scalar(need_t[:], more[:, 0, :], float(CHUNKS[1]), float(CHUNKS[0]), ALU.mult, ALU.add))
            step(v.scalar_tensor_tensor(need_t[:], more[:, 1, :], float(CHUNKS[2]), need_t[:], ALU.mult, ALU.add))
            v.tensor_tensor_scan(metaf[:, 1, 1:EX + 1], need_t[:], zero8[:], 0.0, ALU.add, ALU.add)
            step(v.tensor_tensor_scan(metaf[:, 2, 1:EX + 1], need_i[:], zero8[:], 0.0, ALU.add, ALU.add))
            step(v.tensor_scalar(metaf[:, 3, 1:EX + 1], metaf[:, 2, 1:EX + 1], 1.0, None, ALU.subtract))
            v.tensor_copy(meta[:], metaf[:]).then_inc(s_meta, 1)
            dve.wait_ge(s_meta, 1)

            def w_parts(s):
                if s < W1P:
                    return [t[:, s].rearrange("p k n -> p (k n)") for t in (w1_lo, w1_hi)]
                return [t[:, 2 * (s - W1P):2 * (s - W1P) + 2].rearrange("p f n -> p (f n)") for t in (w2_lo, w2_hi)]

            def split(e, s):
                dve.wait_ge(s_w_hi, e * WP + s + 1)
                lo, hi = w_parts(s)
                low(lo, stage[s % STG][:], hi).then_inc(s_w_lo, 1)

            def evac_x(first, tiles):
                for i in range(tiles):
                    dve.wait_ge(s_xehi, first + i + 1)
                    low(xe_lo[:, :, i * P:(i + 1) * P], pt[i % 2][:].rearrange("p (k t) -> p k t", k=KC),
                        xe_hi[:, :, i * P:(i + 1) * P]).then_inc(s_xelo, 1)

            for s in range(W1P):
                split(0, s)
            evac_x(0, CHUNKS[0])
            with dve.Fori(0, EX) as e:
                count = dve.value_load(meta[0:1, 0, bass.ds(e, 1)], min_val=0, max_val=CAP)
                tb = dve.value_load(meta[0:1, 1, bass.ds(e, 1)], min_val=0, max_val=EX * ET)
                ib = dve.value_load(meta[0:1, 2, bass.ds(e, 1)], min_val=0, max_val=EX * 3)

                def jobs(c):
                    w = CHUNKS[c] * P
                    for j in range(FJ + 1):
                        if j < FJ:
                            dve.wait_ge(s_gl, (ib + c) * FJ + j + 1)
                            dve.wait_ge(s_hglo, (ib + c) * FJ + max(j, 1))
                            v.tensor_tensor(hp[j % 2][:, 0:w], gl[j % 2][:, 0:w], pg[:, 2 + j % 2, 0:w],
                                            ALU.mult).then_inc(s_hp, 1)
                        if j >= 1:
                            dve.wait_ge(s_hghi, (ib + c) * FJ + j)
                            dve.wait_ge(s_hp, (ib + c) * FJ + j)
                            low(hg_lo[:, j - 1, 0:w], hp[(j - 1) % 2][:, 0:w],
                                hg_hi[:, j - 1, 0:w]).then_inc(s_hglo, 1)
                        if c == 0 and 2 <= j < 2 + W2P:
                            split(e, W1P + j - 2)

                jobs(0)
                with dve.If(count > 4 * P):
                    evac_x(tb + 4, CHUNKS[1])
                    jobs(1)
                    with dve.If(count > 8 * P):
                        evac_x(tb + 8, CHUNKS[2])
                        jobs(2)
                        evac_x(tb + 10, CHUNKS[0])
                    with dve.Else():
                        evac_x(tb + 8, CHUNKS[0])
                with dve.Else():
                    evac_x(tb + 4, CHUNKS[0])
                with dve.If(e < EX - 1):
                    for s in range(W1P):
                        split(e + 1, s)


def kernel(x, ctx_1024, mask_BxS2_bk0, L0_attn_Wq, L0_attn_bq, L0_attn_Wk, L0_attn_bk, L0_attn_Wv,
           L0_attn_bv, L0_xattn_Wq, L0_xattn_bq, L0_xattn_Wk, L0_xattn_bk, L0_xattn_Wv, L0_xattn_bv,
           L0_xattn_Wout, L0_xattn_bout, L0_ffn_Wg, L0_ffn_W1, L0_ffn_W2):
    import numpy as np
    import concourse.bacc as bacc
    from concourse.bass_utils import run_bass_kernel_spmd

    def a(t):
        return np.asarray(t)

    arrays = {
        "x": a(x).reshape(N, D),
        "wq": a(L0_attn_Wq), "wk": a(L0_attn_Wk), "wv": a(L0_attn_Wv),
        "bq": a(L0_attn_bq).reshape(KC, P).T, "bk": a(L0_attn_bk).reshape(1, D), "bv": a(L0_attn_bv).reshape(1, D),
        "ctxT": a(ctx_1024).reshape(NB * CK, KC, P).transpose(2, 1, 0),
        "xwqT": a(L0_xattn_Wq).T, "xbq": a(L0_xattn_bq).reshape(XH, 1),
        "xwk": a(L0_xattn_Wk).reshape(KC, P, XH).transpose(1, 0, 2), "xbk": a(L0_xattn_bk).reshape(XH, 1),
        "xwv4": np.tile(a(L0_xattn_Wv), (1, P // XH)).reshape(KC, P, P).transpose(1, 0, 2),
        "xbv4": np.tile(a(L0_xattn_bv), P // XH).reshape(P, 1),
        "wout": a(L0_xattn_Wout), "bout": a(L0_xattn_bout).reshape(1, D),
        "mask": a(mask_BxS2_bk0).reshape(NB * CK),
        "wg": a(L0_ffn_Wg).reshape(EX, KC, P).transpose(2, 1, 0),
        "w1": a(L0_ffn_W1).reshape(EX, KC, P, 2, FJ, P).transpose(0, 4, 2, 1, 3, 5).reshape(EX, FJ, P, 1024),
        "w2": a(L0_ffn_W2),
    }
    nc = bacc.Bacc("TRN2", target_bir_lowering=False, num_devices=1)
    args = {}
    for name, value in arrays.items():
        arrays[name] = value = np.ascontiguousarray(value)
        args[name] = nc.dram_tensor(name, value.shape, mybir.dt.from_np(value.dtype), kind="ExternalInput").ap()
    args["out"] = nc.dram_tensor("out_rows", (N + P, D), F32, kind="ExternalOutput").ap()
    decoder(nc, **args)
    r = run_bass_kernel_spmd(nc, [arrays], core_ids=[0])
    return r.results[0]["out_rows"][:N].reshape(NB, S, D)
```
